# Optimizing a Trainium2 kernel written in Bass

```python
import numpy as np
import jax
import jax.numpy as jnp

def _softmax(x, axis=-1):
    return jax.nn.softmax(x, axis=axis)

def _gelu(x):
    return jax.nn.gelu(x, approximate=True)

def _silu(x):
    return jax.nn.silu(x)

def _sigmoid(x):
    return jax.nn.sigmoid(x)

def _layernorm(x, axis=-1, eps=1e-05):
    m = jnp.mean(x, axis=axis, keepdims=True)
    v = jnp.var(x, axis=axis, keepdims=True)
    return (x - m) / jnp.sqrt(v + eps)

def _scatter_add(tgt, idx, src, axis=0):
    return tgt.at[idx].add(src)

def _segment_sum(src, seg, n):
    return jax.ops.segment_sum(src, seg, n)
kernel_name = 'mk_early_fusion_d1_tok_img1024_r4_d589b7'

def setup_inputs(seed: int=0):
    np.random.seed(seed)
    _w = jnp.asarray

    def _rec_inputs():
        import jax
        import jax.numpy as jnp
        _rk = jax.random.key(seed)
        x = -0.00016672 + 0.999947 * jax.random.normal(jax.random.fold_in(_rk, 1), (32, 96, 96, 3), jnp.float32)
        txt = -3.39011e-05 + 0.925824 * jax.random.normal(jax.random.fold_in(_rk, 2), (32, 128, 256), jnp.float32)
        return (x, txt)
    x, txt = _rec_inputs()

    def _L0_tok_setup():
        import jax, jax.numpy as jnp
        import numpy as np
        B, H, W_IMG, C = (64, 96, 96, 3)
        P1, P2 = (16, 16)
        DIM_OUT = 256
        DIM_PATCH = P1 * P2 * C

        def patchify(x, p1, p2):
            bb, s1, s2, d = x.shape
            n1, n2 = (s1 // p1, s2 // p2)
            x = x.reshape(bb, n1, p1, n2, p2, d)
            x = x.transpose(0, 1, 3, 2, 4, 5)
            return (x.reshape(bb, n1 * n2, p1 * p2 * d), [n1, n2])
        key = jax.random.key(seed)
        k1, k2 = jax.random.split(key)
        x = jax.random.normal(k1, (B, H, W_IMG, C), dtype=jnp.float32)
        limit = float(np.sqrt(6.0 / (DIM_PATCH + DIM_OUT)))
        W = jax.random.uniform(k2, (DIM_OUT, DIM_PATCH), dtype=jnp.float32, minval=-limit, maxval=limit)
        b = jnp.zeros((DIM_OUT,), dtype=jnp.float32)
        return {'x': x, 'W': W, 'b': b}
    _L0_tok_all = _L0_tok_setup()
    _L0_tok_in = {k: v for k, v in _L0_tok_all.items() if k in ('W', 'b')}
    del _L0_tok_all

    def _L0_attn_setup():
        import jax, jax.numpy as jnp
        import numpy as np
        B, S, D = (4, 512, 256)

        def _xavier(key, shape):
            bound = float(np.sqrt(6.0 / (shape[0] + shape[1])))
            return jax.random.uniform(key, shape, dtype=jnp.float32, minval=-bound, maxval=bound)
        key = jax.random.key(seed)
        k0, k1, k2, k3 = jax.random.split(key, 4)
        return {'embeddings': jax.random.normal(k0, (B, S, D), dtype=jnp.float32), 'W_Q': _xavier(k1, (D, D)), 'W_K': _xavier(k2, (D, D)), 'W_V': _xavier(k3, (D, D))}
    _L0_attn_all = _L0_attn_setup()
    _L0_attn_in = {k: v for k, v in _L0_attn_all.items() if k in ('W_Q', 'W_K', 'W_V')}
    del _L0_attn_all

    def _L0_ffn_setup():
        import jax, jax.numpy as jnp
        import numpy as np
        B, N, C, H, REG = (1, 2309, 256, 16, 5)
        D = C // H
        key = jax.random.key(seed)
        k0, k1, k2, k3 = jax.random.split(key, 4)
        x = jax.random.normal(k0, (B, N, C), dtype=jnp.float32)
        g_info = jax.random.normal(k1, (12, 2, C), dtype=jnp.float32)
        W_qkv = jax.random.normal(k2, (C, 3 * C), dtype=jnp.float32) * 0.02
        W_proj = jax.random.normal(k3, (C, C), dtype=jnp.float32) * 0.02
        b_proj = jnp.zeros((C,), dtype=jnp.float32)
        return {'x': x, 'g_info': g_info, 'W_qkv': W_qkv, 'W_proj': W_proj, 'b_proj': b_proj}
    _L0_ffn_all = _L0_ffn_setup()
    _L0_ffn_in = {k: v for k, v in _L0_ffn_all.items() if k in ('g_info', 'W_qkv', 'W_proj', 'b_proj')}
    del _L0_ffn_all
    return {'x': x, 'txt': txt, 'L0_tok_W': _L0_tok_in['W'], 'L0_tok_b': _L0_tok_in['b'], 'L0_attn_W_Q': _L0_attn_in['W_Q'], 'L0_attn_W_K': _L0_attn_in['W_K'], 'L0_attn_W_V': _L0_attn_in['W_V'], 'L0_ffn_g_info': _L0_ffn_in['g_info'], 'L0_ffn_W_qkv': _L0_ffn_in['W_qkv'], 'L0_ffn_W_proj': _L0_ffn_in['W_proj'], 'L0_ffn_b_proj': _L0_ffn_in['b_proj']}

def reference(x, txt, L0_tok_W, L0_tok_b, L0_attn_W_Q, L0_attn_W_K, L0_attn_W_V, L0_ffn_g_info, L0_ffn_W_qkv, L0_ffn_W_proj, L0_ffn_b_proj):
    import jax
    import jax.numpy as jnp

    def _L0_tok_ref(x, W, b):
        import jax, jax.numpy as jnp
        import numpy as np
        B, H, W_IMG, C = (64, 96, 96, 3)
        P1, P2 = (16, 16)
        DIM_OUT = 256
        DIM_PATCH = P1 * P2 * C

        def patchify(x, p1, p2):
            bb, s1, s2, d = x.shape
            n1, n2 = (s1 // p1, s2 // p2)
            x = x.reshape(bb, n1, p1, n2, p2, d)
            x = x.transpose(0, 1, 3, 2, 4, 5)
            return (x.reshape(bb, n1 * n2, p1 * p2 * d), [n1, n2])
        patches, n_list = patchify(x, P1, P2)
        out = jnp.einsum('bnk,ok->bno', patches, W) + b
        return out

    def _L0_attn_ref(embeddings, W_Q, W_K, W_V):
        import jax, jax.numpy as jnp
        import numpy as np
        B, S, D = (4, 512, 256)

        def _xavier(key, shape):
            bound = float(np.sqrt(6.0 / (shape[0] + shape[1])))
            return jax.random.uniform(key, shape, dtype=jnp.float32, minval=-bound, maxval=bound)
        _, seq_len, d = embeddings.shape
        Q = embeddings @ W_Q
        K = embeddings @ W_K
        V = embeddings @ W_V
        scale = 1.0 / jnp.sqrt(jnp.float32(d))
        scores = jnp.einsum('bqd,bkd->bqk', Q, K) * scale
        causal = jnp.tril(jnp.ones((seq_len, seq_len), dtype=bool))
        scores = jnp.where(causal[None, :, :], scores, -jnp.inf)
        probs = jax.nn.softmax(scores, axis=-1)
        return jnp.einsum('bqk,bkd->bqd', probs, V)

    def _L0_ffn_ref(x, g_info, W_qkv, W_proj, b_proj):
        import jax, jax.numpy as jnp
        import numpy as np
        B, N, C, H, REG = (1, 2309, 256, 16, 5)
        D = C // H
        Bx, Nx, Cx = x.shape
        scale = D ** (-0.5)
        qkv = (x @ W_qkv).reshape(Bx, Nx, 3, H, D)
        q, k, v = (qkv[:, :, 0], qkv[:, :, 1], qkv[:, :, 2])
        g_layer = g_info[0].reshape(-1, H, D)
        q_g = g_layer[0]
        q_pure = q[:, REG:]
        q_n = q_pure / jnp.linalg.norm(q_pure, axis=-1, keepdims=True)
        qg_n = q_g / jnp.linalg.norm(q_g, axis=-1, keepdims=True)
        sim = (qg_n[None, None] * q_n).sum(-1).mean(-1)
        sim = (sim - sim.min()) / (sim.max() - sim.min())
        pos = sim > 0.9
        logits = jnp.einsum('bqhd,bkhd->bhqk', q * scale, k)

        def masked_attn(tok_mask):
            key_mask = jnp.concatenate([jnp.ones((Bx, REG), bool), tok_mask], axis=1)
            l = jnp.where(key_mask[:, None, None, :], logits, -jnp.inf)
            a = jax.nn.softmax(l, axis=-1)
            return jnp.einsum('bhqk,bkhd->bqhd', a, v)
        x_pos = masked_attn(pos)
        x_neg = masked_attn(~pos)
        reg_out = (x_pos[:, :REG] + x_neg[:, :REG]) * 0.5
        tok_out = jnp.where(pos[:, :, None, None], x_pos[:, REG:], x_neg[:, REG:])
        out = jnp.concatenate([reg_out, tok_out], axis=1).reshape(Bx, Nx, Cx)
        return out @ W_proj + b_proj
    h = _L0_tok_ref(x, L0_tok_W, L0_tok_b)
    h = jnp.concatenate([h, txt], axis=1)
    h = h + _L0_attn_ref(_layernorm(h, axis=-1), L0_attn_W_Q, L0_attn_W_K, L0_attn_W_V)
    h = h + _L0_ffn_ref(_layernorm(h, axis=-1), L0_ffn_g_info, L0_ffn_W_qkv, L0_ffn_W_proj, L0_ffn_b_proj)
    return h

_drawn_inputs = setup_inputs


def setup_inputs(seed=0):
    import zlib

    import numpy as np

    out = dict(_drawn_inputs(seed))
    spreads = {'L0_tok_b': (0.0, 0.1), 'L0_ffn_b_proj': (0.0, 0.1)}
    factors = {'L0_ffn_g_info': 8.0, 'L0_ffn_W_qkv': 3.955, 'L0_ffn_W_proj': 3.972}
    for name, (base, spread) in spreads.items():
        noise = np.random.default_rng([zlib.crc32(name.encode()), seed]).standard_normal(out[name].shape)
        drawn = base * np.exp(spread * noise) if base else spread * noise
        out[name] = jnp.asarray(drawn.astype(out[name].dtype))
    for name, factor in factors.items():
        out[name] = (out[name] * factor).astype(out[name].dtype)
    return out
```

```python
from contextlib import ExitStack

import concourse.bass as bass
from concourse import mybir

F32 = mybir.dt.float32
F16 = mybir.dt.float16
ALU = mybir.AluOpType
ACT = mybir.ActivationFunctionType
AX_X = mybir.AxisListType.X

B, D = 32, 256
NTOK, NTXT = 36, 128
T = NTOK + NTXT
PATCH = 768
H, DH, REG = 16, 16, 5
P = 128
TAIL = T - P
GAP = 64
PT = GAP + TAIL
NPAIR = B // 2
TQ = T + REG
QTAIL = TQ - P
KC = D // P
NE = B * NTOK // P
KE = PATCH // P
EPS = 1e-5
MASKED = -1e30
QUARTER = T // 4
CLASS = 60000.0
KPAD = 192
SHIFT_ROW = 127

C_ID, C_M0, C_MT, C_BB, C_OB = 0, 128, 256, 420, 548
C_REGBIG, C_NREG, C_REG, C_HALF = 612, 653, 694, 735
C_END = 737


def need(eng, sem, count):
    if not isinstance(count, int) or count > 0:
        eng.wait_ge(sem, count)


def upto(count, most):
    return min(count, most) if isinstance(count, int) else count


def run_steps(eng, stages, first, loop_from, loop_to, last, unroll):
    def one(step, t, u):
        for lag, total, emit in stages:
            if t is None:
                n = step - lag
                if 0 <= n < total:
                    emit(n, n % unroll, n // unroll)
            else:
                emit(t * unroll + (u - lag), (u - lag) % unroll, t + (u - lag) // unroll)

    for step in range(first, loop_from):
        one(step, None, 0)
    with eng.Fori(loop_from // unroll, loop_to // unroll) as t:
        for u in range(unroll):
            one(None, t, u)
    for step in range(loop_to, last):
        one(step, None, 0)


def fusion_program(nc, xt, txt, w_tok, b_tok, a_wqt, a_wkt, a_wv, f_wqkv, f_wqt, f_g, f_wp, f_bp, consts, consts16, out):
    scratch = {
        "h_tok": nc.dram_tensor("h_tok", (B * NTOK, D), F32).ap(),
        "q": nc.dram_tensor("q_split", (H, 2, DH, B, TQ), F16).ap(),
        "k": nc.dram_tensor("k_split", (H, 2, DH, B, T), F16).ap(),
        "sim": nc.dram_tensor("sim_parts", (2, H, B * T), F32).ap(),
        "cls": nc.dram_tensor("class_rows", (4, B * T), F16).ap(),
    }
    with ExitStack() as whole:
        def sb(name, shape, dt=F32, ctx=whole):
            return ctx.enter_context(nc.sbuf_tensor(name, shape, dt))

        con = sb("con", [P, C_END])
        ident16 = sb("ident16", [P, P], F16)
        h0 = sb("h0", [P, B, D])
        ht = sb("ht", [P, NPAIR, D])
        x2t = sb("x2t", [P, KC, B * T])
        wv2 = sb("wv2", [P, KC, D])
        wp = sb("wp", [P, KC, D])
        bp = sb("bp", [P, D])
        ident = con[:, C_ID:C_ID + P]
        keep = (con, ident16, ident, h0, ht, x2t, wv2, wp, bp)
        first_phase(nc, keep, scratch, xt, txt, w_tok, b_tok, a_wqt, a_wkt, a_wv, f_wqkv, f_wqt, f_g, f_wp, f_bp, consts)
        class_phase(nc, keep, scratch)
        second_phase(nc, keep, scratch, consts16, out)


def first_phase(nc, keep, scratch, xt, txt, w_tok, b_tok, a_wqt, a_wkt, a_wv, f_wqkv, f_wqt, f_g, f_wp, f_bp, consts):
    con, ident16, ident, h0, ht, x2t, wv2, wp, bp = keep
    with ExitStack() as ctx:
        def sb(name, shape, dt=F32):
            return ctx.enter_context(nc.sbuf_tensor(name, shape, dt))

        def sem(name):
            return ctx.enter_context(nc.semaphore(name))

        wt = sb("wt", [P, KE, D])
        bt = sb("bt", [P, D])
        wqt, wkt, wv = (sb(n, [P, KC, D]) for n in ("wqt", "wkt", "wv"))
        wqk = sb("wqk", [P, KC, D])
        wqk2 = sb("wqk2", [P, KC, 2 * D])
        wqt2 = sb("wqt2", [P, KC, D])
        gcol = sb("gcol", [P, KC])
        gsq = sb("gsq", [P, KC])
        gss = sb("gss", [P, KC])
        grn = sb("grn", [P, KC])
        gn = sb("gn", [P, KC])
        gblk = sb("gblk", [P, KC, H])
        wg = sb("wg", [P, KC, 32])
        mhalf = sb("mhalf", [P, 3])
        xi = [sb(f"xi{j}", [P, KE, P]) for j in range(3)]
        he = [sb(f"he{j}", [P, D]) for j in range(3)]
        st1, st2 = sb("st1", [P, 3, 6]), sb("st2", [P, 3, 6])
        mv1, mv2 = sb("mv1", [P, 3, 2]), sb("mv2", [P, 3, 2])
        ve1, ve2 = sb("ve1", [P, 3]), sb("ve2", [P, 3])
        rs1, rs2 = sb("rs1", [P, 3]), sb("rs2", [P, 3])
        x1, x2 = sb("x1", [P, 3, D]), sb("x2", [P, 3, D])
        x1t = [sb(f"x1t{j}", [P, KC, 2, T]) for j in range(2)]
        qt = sb("qt", [P, KC, 2 * T])
        v0 = [sb(f"v0_{j}", [P, 2, D]) for j in range(2)]
        vt = [sb(f"vt_{j}", [P, D]) for j in range(2)]
        sm = sb("sm", [P, 2 * P + T])
        mx, nm, su, rsum = sb("mx", [P, 3]), sb("nm", [P, 3]), sb("su", [P, 4]), sb("rsum", [P, 3])
        p0 = sb("p0", [P, 2, P])
        p2 = sb("p2", [P, P + PT])
        pts = sb("pts", [P, 2 * P + PT])
        ptt = sb("ptt", [P, PT])
        qh, ql = ([sb(f"{n}{j}", [P, KC, 2, TQ], F16) for j in range(2)] for n in ("qh", "ql"))
        kh, kl = ([sb(f"{n}{j}", [P, KC, 2 * T], F16) for j in range(2)] for n in ("kh", "kl"))
        qsq = sb("qsq", [P, KC, 2 * T])
        ss = [sb(f"ss{j}", [64, 2 * T]) for j in range(2)]

        def ps(name, shape):
            return ctx.enter_context(nc.psum_tensor(name, shape, F32))

        pT = ps("pT", [P, 2, 512])
        pP = ps("pP", [P, 2, 512])
        pV = ps("pV", [P, 2, 512])
        pS = ps("pS", [P, 512])
        pR = ps("pR", [P, 512])

        ld_w0, ld_w1, ld_w2 = sem("ld_w0"), sem("ld_w1"), sem("ld_w2")
        ld_xi = [sem(f"ld_xi{j}") for j in range(3)]
        ld_h = [sem(f"ld_h{j}") for j in range(2)]
        names = ("cleared e_done e_evac wqk_done wqk_ready gsq_ready gss_done gss_ready grn_ready gn_ready gblk_ready "
                 "wg_done wg_ready id16_ready st1_done mv1_done ve1_done rs1_done x1_ready t1_done x1t_ready qt_done qt_ready "
                 "v_done v_ready s_done sm_done nm_ready p_ready sum_added rsum_ready pt_done pts_ready pv_done h1_done "
                 "st2_done mv2_done ve2_done rs2_done x2_ready t2_done x2t_ready q_done q_hi q_lo q_dup k_done k_hi k_lo "
                 "sim_done sim_evac dve_turn pool_turn sp_turn").split()
        s = {n: sem(n) for n in names}
        st_he = [sem(f"st_he{j}") for j in range(3)]
        st_q = [sem(f"st_q{j}") for j in range(2)]
        st_k = [sem(f"st_k{j}") for j in range(2)]
        st_s = [sem(f"st_s{j}") for j in range(2)]

        NS = 20
        LOOP = (6, 16)

        with nc.Block() as block:

            @block.sync
            def _(sp):
                sp.dma_start(wt[:, :, :], w_tok).then_inc(ld_w0, 16)
                sp.dma_start(bt[:, :], b_tok.broadcast_to([P, D])).then_inc(ld_w0, 16)
                sp.dma_start(con[:, :], consts).then_inc(ld_w0, 16)
                for j in range(3):
                    sp.dma_start(xi[j][:, :, :], xt[:, j, :, :]).then_inc(ld_xi[j], 16)
                for dst, src in ((wqt, a_wqt), (wkt, a_wkt), (wv, a_wv)):
                    sp.dma_start(dst[:, :, :], src).then_inc(ld_w1, 16)
                sp.dma_start(wqk2[:, :, :], f_wqkv[:, :, 0:2 * D]).then_inc(ld_w2, 16)
                sp.dma_start(wv2[:, :, :], f_wqkv[:, :, 2 * D:3 * D]).then_inc(ld_w2, 16)
                sp.dma_start(wqt2[:, :, :], f_wqt).then_inc(ld_w2, 16)
                sp.dma_start(gcol[:, :], f_g).then_inc(ld_w2, 16)
                sp.dma_start(wp[:, :, :], f_wp).then_inc(ld_w2, 16)
                sp.dma_start(bp[:, :], f_bp.broadcast_to([P, D])).then_inc(ld_w2, 16)
                for g in range(NE // 3):
                    for j in range(3):
                        n = 3 * g + j
                        sp.wait_ge(s["e_evac"], n + 1)
                        sp.dma_start(scratch["h_tok"][n * P:(n + 1) * P, :], he[j][:, :]).then_inc(st_he[j], 16)
                        if n + 3 < NE:
                            sp.dma_start(xi[j][:, :, :], xt[:, n + 3, :, :]).then_inc(ld_xi[j], 16)
                for j in range(3):
                    sp.wait_ge(st_he[j], 16 * NE // 3)
                sp.wait_ge(s["cleared"], 1)

                def load_h(n, k, half):
                    need(sp, s["st1_done"], (n - 1) * 3)
                    for b in range(2):
                        tok = scratch["h_tok"][bass.ds(n * 2 * NTOK + b * NTOK, NTOK), :]
                        sp.dma_start(h0[0:NTOK, bass.ds(n * 2 + b, 1), :], tok).then_inc(ld_h[k], 16)
                        sp.dma_start(h0[NTOK:P, bass.ds(n * 2 + b, 1), :],
                                     txt[bass.ds(n * 2 + b, 1), 0:P - NTOK, :].rearrange("b t d -> t b d")).then_inc(ld_h[k], 16)
                        sp.dma_start(ht[GAP * b:GAP * b + TAIL, bass.ds(n, 1), :],
                                     txt[bass.ds(n * 2 + b, 1), P - NTOK:NTXT, :].rearrange("b t d -> t b d")).then_inc(ld_h[k], 16)

                def store_q(n, k, half):
                    sp.wait_ge(s["q_dup"], 2 * n + 2)
                    for i, src in enumerate((qh, ql)):
                        for c in range(KC):
                            dst = scratch["q"][c * 8:c * 8 + 8, i, :, :, :].rearrange("h d b t -> h d (b t)")
                            sp.dma_start(dst[:, :, bass.ds(n * 2 * TQ, 2 * TQ)],
                                         src[k][:, c, :, :].rearrange("p b t -> p (b t)")).then_inc(st_q[k], 16)

                def store_k(n, k, half):
                    sp.wait_ge(s["k_lo"], n + 1)
                    for i, src in enumerate((kh, kl)):
                        for c in range(KC):
                            dst = scratch["k"][c * 8:c * 8 + 8, i, :, :, :].rearrange("h d b t -> h d (b t)")
                            sp.dma_start(dst[:, :, bass.ds(n * 2 * T, 2 * T)], src[k][:, c, :]).then_inc(st_k[k], 16)

                def store_sim(n, k, half):
                    sp.wait_ge(s["sim_evac"], n + 1)
                    sp.sem_inc(s["sp_turn"], 1)
                    for i in range(2):
                        sp.dma_start(scratch["sim"][i, :, bass.ds(n * 2 * T, 2 * T)],
                                     ss[k][32 * (1 - i):32 * (1 - i) + H, :]).then_inc(st_s[k], 16)

                run_steps(sp, [(-1, NPAIR, load_h), (4, NPAIR, store_q), (4, NPAIR, store_k), (4, NPAIR, store_sim)],
                          -1, 6, 14, NS, 2)
                for j in range(2):
                    sp.wait_ge(st_q[j], 64 * NPAIR // 2)
                    sp.wait_ge(st_k[j], 64 * NPAIR // 2)
                    sp.wait_ge(st_s[j], 32 * NPAIR // 2)

            @block.gpsimd
            def _(pool):
                for i, (t, value) in enumerate(((ht[32:64, :, :], 0.0), (p2[:, P:P + PT], 0.0), (mx[96:P, :], 0.0),
                                                (mv1[96:P, :, :], 0.0), (mv2[96:P, :, :], 0.0), (su[:, :], 1.0),
                                                (mhalf[:, :], -0.5), (wg[:, :, :], 0.0))):
                    pool.memset(t, value).then_inc(s["cleared"], 1)
                    pool.wait_ge(s["cleared"], i + 1)
                pool.wait_ge(s["gss_ready"], 1)
                pool.tensor_tensor(grn[:, :], gss[:, :], mhalf[:, 0:KC], ALU.pow).then_inc(s["grn_ready"], 1)
                pool.wait_ge(s["grn_ready"], 1)

                def rstd(mv, ve, rs, i):
                    def emit(n, k, half):
                        pool.wait_ge(s[f"mv{i}_done"], (n + 1) * 3)
                        pool.sem_inc(s["pool_turn"], 1)
                        pool.tensor_scalar(ve[:, :], mv[:, :, 1], EPS, 1.0, ALU.add, ALU.mult).then_inc(s[f"ve{i}_done"], 1)
                        pool.wait_ge(s[f"ve{i}_done"], n + 1)
                        pool.tensor_tensor(rs[:, :], ve[:, :], mhalf[:, :], ALU.pow).then_inc(s[f"rs{i}_done"], 1)
                        pool.wait_ge(s[f"rs{i}_done"], n + 1)
                    return emit

                def register_copies(n, k, half):
                    pool.wait_ge(s["q_lo"], n + 1)
                    pool.sem_inc(s["pool_turn"], 1)
                    for i, t in enumerate((qh[k], ql[k])):
                        t3 = t[:, :, :, :].rearrange("p c b t -> p (c b) t")
                        pool.tensor_copy(t3[:, :, T:TQ], t3[:, :, 0:REG]).then_inc(s["q_dup"], 1)
                        pool.wait_ge(s["q_dup"], 2 * n + i + 1)
                        pool.sem_inc(s["pool_turn"], 1)

                run_steps(pool, [(4, NPAIR, register_copies), (0, NPAIR, rstd(mv1, ve1, rs1, 1)), (3, NPAIR, rstd(mv2, ve2, rs2, 2))],
                          0, 6, 16, NS, 2)

            @block.tensor
            def _(pe):
                pe.wait_ge(ld_w0, 48)
                for n in range(NE):
                    pe.wait_ge(ld_xi[n % 3], 16 * (n // 3 + 1))
                    if n >= 2:
                        pe.wait_ge(s["e_evac"], n - 1)
                    for c in range(KE):
                        mm = pe.matmul(pP[:, n % 2, 0:D], xi[n % 3][:, c, :], wt[:, c, :], start=(c == 0), stop=(c == KE - 1))
                    mm.then_inc(s["e_done"], 1)
                pe.wait_ge(ld_w1, 48)
                for i in range(KC):
                    for c in range(KC):
                        mm = pe.matmul(pV[:, 0, i * D:(i + 1) * D], wqt[:, c, i * P:(i + 1) * P], wkt[:, c, :],
                                       start=(c == 0), stop=(c == KC - 1))
                mm.then_inc(s["wqk_done"], 1)
                pe.wait_ge(s["gsq_ready"], 1)
                pe.matmul(pR[:, 0:KC], con[:, C_BB:C_BB + P], gsq[:, :], start=True, stop=True).then_inc(s["gss_done"], 1)
                pe.wait_ge(s["gblk_ready"], KC)
                for i in range(KC):
                    for c in range(KC):
                        mm = pe.matmul(pS[:, i * H:(i + 1) * H], wqt2[:, c, i * P:(i + 1) * P], gblk[:, c, :],
                                       start=(c == 0), stop=(c == KC - 1))
                mm.then_inc(s["wg_done"], 1)
                pe.wait_ge(s["wqk_ready"], 1)
                pe.wait_ge(s["wg_ready"], 1)
                pe.wait_ge(s["e_evac"], NE)

                def transpose_in(x, done):
                    for c in range(KC):
                        for j in range(3):
                            w = PT if j == 2 else P
                            mm = pe.transpose(pT[:, c, j * P:j * P + w], x[0:w, j, c * P:(c + 1) * P], ident[0:w, 0:w])
                    mm.then_inc(s[done], 1)

                def t1(n, k, half):
                    pe.wait_ge(s["x1_ready"], 3 * n + 3)
                    need(pe, s["x2t_ready"], (n - 2) * 2)
                    transpose_in(x1, "t1_done")

                def t2(n, k, half):
                    pe.wait_ge(s["x2_ready"], 3 * n + 3)
                    need(pe, s["x1t_ready"], upto((n + 3) * 2, 2 * NPAIR))
                    transpose_in(x2, "t2_done")

                def qproj(n, k, half):
                    pe.wait_ge(s["x1t_ready"], (n + 1) * 2)
                    need(pe, s["k_lo"], n - 2)
                    for m in range(KC):
                        for c in range(KC):
                            mm = pe.matmul(pP[:, m, 0:2 * T], wqk[:, c, m * P:(m + 1) * P],
                                           x1t[k][:, c, :, :].rearrange("p b t -> p (b t)"), start=(c == 0), stop=(c == KC - 1))
                    mm.then_inc(s["qt_done"], 1)

                def rows_by(lhs, rhs, done):
                    for b in range(2):
                        for c in range(KC):
                            pe.matmul(pV[:, 0, b * D:(b + 1) * D], lhs(b, c, 0, P), rhs(c), start=(c == 0), stop=(c == KC - 1))
                    for b in range(2):
                        w = GAP if b == 0 else TAIL
                        for c in range(KC):
                            mm = pe.matmul(pV[GAP * b:GAP * b + w, 1, 0:D], lhs(b, c, P, w), rhs(c), start=(c == 0), stop=(c == KC - 1))
                    mm.then_inc(s[done], 1)

                def vproj(n, k, half):
                    need(pe, s["h1_done"], (n - 1) * 3)
                    flat = x1t[k][:, :, :, :].rearrange("p c b t -> p c (b t)")
                    rows_by(lambda b, c, t, w: flat[:, c, b * T + t:b * T + t + w], lambda c: wv[:, c, :], "v_done")

                def scores(n, k, half):
                    pe.wait_ge(s["qt_ready"], n + 1)
                    need(pe, s["sm_done"], 3 * n)
                    flat = x1t[k][:, :, :, :].rearrange("p c b t -> p c (b t)")
                    for b in range(2):
                        for c in range(KC):
                            pe.matmul(pS[:, b * P:(b + 1) * P], qt[:, c, b * T:b * T + P], flat[:, c, b * T:b * T + P],
                                      start=(c == 0), stop=(c == KC - 1))
                    for b in range(2):
                        w = GAP if b == 0 else TAIL
                        for c in range(KC):
                            mm = pe.matmul(pS[GAP * b:GAP * b + w, 2 * P:2 * P + T], qt[:, c, b * T + P:b * T + P + w],
                                           flat[:, c, b * T:b * T + T], start=(c == 0), stop=(c == KC - 1))
                    mm.then_inc(s["s_done"], 1)

                def ptrans(n, k, half):
                    pe.wait_ge(s["p_ready"], 5 * n + 5)
                    need(pe, s["sim_evac"], n - 1)
                    for b in range(2):
                        pe.transpose(pR[:, b * P:(b + 1) * P], p0[:, b, :], ident)
                    pe.transpose(pR[:, 2 * P:2 * P + PT], p2[0:PT, 0:P], ident[0:PT, 0:PT])
                    pe.transpose(pR[0:PT, 2 * P + PT:2 * P + 2 * PT], p2[0:PT, P:P + PT], ident[0:PT, 0:PT]).then_inc(s["pt_done"], 1)

                def context(n, k, half):
                    pe.wait_ge(s["pts_ready"], (n + 1) * 2)
                    need(pe, s["v_ready"], upto((n + 2) * 2, 2 * NPAIR))
                    for b in range(2):
                        pe.matmul(pV[:, 0, b * D:(b + 1) * D], pts[:, b * P:(b + 1) * P], v0[k][:, b, :], start=True, stop=True)
                    for b in range(2):
                        w = GAP if b == 0 else TAIL
                        pe.matmul(pV[GAP * b:GAP * b + w, 1, 0:D], pts[:, 2 * P + GAP * b:2 * P + GAP * b + w], v0[k][:, b, :],
                                  start=True, stop=False, skip_group_check=True)
                    pe.matmul(pV[0:PT, 1, 0:D], ptt[0:PT, :], vt[k][0:PT, :], start=False, stop=True,
                              skip_group_check=True).then_inc(s["pv_done"], 1)

                def qk_columns(n, col, done):
                    for m in range(KC):
                        for c in range(KC):
                            mm = pe.matmul(pP[:, m, 0:2 * T], wqk2[:, c, col + m * P:col + (m + 1) * P],
                                           x2t[:, c, bass.ds(n * 2 * T, 2 * T)], start=(c == 0), stop=(c == KC - 1))
                    mm.then_inc(s[done], 1)

                def qcols(n, k, half):
                    pe.wait_ge(s["x2t_ready"], (n + 1) * 2)
                    need(pe, s["qt_ready"], upto(n + 3, NPAIR))
                    qk_columns(n, 0, "q_done")

                def kcols(n, k, half):
                    pe.wait_ge(s["q_lo"], n + 1)
                    qk_columns(n, D, "k_done")

                def simparts(n, k, half):
                    pe.wait_ge(s["q_hi"], 2 * n + 2)
                    need(pe, s["pts_ready"], upto((n + 2) * 2, 2 * NPAIR))
                    for c in range(KC):
                        pe.matmul(pR[32:64, 0:2 * T], con[:, C_OB + 32 * c:C_OB + 32 * c + 32], qsq[:, c, :],
                                  start=(c == 0), stop=(c == KC - 1), skip_group_check=True)
                        mm = pe.matmul(pR[0:32, 0:2 * T], wg[:, c, :], x2t[:, c, bass.ds(n * 2 * T, 2 * T)],
                                       start=(c == 0), stop=(c == KC - 1), skip_group_check=True)
                    mm.then_inc(s["sim_done"], 1)

                run_steps(pe, [(2, NPAIR, qproj), (4, NPAIR, t2), (2, NPAIR, vproj), (1, NPAIR, t1), (4, NPAIR, qcols),
                               (3, NPAIR, ptrans), (3, NPAIR, context), (4, NPAIR, kcols), (2, NPAIR, scores),
                               (4, NPAIR, simparts)], 0, *LOOP, NS, 2)

            @block.scalar
            def _(act):
                act.wait_ge(s["wqk_done"], 1)
                nc.scalar.activation(wqk[:, :, :].rearrange("p c d -> p (c d)"), pV[:, 0, :], ACT.Copy, scale=1.0 / 16.0).then_inc(s["wqk_ready"], 1)

                def exps(n, k, half):
                    act.wait_ge(s["nm_ready"], n + 1)
                    need(act, s["pt_done"], n)
                    for b in range(2):
                        nc.scalar.activation(p0[:, b, :], sm[:, b * P:(b + 1) * P], ACT.Exp, bias=nm[:, b:b + 1],
                                             accum_out=su[:, b:b + 1]).then_inc(s["p_ready"], 1)
                    nc.scalar.activation(p2[0:PT, 0:P], sm[0:PT, 2 * P:3 * P], ACT.Exp, bias=nm[0:PT, 2:3],
                                         accum_out=su[0:PT, 2:3]).then_inc(s["p_ready"], 1)
                    for b in range(2):
                        r = slice(GAP * b, GAP * b + (GAP if b == 0 else TAIL))
                        nc.scalar.activation(p2[r, P + GAP * b:P + GAP * b + TAIL], sm[r, 3 * P:2 * P + T], ACT.Exp, bias=nm[r, 2:3],
                                             accum_out=su[r, 3:4]).then_inc(s["p_ready"], 1)

                def qt_copy(n, k, half):
                    act.wait_ge(s["qt_done"], n + 1)
                    need(act, s["s_done"], n)
                    nc.scalar.activation(qt[:, :, :], pP[:, :, 0:2 * T], ACT.Copy).then_inc(s["qt_ready"], 1)

                def v_copy(n, k, half):
                    act.wait_ge(s["v_done"], n + 1)
                    nc.scalar.activation(v0[k][:, :, :].rearrange("p b d -> p (b d)"), pV[:, 0, :], ACT.Copy).then_inc(s["v_ready"], 1)
                    nc.scalar.activation(vt[k][0:PT, :], pV[0:PT, 1, 0:D], ACT.Copy).then_inc(s["v_ready"], 1)

                def x1t_copy(n, k, half):
                    act.wait_ge(s["t1_done"], n + 1)
                    need(act, s["s_done"], n - 1)
                    nc.scalar.activation(x1t[k][:, :, :, 0:P], pT[:, :, 0:2 * P].rearrange("p c (b t) -> p c b t", b=2),
                                         ACT.Copy).then_inc(s["x1t_ready"], 1)
                    nc.scalar.activation(x1t[k][:, :, :, P:T],
                                         pT[:, :, 2 * P:3 * P].rearrange("p c (b t) -> p c b t", b=2)[:, :, :, 0:TAIL],
                                         ACT.Copy).then_inc(s["x1t_ready"], 1)

                def q_high(n, k, half):
                    act.wait_ge(s["q_done"], n + 1)
                    need(act, st_q[k], half * 64)
                    need(act, s["sim_done"], n)
                    q4 = pP[:, :, 0:2 * T].rearrange("p c (b t) -> p c b t", b=2)
                    nc.scalar.activation(qsq[:, :, :], pP[:, :, 0:2 * T], ACT.Square).then_inc(s["q_hi"], 1)
                    nc.scalar.activation(qh[k][:, :, :, 0:T], q4, ACT.Copy, scale=0.25).then_inc(s["q_hi"], 1)

                def k_high(n, k, half):
                    act.wait_ge(s["k_done"], n + 1)
                    need(act, st_k[k], half * 64)
                    nc.scalar.activation(kh[k][:, :, :], pP[:, :, 0:2 * T], ACT.Copy).then_inc(s["k_hi"], 1)

                def sim_copy(n, k, half):
                    act.wait_ge(s["sim_done"], n + 1)
                    need(act, st_s[k], half * 32)
                    nc.scalar.activation(ss[k][:, :], pR[0:64, 0:2 * T], ACT.Copy).then_inc(s["sim_evac"], 1)

                run_steps(act, [(3, NPAIR, exps), (2, NPAIR, qt_copy), (2, NPAIR, v_copy), (1, NPAIR, x1t_copy), (4, NPAIR, q_high),
                                (4, NPAIR, k_high), (4, NPAIR, sim_copy)], 0, *LOOP, NS, 2)

            @block.vector
            def _(dve):
                dve.wait_ge(ld_w0, 48)
                dve.tensor_copy(ident16[:, :], ident).then_inc(s["id16_ready"], 1)
                for n in range(NE):
                    dve.wait_ge(s["e_done"], n + 1)
                    if n >= 3:
                        dve.wait_ge(st_he[n % 3], 16 * (n // 3))
                    dve.tensor_tensor(he[n % 3][:, :], pP[:, n % 2, 0:D], bt[:, :], ALU.add).then_inc(s["e_evac"], 1)
                dve.wait_ge(ld_w2, 96)
                dve.tensor_tensor(gsq[:, :], gcol[:, :], gcol[:, :], ALU.mult).then_inc(s["gsq_ready"], 1)
                dve.wait_ge(s["gss_done"], 1)
                dve.tensor_copy(gss[:, :], pR[:, 0:KC]).then_inc(s["gss_ready"], 1)
                dve.wait_ge(s["grn_ready"], 1)
                dve.tensor_tensor(gn[:, :], gcol[:, :], grn[:, :], ALU.mult).then_inc(s["gn_ready"], 1)
                dve.wait_ge(s["gn_ready"], 1)
                for c in range(KC):
                    dve.tensor_scalar(gblk[:, c, :], con[:, C_OB + 32 * c:C_OB + 32 * c + H], gn[:, c:c + 1], None,
                                      ALU.mult).then_inc(s["gblk_ready"], 1)
                dve.wait_ge(s["wg_done"], 1)
                dve.wait_ge(s["cleared"], 8)
                dve.tensor_copy(wg[:, :, 0:H], pS[:, 0:KC * H].rearrange("p (c h) -> p c h", c=KC)).then_inc(s["wg_ready"], 1)

                def rows(n, j):
                    return h0[:, bass.ds(n * 2 + j, 1), :].rearrange("p a d -> p (a d)") if j < 2 else \
                        ht[0:PT, bass.ds(n, 1), :].rearrange("p a d -> p (a d)")

                def width(j):
                    return PT if j == 2 else P

                def stats(n, st, mv, i):
                    dve.sem_inc(s["dve_turn"], 1)
                    for j in range(3):
                        dve.bn_stats(st[0:width(j), j, :], rows(n, j)).then_inc(s[f"st{i}_done"], 1)
                    dve.wait_ge(s[f"st{i}_done"], 3 * n + 3)
                    dve.sem_inc(s["dve_turn"], 1)
                    for j in range(3):
                        dve.bn_aggr(mv[0:width(j), j, :], st[0:width(j), j, :]).then_inc(s[f"mv{i}_done"], 1)

                def normalise(n, x, mv, rs, ready):
                    for j in range(3):
                        w = width(j)
                        dve.tensor_scalar(x[0:w, j, :], rows(n, j), mv[0:w, j, 0:1], rs[0:w, j:j + 1],
                                          ALU.subtract, ALU.mult).then_inc(s[ready], 1)

                def stats1(n, k, half):
                    dve.wait_ge(ld_h[k], half * 96 + 96)
                    stats(n, st1, mv1, 1)

                def norm1(n, k, half):
                    dve.wait_ge(s["rs1_done"], n + 1)
                    need(dve, s["t1_done"], n)
                    normalise(n, x1, mv1, rs1, "x1_ready")

                def masks(n, k, half):
                    dve.wait_ge(s["s_done"], n + 1)
                    need(dve, s["p_ready"], 5 * n)
                    dve.sem_inc(s["dve_turn"], 1)
                    for j, (c0, w, c) in enumerate(((0, P, C_M0), (P, P, C_M0), (2 * P, T, C_MT))):
                        r = width(j)
                        dve.tensor_tensor_reduce(sm[0:r, c0:c0 + w], pS[0:r, c0:c0 + w], con[0:r, c:c + w], 1.0, -3e38,
                                                 ALU.add, ALU.max, mx[0:r, j:j + 1]).then_inc(s["sm_done"], 1)
                    dve.wait_ge(s["sm_done"], 3 * n + 3)
                    dve.tensor_scalar(nm[:, :], mx[:, :], -1.0, None, ALU.mult).then_inc(s["nm_ready"], 1)

                def sums(n, k, half):
                    dve.wait_ge(s["p_ready"], 5 * n + 5)
                    dve.tensor_tensor(su[0:PT, 2:3], su[0:PT, 2:3], su[0:PT, 3:4], ALU.add).then_inc(s["sum_added"], 1)
                    dve.wait_ge(s["sum_added"], n + 1)
                    dve.reciprocal(rsum[:, :], su[:, 0:3]).then_inc(s["rsum_ready"], 1)

                def pts_copy(n, k, half):
                    dve.wait_ge(s["pt_done"], n + 1)
                    need(dve, s["pv_done"], n)
                    dve.tensor_copy(pts[:, :], pR[:, 0:2 * P + PT]).then_inc(s["pts_ready"], 1)
                    dve.tensor_copy(ptt[0:PT, :], pR[0:PT, 2 * P + PT:2 * P + 2 * PT]).then_inc(s["pts_ready"], 1)

                def h1_stats2(n, k, half):
                    dve.wait_ge(s["pv_done"], n + 1)
                    dve.wait_ge(s["rsum_ready"], n + 1)
                    for j in range(3):
                        r = width(j)
                        src = pV[:, 0, j * D:(j + 1) * D] if j < 2 else pV[0:PT, 1, 0:D]
                        dve.scalar_tensor_tensor(out=rows(n, j), in0=src, scalar=rsum[0:r, j:j + 1], in1=rows(n, j),
                                                 op0=ALU.mult, op1=ALU.add).then_inc(s["h1_done"], 1)
                    dve.wait_ge(s["h1_done"], 3 * n + 3)
                    stats(n, st2, mv2, 2)

                def norm2(n, k, half):
                    dve.wait_ge(s["rs2_done"], n + 1)
                    need(dve, s["t2_done"], n)
                    normalise(n, x2, mv2, rs2, "x2_ready")

                def x2t_copy(n, k, half):
                    dve.wait_ge(s["t2_done"], n + 1)
                    pair = x2t[:, :, bass.ds(n * 2 * T, 2 * T)].rearrange("p c (b t) -> p c b t", b=2)
                    dve.tensor_copy(pair[:, :, :, 0:P], pT[:, :, 0:2 * P].rearrange("p c (b t) -> p c b t", b=2)).then_inc(s["x2t_ready"], 1)
                    dve.tensor_copy(pair[:, :, :, P:T],
                                    pT[:, :, 2 * P:3 * P].rearrange("p c (b t) -> p c b t", b=2)[:, :, :, 0:TAIL]).then_inc(s["x2t_ready"], 1)

                def q_low(n, k, half):
                    dve.wait_ge(s["q_hi"], 2 * n + 2)
                    q4 = pP[:, :, 0:2 * T].rearrange("p c (b t) -> p c b t", b=2)
                    dve.scalar_tensor_tensor(out=ql[k][:, :, :, 0:T], in0=q4, scalar=0.25, in1=qh[k][:, :, :, 0:T],
                                             op0=ALU.mult, op1=ALU.subtract).then_inc(s["q_lo"], 1)

                def k_low(n, k, half):
                    dve.wait_ge(s["k_hi"], n + 1)
                    dve.tensor_tensor(kl[k][:, :, :], pP[:, :, 0:2 * T], kh[k][:, :, :], ALU.subtract).then_inc(s["k_lo"], 1)

                run_steps(dve, [(3, NPAIR, masks), (4, NPAIR, x2t_copy), (1, NPAIR, norm1), (3, NPAIR, sums), (3, NPAIR, pts_copy),
                                (4, NPAIR, q_low), (3, NPAIR, h1_stats2), (0, NPAIR, stats1), (4, NPAIR, k_low), (3, NPAIR, norm2)],
                          0, 6, 16, NS, 2)


def class_phase(nc, keep, scratch):
    con, ident16, ident = keep[:3]
    with ExitStack() as ctx:
        def sb(name, shape, dt=F32):
            return ctx.enter_context(nc.sbuf_tensor(name, shape, dt))

        def sem(name):
            return ctx.enter_context(nc.semaphore(name))

        sq = sb("sq", [P, H, QUARTER])
        num = sb("num", [P, H, QUARTER])
        nrm = sb("nrm", [P, H * QUARTER])
        rec = sb("rec", [P, H * QUARTER])
        cos = sb("cos", [P, H, QUARTER])
        sim = sb("sim", [P, QUARTER])
        nsim = sb("nsim", [P, QUARTER])
        junk = sb("junk", [P, 2, QUARTER])
        ext = sb("ext", [P, 2])
        g2 = sb("g2", [2, 1])
        gd = sb("gd", [2, 2])
        ones2 = sb("ones2", [2, P])
        rng = sb("rng", [P, 2])
        dd = sb("dd", [P, 2])
        pos = sb("pos", [P, QUARTER])
        ca = sb("ca", [P, QUARTER])
        cn = sb("cn", [P, QUARTER])
        cls = sb("cls", [P, 4, QUARTER], F16)
        ps = ctx.enter_context(nc.psum_tensor("ps_class", [P, 512], F32))
        pb = ctx.enter_context(nc.psum_tensor("ps_range", [P, 512], F32))
        ld, nrm_ready, dve_step, ext_t, ext_b, st = (sem(n) for n in
                                                     ("ld_sim", "nrm_ready", "class_step", "ext_transposed", "range_spread", "st_class"))
        with nc.Block() as block:
            @block.sync
            def _(sp):
                for i, dst in enumerate((sq, num)):
                    sp.dma_start(dst[:, :, :], scratch["sim"][i, :, :].rearrange("h (p t) -> p h t", t=QUARTER)).then_inc(ld, 16)
                sp.wait_ge(dve_step, 19)
                sp.dma_start(scratch["cls"].rearrange("r (p t) -> p r t", t=QUARTER), cls[:, :, :]).then_inc(st, 16)
                sp.wait_ge(st, 16)

            @block.scalar
            def _(act):
                act.wait_ge(ld, 32)
                nc.scalar.activation(nrm[:, :], sq[:, :, :].rearrange("p h t -> p (h t)"), ACT.Sqrt).then_inc(nrm_ready, 1)

            @block.tensor
            def _(pe):
                pe.wait_ge(dve_step, 8)
                pe.transpose(ps[0:2, 0:P], ext[:, :], ident).then_inc(ext_t, 1)
                pe.wait_ge(dve_step, 10)
                pe.matmul(pb[:, 0:2], ones2[:, :], gd[:, :], start=True, stop=True).then_inc(ext_b, 1)

            @block.vector
            def _(dve):
                chain = [0]

                def step(ins):
                    ins.then_inc(dve_step, 1)
                    chain[0] += 1
                    dve.wait_ge(dve_step, chain[0])

                step(dve.memset(ones2[:, :], 1.0))
                dve.wait_ge(nrm_ready, 1)
                step(dve.reciprocal(rec[:, :], nrm[:, :]))
                step(dve.scalar_tensor_tensor(out=cos[:, :, :].rearrange("p h t -> p (h t)"), in0=num[:, :, :].rearrange("p h t -> p (h t)"),
                                              scalar=1.0 / H, in1=rec[:, :], op0=ALU.mult, op1=ALU.mult))
                step(dve.tensor_reduce(sim[:, :], cos[:, :, :].rearrange("p h t -> p t h"), AX_X, ALU.add))
                step(dve.tensor_scalar(nsim[:, :], sim[:, :], -1.0, None, ALU.mult))
                big = con[:, C_REGBIG:C_REGBIG + QUARTER]
                step(dve.tensor_tensor_reduce(junk[:, 0, :], nsim[:, :], big, 1.0, -3e38, ALU.subtract, ALU.max, ext[:, 0:1]))
                step(dve.tensor_tensor_reduce(junk[:, 1, :], sim[:, :], big, 1.0, -3e38, ALU.subtract, ALU.max, ext[:, 1:2]))
                step(dve.memset(cls[:, :, :], 0.0))
                dve.wait_ge(ext_t, 1)
                step(dve.tensor_reduce(g2[:, :], ps[0:2, 0:P], AX_X, ALU.max))
                step(dve.tensor_scalar(gd[:, :], ident[0:2, 0:2], g2[:, 0:1], None, ALU.mult))
                dve.wait_ge(ext_b, 1)
                step(dve.tensor_copy(rng[:, :], pb[:, 0:2]))
                step(dve.tensor_tensor(dd[:, 0:1], rng[:, 0:1], rng[:, 1:2], ALU.add))
                step(dve.tensor_scalar(dd[:, 1:2], dd[:, 0:1], 0.9, None, ALU.mult))
                step(dve.tensor_scalar(pos[:, :], sim[:, :], rng[:, 0:1], dd[:, 1:2], ALU.add, ALU.is_gt))
                nreg = con[:, C_NREG:C_NREG + QUARTER]
                reg = con[:, C_REG:C_REG + QUARTER]
                step(dve.tensor_tensor(ca[:, :], pos[:, :], nreg, ALU.mult))
                dve.scalar_tensor_tensor(out=cn[:, :], in0=ca[:, :], scalar=-1.0, in1=nreg, op0=ALU.mult, op1=ALU.add).then_inc(dve_step, 1)
                chain[0] += 1
                dve.wait_ge(dve_step, chain[0])
                step(dve.tensor_scalar(cls[:, 3, :], ca[:, :], -CLASS, None, ALU.mult))
                step(dve.tensor_tensor(ca[:, :], ca[:, :], reg, ALU.add))
                dve.tensor_scalar(cls[:, 0, :], ca[:, :], CLASS, None, ALU.mult)
                dve.tensor_scalar(cls[:, 1, :], cn[:, :], CLASS, None, ALU.mult)
                dve.tensor_scalar(cls[:, 2, :], cn[:, :], -CLASS, None, ALU.mult).then_inc(dve_step, 1)


def second_phase(nc, keep, scratch, consts16, out):
    con, ident16, ident, h0, ht, x2t, wv2, wp, bp = keep
    with ExitStack() as ctx:
        def sb(name, shape, dt=F32):
            return ctx.enter_context(nc.sbuf_tensor(name, shape, dt))

        def sem(name):
            return ctx.enter_context(nc.semaphore(name))

        def ps(name, shape):
            return ctx.enter_context(nc.psum_tensor(name, shape, F32))

        QW = H * TQ + 32
        qs = [sb(f"qs{j}", [P, QW], F16) for j in range(4)]
        ks = [sb(f"ks{j}", [P, H, KPAD], F16) for j in range(4)]
        mx = [sb(f"mx{j}", [P, 24]) for j in range(2)]
        mh = [sb(f"mh{j}", [P, 24], F16) for j in range(2)]
        mr = [sb(f"mr{j}", [16, P], F16) for j in range(2)]
        mrt = [sb(f"mrt{j}", [8, P], F16) for j in range(2)]
        em = sb("em", [P, H, TQ])
        et = sb("et", [P, H // 2, TQ])
        xc = [sb(f"xc{j}", [P, KC, 2 * T]) for j in range(2)]
        vm = [sb(f"vm{j}", [P, H, 32]) for j in range(4)]
        vt = [sb(f"vt2_{j}", [P, H, 32]) for j in range(4)]
        os_ = sb("os", [P, 4, TQ])
        rd = sb("rd", [P, 2, H])
        on = sb("on", [P, 2, D])
        OFW = KC * TQ + 24
        of = [sb(f"of{j}", [P, OFW]) for j in range(2)]
        hb = sb("hb", [P, 3, D])
        ot = [sb(f"ot{j}", [P, 3, D]) for j in range(2)]

        pA = [ps(f"pA{j}", [P, 512]) for j in range(2)]
        pB = [ps(f"pB{j}", [P, 512]) for j in range(2)]
        pO = ps("pO", [P, 2, 512])
        pX = ps("pX", [P, 2, 512])
        pM16 = pX[:, 1, :].bitcast(F16)

        names = ("set_up a_done a_max mh_ready mt_done mt_evac b_done e_ready pv_done os_ready c1_done rd_ready on_ready "
                 "c2_done of_copied of_ready v_done v_ready f_done hb_ready out_ready").split()
        s = {n: sem(n) for n in names}
        ld_set = sem("ld_set")
        ld_stack = [sem(f"ld_stack{j}") for j in range(4)]
        ld_shift = [sem(f"ld_shift{j}") for j in range(4)]
        ld_xc = [sem(f"ld_xc{j}") for j in range(2)]
        st_out = [sem(f"st_out{j}") for j in range(2)]

        def q_head(j, rows, h, c0, w):
            return qs[j][0:rows, h * TQ + c0:h * TQ + c0 + w]

        GROUPS = [g for a in range(4) for g in ((False, 2 * a), (False, 2 * a + 1), (True, a))]
        NG = len(GROUPS)
        SETUP = 4 * 5 + 2
        LOOP = (8, 32)
        NSTEP = 36

        def tiles(group):
            tail, g = group
            if not tail:
                return [(2 * g + i, 0, i) for i in range(2)]
            return [(4 * g + 2 * i + j, GAP * j, i) for i in range(2) for j in range(2)]

        def pair_of(n, half, k):
            return half * 2 + k // 2

        with nc.Block() as block:

            @block.gpsimd
            def _(pool):
                blank = []
                for j in range(4):
                    blank += [(qs[j][64:P, :], 0.0), (qs[j][0:64, H * TQ:QW], 0.0), (ks[j][:, :, :], 0.0),
                              (vm[j][:, :, 16:32], 1.0), (vt[j][:, :, :], 0.0)]
                blank += [(of[j][:, KC * TQ:OFW], 0.0) for j in range(2)]
                for j in range(4):
                    v4 = vt[j][:, :, :].rearrange("p (g e) c -> p g e c", e=2)
                    blank += [(v4[GAP * e:GAP * e + TAIL, :, e, 16:17], 1.0) for e in range(2)]
                for i, (t, value) in enumerate(blank):
                    pool.memset(t, value).then_inc(s["set_up"], 1)
                    pool.wait_ge(s["set_up"], i + 1)

                def biased(n, k, half):
                    if k % 2 == 0:
                        return
                    p = pair_of(n, half, k)
                    need(pool, s["out_ready"], 3 * p)
                    pool.tensor_tensor(hb[:, 0:2, :], h0[:, bass.ds(p * 2, 2), :], bp[:, :].rearrange("p (a d) -> p a d", a=1).broadcast_to([P, 2, D]),
                                       ALU.add).then_inc(s["hb_ready"], 1)
                    pool.wait_ge(s["hb_ready"], 2 * p + 1)
                    pool.tensor_tensor(hb[0:PT, 2, :], ht[0:PT, bass.ds(p, 1), :].rearrange("p a d -> p (a d)"), bp[0:PT, :],
                                       ALU.add).then_inc(s["hb_ready"], 1)

                run_steps(pool, [(3, B, biased)], 2, *LOOP, NSTEP, 4)

            @block.sync
            def _(sp):
                sp.wait_ge(s["set_up"], SETUP + 8)
                for j in range(4):
                    q3 = qs[j][:, 0:H * TQ].rearrange("p (h t) -> p h t", h=H)
                    sp.dma_start(q3[65:66, :, T:TQ], consts16[0:1, 0:H * REG].rearrange("o (h t) -> o h t", h=H)).then_inc(ld_set, 16)
                    sp.dma_start(ks[j][SHIFT_ROW:P, :, 0:T], consts16[1:2, 0:H * T].rearrange("o (h t) -> o h t", h=H)).then_inc(ld_set, 16)

                def load_stack(n, k, half):
                    need(sp, s["b_done"], NG * (n - 3))
                    q3 = qs[k][:, 0:H * TQ].rearrange("p (h t) -> p h t", h=H)
                    for r in range(2):
                        sp.dma_start(q3[32 * r:32 * r + 32, :, :],
                                     scratch["q"][:, :, :, bass.ds(n, 1), :].rearrange("h k d b t -> (k d) h (b t)")).then_inc(ld_stack[k], 16)
                    sp.dma_start(ks[k][0:32, :, 0:T],
                                 scratch["k"][:, :, :, bass.ds(n, 1), :].rearrange("h k d b t -> (k d) h (b t)")).then_inc(ld_stack[k], 16)
                    for r, i in ((32, 1), (48, 0)):
                        sp.dma_start(ks[k][r:r + 16, :, 0:T],
                                     scratch["k"][:, i, :, bass.ds(n, 1), :].rearrange("h d b t -> d h (b t)")).then_inc(ld_stack[k], 16)
                    for i, dst in enumerate((q3[64:66, :, 0:T], ks[k][64:66, :, 0:T])):
                        row = scratch["cls"][2 * i:2 * i + 2, bass.ds(n * T, T)].rearrange("r (a t) -> r a t", a=1)
                        sp.dma_start(dst, row.broadcast_to([2, H, T])).then_inc(ld_stack[k], 16)

                def load_xc(n, k, half):
                    if k % 2 == 1:
                        return
                    p = pair_of(n, half, k)
                    need(sp, s["v_done"], p - 1)
                    sp.dma_start(xc[k // 2][:, :, :], x2t[:, :, bass.ds(p * 2 * T, 2 * T)]).then_inc(ld_xc[k // 2], 16)

                def load_shift(n, k, half):
                    sp.wait_ge(s["mt_evac"], 2 * n + 2)
                    q3 = qs[k][:, 0:H * TQ].rearrange("p (h t) -> p h t", h=H)
                    q4 = qs[k][:, 0:H * TQ].rearrange("p (g e t) -> p g e t", e=2, t=TQ)
                    sp.dma_start(q3[SHIFT_ROW:P, :, 0:P], mr[k % 2][:, :]).then_inc(ld_shift[k], 16)
                    for e in range(2):
                        sp.dma_start(q4[SHIFT_ROW:P, :, e, P:TQ], mrt[k % 2][:, GAP * e:GAP * e + QTAIL]).then_inc(ld_shift[k], 16)

                def store_out(n, k, half):
                    if k % 2 == 0:
                        return
                    p = pair_of(n, half, k)
                    pp = k // 2
                    sp.wait_ge(s["out_ready"], 3 * p + 3)
                    sp.dma_start(out[bass.ds(p * 2, 2), 0:P, :].rearrange("b t d -> t b d"), ot[pp][:, 0:2, :]).then_inc(st_out[pp], 16)
                    for b in range(2):
                        sp.dma_start(out[bass.ds(p * 2 + b, 1), P:T, :].rearrange("b t d -> t (b d)"),
                                     ot[pp][GAP * b:GAP * b + TAIL, 2, :]).then_inc(st_out[pp], 16)

                run_steps(sp, [(-1, B, load_stack), (0, B, load_xc), (1, B, load_shift), (3, B, store_out)], -1, 4, 28, NSTEP, 4)
                for j in range(2):
                    sp.wait_ge(st_out[j], 48 * NPAIR // 2)

            @block.tensor
            def _(pe):
                pe.wait_ge(ld_set, 128)
                pe.wait_ge(s["set_up"], SETUP + 8)

                def logits(pD, group, n, k, rows, shifted):
                    for h, at, slot in tiles(group):
                        if shifted:
                            lhs = ks[k][:, h, P:KPAD] if group[0] else ks[k][:, h, 0:P]
                            rhs = q_head(k, P, h, 0, TQ)
                        else:
                            lhs = q_head(k, rows, h, P, GAP) if group[0] else q_head(k, rows, h, 0, P)
                            rhs = ks[k][0:rows, h, 0:T]
                        w = TQ if shifted else T
                        m = GAP if group[0] else P
                        mm = pe.matmul(pD[at:at + m, slot * w:(slot + 1) * w], lhs, rhs, start=True, stop=True)
                    return mm

                def a_group(i):
                    def emit(n, k, half):
                        if i == 0:
                            pe.wait_ge(ld_stack[k], half * 112 + 112)
                        need(pe, s["a_max"], NG * n + i - 1)
                        logits(pA[i % 2], GROUPS[i], n, k, SHIFT_ROW, False).then_inc(s["a_done"], 1)
                    return emit

                def b_group(i):
                    def emit(n, k, half):
                        if i == 0:
                            pe.wait_ge(ld_shift[k], half * 48 + 48)
                        need(pe, s["e_ready"], NG * n + i - 1)
                        logits(pB[i % 2], GROUPS[i], n, k, P, True).then_inc(s["b_done"], 1)
                    return emit

                def pv_group(a):
                    def emit(n, k, half):
                        if a == 0:
                            p = pair_of(n, half, k)
                            pe.wait_ge(s["v_ready"], 6 * p + 6)
                            need(pe, s["os_ready"], n)
                        pe.wait_ge(s["e_ready"], NG * n + 3 * a + 3)
                        for q in range(4):
                            h = 4 * a + q
                            dst = pO[32 * q:32 * q + 32, a // 2, (a % 2) * TQ:(a % 2 + 1) * TQ]
                            pe.matmul(dst, vm[k][:, h, :], em[:, h, :], start=True, stop=False, skip_group_check=True)
                        for q in range(4):
                            h = 4 * a + q
                            dst = pO[32 * q:32 * q + 32, a // 2, (a % 2) * TQ:(a % 2 + 1) * TQ]
                            mm = pe.matmul(dst, vt[k][:, h, :], et[:, h // 2, :], start=False, stop=True, skip_group_check=True)
                        mm.then_inc(s["pv_done"], 1)
                    return emit

                def max_rows(n, k, half):
                    pe.wait_ge(s["mh_ready"], n + 1)
                    if k % 2 == 0:
                        need(pe, s["out_ready"], 3 * (pair_of(n, half, k) - 1))
                    else:
                        need(pe, s["v_ready"], 6 * (pair_of(n, half, k) + 1))
                    pe.transpose(pM16[0:16, 0:P], mh[k % 2][:, 0:16], ident16[:, :])
                    pe.transpose(pM16[0:8, P:2 * P], mh[k % 2][:, 16:24], ident16[:, :]).then_inc(s["mt_done"], 1)

                def c1(n, k, half):
                    pe.wait_ge(s["os_ready"], n + 1)
                    need(pe, s["mt_evac"], upto(2 * n + 6, 2 * B))
                    if isinstance(n, int) and n == B - 2:
                        pe.wait_ge(s["out_ready"], 3 * (NPAIR - 1))
                    if isinstance(n, int) and n == B - 1:
                        pe.wait_ge(s["of_copied"], n)
                    for a in range(4):
                        pe.transpose(pX[:, 0, a * P:(a + 1) * P], os_[:, a, 0:P], ident)
                    for a in range(4):
                        mm = pe.transpose(pX[0:QTAIL, 1, a * P:(a + 1) * P], os_[:, a, P:TQ], ident)
                    mm.then_inc(s["c1_done"], 1)

                def c2(n, k, half):
                    pe.wait_ge(s["on_ready"], 2 * n + 2)
                    for c in range(KC):
                        pe.transpose(pX[:, 0, c * TQ:c * TQ + P], on[:, 0, c * P:(c + 1) * P], ident)
                        mm = pe.transpose(pX[:, 0, c * TQ + P:(c + 1) * TQ], on[0:QTAIL, 1, c * P:(c + 1) * P], ident[0:QTAIL, 0:QTAIL])
                    mm.then_inc(s["c2_done"], 1)

                def rows_of(lhs, w_, done):
                    for b in range(2):
                        for c in range(KC):
                            pe.matmul(pX[:, 0, b * D:(b + 1) * D], lhs(b, c, 0, P), w_[:, c, :], start=(c == 0), stop=(c == KC - 1))
                    for b in range(2):
                        w = GAP if b == 0 else TAIL
                        for c in range(KC):
                            mm = pe.matmul(pX[GAP * b:GAP * b + w, 1, 0:D], lhs(b, c, P, w), w_[:, c, :], start=(c == 0), stop=(c == KC - 1))
                    mm.then_inc(s[done], 1)

                def vproj(n, k, half):
                    if k % 2 == 1:
                        return
                    p, pp = pair_of(n, half, k), k // 2
                    pe.wait_ge(ld_xc[pp], half * 16 + 16)
                    pe.wait_ge(s["mt_evac"], 2 * n + 2)
                    need(pe, s["of_copied"], n - 1)
                    rows_of(lambda b, c, t, w: xc[pp][:, c, b * T + t:b * T + t + w], wv2, "v_done")

                def project(n, k, half):
                    if k % 2 == 0:
                        return
                    pe.wait_ge(s["of_ready"], n + 1)
                    rows_of(lambda b, c, t, w: of[b][:, c * TQ + t:c * TQ + t + w], wp, "f_done")

                between = {1: [(3, B, pv_group(3)), (1, B, max_rows)], 3: [(3, B, c1)], 4: [(2, B, pv_group(0))], 6: [(3, B, c2)],
                           7: [(2, B, pv_group(1))], 9: [(1, B, vproj), (3, B, project)], 10: [(2, B, pv_group(2))]}
                run_steps(pe, [stage for i in range(NG) for stage in [(2, B, b_group(i)), (0, B, a_group(i))] + between.get(i, [])],
                          0, *LOOP, NSTEP, 4)

            @block.scalar
            def _(act):
                act.wait_ge(s["set_up"], SETUP + 8)

                def mt_copy(n, k, half):
                    act.wait_ge(s["mt_done"], n + 1)
                    if not isinstance(n, int) or n >= 2:
                        act.wait_ge(ld_shift[(k - 2) % 4], 48 * (half + 1 if k >= 2 else half))
                    nc.scalar.activation(mr[k % 2][:, :], pM16[0:16, 0:P], ACT.Copy).then_inc(s["mt_evac"], 1)
                    nc.scalar.activation(mrt[k % 2][:, :], pM16[0:8, P:2 * P], ACT.Copy).then_inc(s["mt_evac"], 1)

                def os_copy(n, k, half):
                    act.wait_ge(s["pv_done"], 4 * n + 4)
                    need(act, s["c1_done"], n)
                    nc.scalar.activation(os_[:, :, :].rearrange("p (i a) t -> p i (a t)", i=2), pO[:, :, 0:2 * TQ], ACT.Copy).then_inc(s["os_ready"], 1)

                def of_copy(n, k, half):
                    act.wait_ge(s["c2_done"], n + 1)
                    nc.scalar.activation(of[k % 2][:, 0:KC * TQ], pX[:, 0, 0:KC * TQ], ACT.Copy).then_inc(s["of_copied"], 1)

                def v_copy(n, k, half):
                    if k % 2 == 1:
                        return
                    p = pair_of(n, half, k)
                    act.wait_ge(s["v_done"], p + 1)
                    need(act, s["pv_done"], 4 * (n - 2))
                    for b in range(2):
                        nc.scalar.activation(vm[k + b][:, :, 0:16], pX[:, 0, b * D:(b + 1) * D].rearrange("p (h d) -> p h d", h=H),
                                             ACT.Copy).then_inc(s["v_ready"], 1)
                    for b in range(2):
                        src = pX[GAP * b:GAP * b + TAIL, 1, 0:D].rearrange("p (g e d) -> p g e d", e=2, d=DH)
                        dst = vt[k + b][:, :, 0:16].rearrange("p (g e) d -> p g e d", e=2)
                        for e in range(2):
                            nc.scalar.activation(dst[GAP * e:GAP * e + TAIL, :, e, :], src[:, :, e, :], ACT.Copy).then_inc(s["v_ready"], 1)

                def e_group(i):
                    tail, g = GROUPS[i]

                    def emit(n, k, half):
                        act.wait_ge(s["b_done"], NG * n + i + 1)
                        need(act, s["pv_done"], 4 * (n - 1) + i // 3 + 1)
                        dst = (et if tail else em)[:, 2 * g:2 * g + 2, :].rearrange("p a t -> p (a t)")
                        nc.scalar.activation(dst, pB[i % 2][:, 0:2 * TQ], ACT.Exp).then_inc(s["e_ready"], 1)
                    return emit

                between = {0: [(1, B, mt_copy)], 1: [(3, B, os_copy)], 6: [(3, B, of_copy)], 9: [(1, B, v_copy)]}
                run_steps(act, [stage for i in range(NG) for stage in [(2, B, e_group(i))] + between.get(i, [])], 0, *LOOP, NSTEP, 4)

            @block.vector
            def _(dve):
                dve.wait_ge(s["set_up"], SETUP + 8)

                def a_max(i):
                    tail, g = GROUPS[i]

                    def emit(n, k, half):
                        dve.wait_ge(s["a_done"], NG * n + i + 1)
                        c0 = 16 + 2 * g if tail else 2 * g
                        dve.tensor_reduce(mx[k % 2][:, c0:c0 + 2], pA[i % 2][:, 0:2 * T].rearrange("p (a t) -> p a t", t=T),
                                          AX_X, ALU.max).then_inc(s["a_max"], 1)
                    return emit

                def negate(n, k, half):
                    dve.wait_ge(s["a_max"], NG * n + NG)
                    need(dve, s["mt_done"], n - 1)
                    dve.tensor_scalar(mh[k % 2][:, :], mx[k % 2][:, :], -1.0, -CLASS, ALU.mult, ALU.max).then_inc(s["mh_ready"], 1)

                def norm(n, k, half):
                    dve.wait_ge(s["c1_done"], n + 1)
                    need(dve, s["c2_done"], n)
                    for i, r in ((0, P), (1, QTAIL)):
                        t4 = pX[0:r, i, :].rearrange("p (h e) -> p h e", e=32)
                        dve.reciprocal(rd[0:r, i, :].rearrange("p (h a) -> p h a", a=1), t4[:, :, 16:17]).then_inc(s["rd_ready"], 1)
                    dve.wait_ge(s["rd_ready"], 2 * n + 2)
                    for i, r in ((0, P), (1, QTAIL)):
                        t4 = pX[0:r, i, :].rearrange("p (h e) -> p h e", e=32)
                        dve.scalar_tensor_tensor(out=on[0:r, i, :].rearrange("p (h d) -> p h d", h=H), in0=t4[:, :, 0:16],
                                                 scalar=con[0:r, C_HALF + i:C_HALF + i + 1],
                                                 in1=rd[0:r, i, :].rearrange("p (h a) -> p h a", a=1).broadcast_to([r, H, DH]),
                                                 op0=ALU.mult, op1=ALU.mult).then_inc(s["on_ready"], 1)

                def registers(n, k, half):
                    dve.wait_ge(s["of_copied"], n + 1)
                    o3 = of[k % 2][:, 0:KC * TQ].rearrange("p (c t) -> p c t", c=KC)
                    dve.tensor_tensor(o3[:, :, 0:REG], o3[:, :, 0:REG], o3[:, :, T:TQ], ALU.add).then_inc(s["of_ready"], 1)

                def residual(n, k, half):
                    if k % 2 == 0:
                        return
                    p, pp = pair_of(n, half, k), k // 2
                    dve.wait_ge(s["f_done"], p + 1)
                    dve.wait_ge(s["hb_ready"], 2 * p + 2)
                    need(dve, st_out[pp], 48 * half)
                    for j in range(3):
                        r = PT if j == 2 else P
                        src = pX[:, 0, j * D:(j + 1) * D] if j < 2 else pX[0:PT, 1, 0:D]
                        dve.tensor_tensor(ot[pp][0:r, j, :], src, hb[0:r, j, :], ALU.add).then_inc(s["out_ready"], 1)

                between = {3: [(3, B, norm)], 7: [(3, B, registers)], 10: [(3, B, residual)], 11: [(0, B, negate)]}
                run_steps(dve, [stage for i in range(NG) for stage in [(0, B, a_max(i))] + between.get(i, [])], 0, *LOOP, NSTEP, 4)


def _constants(np):
    c = np.zeros((P, C_END), np.float32)
    r = np.arange(P)
    c[:, C_ID:C_ID + P] = np.eye(P)
    c[:, C_M0:C_M0 + P] = np.where(r[None, :] <= r[:, None], 0.0, MASKED)
    query = np.where(r < TAIL, P + r, np.where(r >= GAP, P + r - GAP, T))
    c[:, C_MT:C_MT + T] = np.where(np.arange(T)[None, :] <= query[:, None], 0.0, MASKED)
    c[:, C_BB:C_BB + P] = r[:, None] // DH == r[None, :] // DH
    for k in range(KC):
        c[:, C_OB + 32 * k:C_OB + 32 * k + H] = (k * P + r[:, None]) // DH == np.arange(H)[None, :]
    reg = (r[:, None] % 4 == 0) & (np.arange(QUARTER)[None, :] < REG)
    c[:, C_REGBIG:C_REGBIG + QUARTER] = np.where(reg, -MASKED, 0.0)
    c[:, C_NREG:C_NREG + QUARTER] = ~reg
    c[:, C_REG:C_REG + QUARTER] = reg
    c[:, C_HALF] = np.where(r < REG, 0.5, 1.0)
    c[:, C_HALF + 1] = np.where((r >= TAIL) & (r < QTAIL), 0.5, 1.0)
    c16 = np.zeros((2, H * T), np.float16)
    c16[0, 0:H * REG] = CLASS
    c16[1, :] = 1.0
    return c, c16


def kernel(**inputs):
    import numpy as np
    import concourse.bacc as bacc
    from concourse.bass_utils import run_bass_kernel_spmd

    a = {n: np.asarray(v) for n, v in inputs.items()}

    def chunks(w):
        return np.ascontiguousarray(w.reshape(-1, P, w.shape[1]).transpose(1, 0, 2))

    side = 16
    n = a["x"].shape[1] // side
    patches = a["x"].reshape(B, n, side, n, side, 3).transpose(2, 4, 5, 0, 1, 3).reshape(KE, P, NE, P)
    c, c16 = _constants(np)
    arrays = {
        "xt": np.ascontiguousarray(patches.transpose(1, 2, 0, 3)),
        "txt": np.ascontiguousarray(a["txt"]),
        "w_tok": chunks(a["L0_tok_W"].T),
        "b_tok": a["L0_tok_b"].reshape(1, D),
        "a_wqt": chunks(a["L0_attn_W_Q"].T),
        "a_wkt": chunks(a["L0_attn_W_K"].T),
        "a_wv": chunks(a["L0_attn_W_V"]),
        "f_wqkv": chunks(a["L0_ffn_W_qkv"]),
        "f_wqt": chunks(a["L0_ffn_W_qkv"][:, 0:D].T),
        "f_g": np.ascontiguousarray(a["L0_ffn_g_info"][0, 0].reshape(KC, P).T),
        "f_wp": chunks(a["L0_ffn_W_proj"]),
        "f_bp": a["L0_ffn_b_proj"].reshape(1, D),
        "consts": c,
        "consts16": c16,
    }
    nc = bacc.Bacc("TRN2", target_bir_lowering=False, num_devices=1)
    args = [nc.dram_tensor(m, v.shape, mybir.dt.from_np(v.dtype), kind="ExternalInput").ap() for m, v in arrays.items()]
    out = nc.dram_tensor("out", (B, T, D), F32, kind="ExternalOutput").ap()
    fusion_program(nc, *args, out)
    r = run_bass_kernel_spmd(nc, [arrays], core_ids=[0])
    return r.results[0]["out"]
```

```python
from contextlib import ExitStack

import concourse.bass as bass
from concourse import mybir

F32 = mybir.dt.float32
F16 = mybir.dt.float16
ALU = mybir.AluOpType
ACT = mybir.ActivationFunctionType
AX_X = mybir.AxisListType.X

B, D = 32, 256
NTOK, NTXT = 36, 128
T = NTOK + NTXT
PATCH = 768
H, DH, REG = 16, 16, 5
P = 128
TAIL = T - P
GAP = 64
PT = GAP + TAIL
NPAIR = B // 2
TQ = T + REG
QTAIL = TQ - P
KC = D // P
NE = B * NTOK // P
KE = PATCH // P
EPS = 1e-5
MASKED = -1e30
QUARTER = T // 4
CLASS = 60000.0
KPAD = 192
TWO_ONES = (1 + 15 * 2.0 ** -13) * 2.0 ** -7
SHIFT_ROW = 127

C_ID, C_M0, C_MT, C_BB, C_OB = 0, 128, 256, 420, 548
C_REGBIG, C_NREG, C_REG, C_HALF = 612, 653, 694, 735
C_END = 737


def need(eng, sem, count):
    if not isinstance(count, int) or count > 0:
        eng.wait_ge(sem, count)


def upto(count, most):
    return min(count, most) if isinstance(count, int) else count


def run_steps(eng, stages, first, loop_from, loop_to, last, unroll):
    def one(step, t, u):
        for lag, total, emit in stages:
            if t is None:
                n = step - lag
                if 0 <= n < total:
                    emit(n, n % unroll, n // unroll)
            else:
                emit(t * unroll + (u - lag), (u - lag) % unroll, t + (u - lag) // unroll)

    for step in range(first, loop_from):
        one(step, None, 0)
    with eng.Fori(loop_from // unroll, loop_to // unroll) as t:
        for u in range(unroll):
            one(None, t, u)
    for step in range(loop_to, last):
        one(step, None, 0)


def fusion_program(nc, xt, txt, w_tok, b_tok, a_wqt, a_wkt, a_wv, f_wqkv, f_wqt, f_g, f_wp, f_bp, consts, consts16, out):
    scratch = {
        "h_tok": nc.dram_tensor("h_tok", (B * NTOK, D), F32).ap(),
        "q": nc.dram_tensor("q_split", (H, 2, DH, B, TQ), F16).ap(),
        "k": nc.dram_tensor("k_split", (H, 2, DH, B, T), F16).ap(),
        "sim": nc.dram_tensor("sim_parts", (2, H, B * T), F32).ap(),
        "cls": nc.dram_tensor("class_rows", (4, B * T), F16).ap(),
    }
    with ExitStack() as whole:
        def sb(name, shape, dt=F32, ctx=whole):
            return ctx.enter_context(nc.sbuf_tensor(name, shape, dt))

        con = sb("con", [P, C_END])
        ident16 = sb("ident16", [P, P], F16)
        h0 = sb("h0", [P, B, D])
        ht = sb("ht", [P, NPAIR, D])
        x2t = sb("x2t", [P, KC, B * T])
        wv2 = sb("wv2", [P, KC, D])
        wp = sb("wp", [P, KC, D])
        bp = sb("bp", [P, D])
        ident = con[:, C_ID:C_ID + P]
        keep = (con, ident16, ident, h0, ht, x2t, wv2, wp, bp)
        first_phase(nc, keep, scratch, xt, txt, w_tok, b_tok, a_wqt, a_wkt, a_wv, f_wqkv, f_wqt, f_g, f_wp, f_bp, consts)
        second_phase(nc, keep, scratch, consts16, out)


def first_phase(nc, keep, scratch, xt, txt, w_tok, b_tok, a_wqt, a_wkt, a_wv, f_wqkv, f_wqt, f_g, f_wp, f_bp, consts):
    con, ident16, ident, h0, ht, x2t, wv2, wp, bp = keep
    with ExitStack() as ctx:
        def sb(name, shape, dt=F32):
            return ctx.enter_context(nc.sbuf_tensor(name, shape, dt))

        def sem(name):
            return ctx.enter_context(nc.semaphore(name))

        wt = sb("wt", [P, KE, D])
        bt = sb("bt", [P, D])
        wqt, wkt, wv = (sb(n, [P, KC, D]) for n in ("wqt", "wkt", "wv"))
        wqk = sb("wqk", [P, KC, D])
        wqk2 = sb("wqk2", [P, KC, 2 * D])
        wqt2 = sb("wqt2", [P, KC, D])
        gcol = sb("gcol", [P, KC])
        gsq = sb("gsq", [P, KC])
        gss = sb("gss", [P, KC])
        grn = sb("grn", [P, KC])
        gn = sb("gn", [P, KC])
        gblk = sb("gblk", [P, KC, H])
        wg = sb("wg", [P, KC, 32])
        mhalf = sb("mhalf", [P, 3])
        xi = [sb(f"xi{j}", [P, KE, P]) for j in range(3)]
        he = [sb(f"he{j}", [P, D]) for j in range(3)]
        st1, st2 = sb("st1", [P, 3, 6]), sb("st2", [P, 3, 6])
        mv1, mv2 = sb("mv1", [P, 3, 2]), sb("mv2", [P, 3, 2])
        ve1, ve2 = sb("ve1", [P, 3]), sb("ve2", [P, 3])
        rs1, rs2 = sb("rs1", [P, 3]), sb("rs2", [P, 3])
        x1, x2 = sb("x1", [P, 3, D]), sb("x2", [P, 3, D])
        x1t = [sb(f"x1t{j}", [P, KC, 2, T]) for j in range(2)]
        qt = sb("qt", [P, KC, 2 * T])
        v0 = [sb(f"v0_{j}", [P, 2, D]) for j in range(2)]
        vt = [sb(f"vt_{j}", [P, D]) for j in range(2)]
        sm = sb("sm", [P, 2 * P + T])
        mx, nm, su, rsum = sb("mx", [P, 3]), sb("nm", [P, 3]), sb("su", [P, 4]), sb("rsum", [P, 3])
        p0 = sb("p0", [P, 2, P])
        p2 = sb("p2", [P, P + PT])
        pts = sb("pts", [P, 2 * P + PT])
        ptt = sb("ptt", [P, PT])
        qh, ql = ([sb(f"{n}{j}", [P, KC, 2, TQ], F16) for j in range(2)] for n in ("qh", "ql"))
        kh, kl = ([sb(f"{n}{j}", [P, KC, 2 * T], F16) for j in range(2)] for n in ("kh", "kl"))
        qsq = sb("qsq", [P, KC, 2 * T])
        ss = [sb(f"ss{j}", [64, 2 * T]) for j in range(2)]

        def ps(name, shape):
            return ctx.enter_context(nc.psum_tensor(name, shape, F32))

        pT = ps("pT", [P, 2, 512])
        pP = ps("pP", [P, 2, 512])
        pV = ps("pV", [P, 2, 512])
        pS = ps("pS", [P, 512])
        pR = ps("pR", [P, 512])

        ld_w0, ld_w1, ld_w2 = sem("ld_w0"), sem("ld_w1"), sem("ld_w2")
        ld_xi = [sem(f"ld_xi{j}") for j in range(3)]
        ld_h = [sem(f"ld_h{j}") for j in range(2)]
        names = ("cleared e_done e_evac wqk_done wqk_ready gsq_ready gss_done gss_ready grn_ready gn_ready gblk_ready "
                 "wg_done wg_ready id16_ready st1_done mv1_done ve1_done rs1_done x1_ready t1_done x1t_ready qt_done qt_ready "
                 "v_done v_ready s_done sm_done nm_ready p_ready sum_added rsum_ready pt_done pts_ready pv_done h1_done "
                 "st2_done mv2_done ve2_done rs2_done x2_ready t2_done x2t_ready q_done q_hi q_lo q_dup k_done k_hi k_lo "
                 "sim_done sim_evac dve_turn pool_turn sp_turn").split()
        s = {n: sem(n) for n in names}
        st_he = [sem(f"st_he{j}") for j in range(3)]
        st_q = [sem(f"st_q{j}") for j in range(2)]
        st_k = [sem(f"st_k{j}") for j in range(2)]
        st_s = [sem(f"st_s{j}") for j in range(2)]

        NS = 20
        LOOP = (6, 16)

        with nc.Block() as block:

            @block.sync
            def _(sp):
                sp.dma_start(wt[:, :, :], w_tok).then_inc(ld_w0, 16)
                sp.dma_start(bt[:, :], b_tok.broadcast_to([P, D])).then_inc(ld_w0, 16)
                sp.dma_start(con[:, :], consts).then_inc(ld_w0, 16)
                for j in range(3):
                    sp.dma_start(xi[j][:, :, :], xt[:, j, :, :]).then_inc(ld_xi[j], 16)
                for dst, src in ((wqt, a_wqt), (wkt, a_wkt), (wv, a_wv)):
                    sp.dma_start(dst[:, :, :], src).then_inc(ld_w1, 16)
                sp.dma_start(wqk2[:, :, :], f_wqkv[:, :, 0:2 * D]).then_inc(ld_w2, 16)
                sp.dma_start(wv2[:, :, :], f_wqkv[:, :, 2 * D:3 * D]).then_inc(ld_w2, 16)
                sp.dma_start(wqt2[:, :, :], f_wqt).then_inc(ld_w2, 16)
                sp.dma_start(gcol[:, :], f_g).then_inc(ld_w2, 16)
                sp.dma_start(wp[:, :, :], f_wp).then_inc(ld_w2, 16)
                sp.dma_start(bp[:, :], f_bp.broadcast_to([P, D])).then_inc(ld_w2, 16)
                for g in range(NE // 3):
                    for j in range(3):
                        n = 3 * g + j
                        sp.wait_ge(s["e_evac"], n + 1)
                        sp.dma_start(scratch["h_tok"][n * P:(n + 1) * P, :], he[j][:, :]).then_inc(st_he[j], 16)
                        if n + 3 < NE:
                            sp.dma_start(xi[j][:, :, :], xt[:, n + 3, :, :]).then_inc(ld_xi[j], 16)
                for j in range(3):
                    sp.wait_ge(st_he[j], 16 * NE // 3)
                sp.wait_ge(s["cleared"], 1)

                def load_h(n, k, half):
                    need(sp, s["st1_done"], (n - 1) * 3)
                    for b in range(2):
                        tok = scratch["h_tok"][bass.ds(n * 2 * NTOK + b * NTOK, NTOK), :]
                        sp.dma_start(h0[0:NTOK, bass.ds(n * 2 + b, 1), :], tok).then_inc(ld_h[k], 16)
                        sp.dma_start(h0[NTOK:P, bass.ds(n * 2 + b, 1), :],
                                     txt[bass.ds(n * 2 + b, 1), 0:P - NTOK, :].rearrange("b t d -> t b d")).then_inc(ld_h[k], 16)
                        sp.dma_start(ht[GAP * b:GAP * b + TAIL, bass.ds(n, 1), :],
                                     txt[bass.ds(n * 2 + b, 1), P - NTOK:NTXT, :].rearrange("b t d -> t b d")).then_inc(ld_h[k], 16)

                def store_q(n, k, half):
                    sp.wait_ge(s["q_dup"], 2 * n + 2)
                    for i, src in enumerate((qh, ql)):
                        for c in range(KC):
                            dst = scratch["q"][c * 8:c * 8 + 8, i, :, :, :].rearrange("h d b t -> h d (b t)")
                            sp.dma_start(dst[:, :, bass.ds(n * 2 * TQ, 2 * TQ)],
                                         src[k][:, c, :, :].rearrange("p b t -> p (b t)")).then_inc(st_q[k], 16)

                def store_k(n, k, half):
                    sp.wait_ge(s["k_lo"], n + 1)
                    for i, src in enumerate((kh, kl)):
                        for c in range(KC):
                            dst = scratch["k"][c * 8:c * 8 + 8, i, :, :, :].rearrange("h d b t -> h d (b t)")
                            sp.dma_start(dst[:, :, bass.ds(n * 2 * T, 2 * T)], src[k][:, c, :]).then_inc(st_k[k], 16)

                def store_sim(n, k, half):
                    sp.wait_ge(s["sim_evac"], n + 1)
                    sp.sem_inc(s["sp_turn"], 1)
                    for i in range(2):
                        sp.dma_start(scratch["sim"][i, :, bass.ds(n * 2 * T, 2 * T)],
                                     ss[k][32 * (1 - i):32 * (1 - i) + H, :]).then_inc(st_s[k], 16)

                run_steps(sp, [(-1, NPAIR, load_h), (4, NPAIR, store_q), (4, NPAIR, store_k), (4, NPAIR, store_sim)],
                          -1, 6, 14, NS, 2)
                for j in range(2):
                    sp.wait_ge(st_q[j], 64 * NPAIR // 2)
                    sp.wait_ge(st_k[j], 64 * NPAIR // 2)
                    sp.wait_ge(st_s[j], 32 * NPAIR // 2)

            @block.gpsimd
            def _(pool):
                for i, (t, value) in enumerate(((ht[32:64, :, :], 0.0), (p2[:, P:P + PT], 0.0), (mx[96:P, :], 0.0),
                                                (mv1[96:P, :, :], 0.0), (mv2[96:P, :, :], 0.0), (su[:, :], 1.0),
                                                (mhalf[:, :], -0.5), (wg[:, :, :], 0.0))):
                    pool.memset(t, value).then_inc(s["cleared"], 1)
                    pool.wait_ge(s["cleared"], i + 1)
                pool.wait_ge(s["gss_ready"], 1)
                pool.tensor_tensor(grn[:, :], gss[:, :], mhalf[:, 0:KC], ALU.pow).then_inc(s["grn_ready"], 1)
                pool.wait_ge(s["grn_ready"], 1)

                def rstd(mv, ve, rs, i):
                    def emit(n, k, half):
                        pool.wait_ge(s[f"mv{i}_done"], (n + 1) * 3)
                        pool.sem_inc(s["pool_turn"], 1)
                        pool.tensor_scalar(ve[:, :], mv[:, :, 1], EPS, 1.0, ALU.add, ALU.mult).then_inc(s[f"ve{i}_done"], 1)
                        pool.wait_ge(s[f"ve{i}_done"], n + 1)
                        pool.tensor_tensor(rs[:, :], ve[:, :], mhalf[:, :], ALU.pow).then_inc(s[f"rs{i}_done"], 1)
                        pool.wait_ge(s[f"rs{i}_done"], n + 1)
                    return emit

                def register_copies(n, k, half):
                    pool.wait_ge(s["q_lo"], n + 1)
                    pool.sem_inc(s["pool_turn"], 1)
                    for i, t in enumerate((qh[k], ql[k])):
                        t3 = t[:, :, :, :].rearrange("p c b t -> p (c b) t")
                        pool.tensor_copy(t3[:, :, T:TQ], t3[:, :, 0:REG]).then_inc(s["q_dup"], 1)
                        pool.wait_ge(s["q_dup"], 2 * n + i + 1)
                        pool.sem_inc(s["pool_turn"], 1)

                run_steps(pool, [(4, NPAIR, register_copies), (0, NPAIR, rstd(mv1, ve1, rs1, 1)), (3, NPAIR, rstd(mv2, ve2, rs2, 2))],
                          0, 6, 16, NS, 2)

            @block.tensor
            def _(pe):
                pe.wait_ge(ld_w0, 48)
                for n in range(NE):
                    pe.wait_ge(ld_xi[n % 3], 16 * (n // 3 + 1))
                    if n >= 2:
                        pe.wait_ge(s["e_evac"], n - 1)
                    for c in range(KE):
                        mm = pe.matmul(pP[:, n % 2, 0:D], xi[n % 3][:, c, :], wt[:, c, :], start=(c == 0), stop=(c == KE - 1))
                    mm.then_inc(s["e_done"], 1)
                pe.wait_ge(ld_w1, 48)
                for i in range(KC):
                    for c in range(KC):
                        mm = pe.matmul(pV[:, 0, i * D:(i + 1) * D], wqt[:, c, i * P:(i + 1) * P], wkt[:, c, :],
                                       start=(c == 0), stop=(c == KC - 1))
                mm.then_inc(s["wqk_done"], 1)
                pe.wait_ge(s["gsq_ready"], 1)
                pe.matmul(pR[:, 0:KC], con[:, C_BB:C_BB + P], gsq[:, :], start=True, stop=True).then_inc(s["gss_done"], 1)
                pe.wait_ge(s["gblk_ready"], KC)
                for i in range(KC):
                    for c in range(KC):
                        mm = pe.matmul(pS[:, i * H:(i + 1) * H], wqt2[:, c, i * P:(i + 1) * P], gblk[:, c, :],
                                       start=(c == 0), stop=(c == KC - 1))
                mm.then_inc(s["wg_done"], 1)
                pe.wait_ge(s["wqk_ready"], 1)
                pe.wait_ge(s["wg_ready"], 1)
                pe.wait_ge(s["e_evac"], NE)

                def transpose_in(x, done):
                    for c in range(KC):
                        for j in range(3):
                            w = PT if j == 2 else P
                            mm = pe.transpose(pT[:, c, j * P:j * P + w], x[0:w, j, c * P:(c + 1) * P], ident[0:w, 0:w])
                    mm.then_inc(s[done], 1)

                def t1(n, k, half):
                    pe.wait_ge(s["x1_ready"], 3 * n + 3)
                    need(pe, s["x2t_ready"], (n - 2) * 2)
                    transpose_in(x1, "t1_done")

                def t2(n, k, half):
                    pe.wait_ge(s["x2_ready"], 3 * n + 3)
                    need(pe, s["x1t_ready"], upto((n + 3) * 2, 2 * NPAIR))
                    transpose_in(x2, "t2_done")

                def qproj(n, k, half):
                    need(pe, s["k_lo"], n - 2)
                    for m in range(KC):
                        for c in range(KC):
                            mm = pe.matmul(pP[:, m, 0:2 * T], wqk[:, c, m * P:(m + 1) * P],
                                           x1t[k][:, c, :, :].rearrange("p b t -> p (b t)"), start=(c == 0), stop=(c == KC - 1))
                    mm.then_inc(s["qt_done"], 1)

                def rows_by(lhs, rhs, done):
                    for b in range(2):
                        for c in range(KC):
                            pe.matmul(pV[:, 0, b * D:(b + 1) * D], lhs(b, c, 0, P), rhs(c), start=(c == 0), stop=(c == KC - 1))
                    for b in range(2):
                        w = GAP if b == 0 else TAIL
                        for c in range(KC):
                            mm = pe.matmul(pV[GAP * b:GAP * b + w, 1, 0:D], lhs(b, c, P, w), rhs(c), start=(c == 0), stop=(c == KC - 1))
                    mm.then_inc(s[done], 1)

                def vproj(n, k, half):
                    pe.wait_ge(s["x1t_ready"], (n + 1) * 2)
                    need(pe, s["h1_done"], (n - 1) * 3)
                    flat = x1t[k][:, :, :, :].rearrange("p c b t -> p c (b t)")
                    rows_by(lambda b, c, t, w: flat[:, c, b * T + t:b * T + t + w], lambda c: wv[:, c, :], "v_done")

                def scores(n, k, half):
                    pe.wait_ge(s["qt_ready"], n + 1)
                    need(pe, s["sm_done"], 3 * n)
                    flat = x1t[k][:, :, :, :].rearrange("p c b t -> p c (b t)")
                    for b in range(2):
                        for c in range(KC):
                            pe.matmul(pS[:, b * P:(b + 1) * P], qt[:, c, b * T:b * T + P], flat[:, c, b * T:b * T + P],
                                      start=(c == 0), stop=(c == KC - 1))
                    for b in range(2):
                        w = GAP if b == 0 else TAIL
                        for c in range(KC):
                            mm = pe.matmul(pS[GAP * b:GAP * b + w, 2 * P:2 * P + T], qt[:, c, b * T + P:b * T + P + w],
                                           flat[:, c, b * T:b * T + T], start=(c == 0), stop=(c == KC - 1))
                    mm.then_inc(s["s_done"], 1)

                def ptrans(n, k, half):
                    pe.wait_ge(s["p_ready"], 5 * n + 5)
                    need(pe, s["sim_evac"], n - 1)
                    for b in range(2):
                        pe.transpose(pR[:, b * P:(b + 1) * P], p0[:, b, :], ident)
                    pe.transpose(pR[:, 2 * P:2 * P + PT], p2[0:PT, 0:P], ident[0:PT, 0:PT])
                    pe.transpose(pR[0:PT, 2 * P + PT:2 * P + 2 * PT], p2[0:PT, P:P + PT], ident[0:PT, 0:PT]).then_inc(s["pt_done"], 1)

                def context(n, k, half):
                    pe.wait_ge(s["pts_ready"], (n + 1) * 2)
                    need(pe, s["v_ready"], upto((n + 2) * 2, 2 * NPAIR))
                    for b in range(2):
                        pe.matmul(pV[:, 0, b * D:(b + 1) * D], pts[:, b * P:(b + 1) * P], v0[k][:, b, :], start=True, stop=True)
                    for b in range(2):
                        w = GAP if b == 0 else TAIL
                        pe.matmul(pV[GAP * b:GAP * b + w, 1, 0:D], pts[:, 2 * P + GAP * b:2 * P + GAP * b + w], v0[k][:, b, :],
                                  start=True, stop=False, skip_group_check=True)
                    pe.matmul(pV[0:PT, 1, 0:D], ptt[0:PT, :], vt[k][0:PT, :], start=False, stop=True,
                              skip_group_check=True).then_inc(s["pv_done"], 1)

                def qk_columns(n, col, done):
                    for m in range(KC):
                        for c in range(KC):
                            mm = pe.matmul(pP[:, m, 0:2 * T], wqk2[:, c, col + m * P:col + (m + 1) * P],
                                           x2t[:, c, bass.ds(n * 2 * T, 2 * T)], start=(c == 0), stop=(c == KC - 1))
                    mm.then_inc(s[done], 1)

                def qcols(n, k, half):
                    pe.wait_ge(s["x2t_ready"], (n + 1) * 2)
                    need(pe, s["qt_ready"], upto(n + 3, NPAIR))
                    qk_columns(n, 0, "q_done")

                def kcols(n, k, half):
                    pe.wait_ge(s["q_lo"], n + 1)
                    qk_columns(n, D, "k_done")

                def simparts(n, k, half):
                    pe.wait_ge(s["q_hi"], 2 * n + 2)
                    need(pe, s["pts_ready"], upto((n + 2) * 2, 2 * NPAIR))
                    for c in range(KC):
                        pe.matmul(pR[32:64, 0:2 * T], con[:, C_OB + 32 * c:C_OB + 32 * c + 32], qsq[:, c, :],
                                  start=(c == 0), stop=(c == KC - 1), skip_group_check=True)
                        mm = pe.matmul(pR[0:32, 0:2 * T], wg[:, c, :], x2t[:, c, bass.ds(n * 2 * T, 2 * T)],
                                       start=(c == 0), stop=(c == KC - 1), skip_group_check=True)
                    mm.then_inc(s["sim_done"], 1)

                run_steps(pe, [(2, NPAIR, vproj), (4, NPAIR, t2), (2, NPAIR, qproj), (1, NPAIR, t1), (3, NPAIR, ptrans),
                               (4, NPAIR, qcols), (2, NPAIR, scores), (3, NPAIR, context), (4, NPAIR, kcols),
                               (4, NPAIR, simparts)], 0, *LOOP, NS, 2)

            @block.scalar
            def _(act):
                act.wait_ge(s["wqk_done"], 1)
                nc.scalar.activation(wqk[:, :, :].rearrange("p c d -> p (c d)"), pV[:, 0, :], ACT.Copy, scale=1.0 / 16.0).then_inc(s["wqk_ready"], 1)

                def exps(n, k, half):
                    act.wait_ge(s["nm_ready"], n + 1)
                    need(act, s["pt_done"], n)
                    for b in range(2):
                        nc.scalar.activation(p0[:, b, :], sm[:, b * P:(b + 1) * P], ACT.Exp, bias=nm[:, b:b + 1],
                                             accum_out=su[:, b:b + 1]).then_inc(s["p_ready"], 1)
                    nc.scalar.activation(p2[0:PT, 0:P], sm[0:PT, 2 * P:3 * P], ACT.Exp, bias=nm[0:PT, 2:3],
                                         accum_out=su[0:PT, 2:3]).then_inc(s["p_ready"], 1)
                    for b in range(2):
                        r = slice(GAP * b, GAP * b + (GAP if b == 0 else TAIL))
                        nc.scalar.activation(p2[r, P + GAP * b:P + GAP * b + TAIL], sm[r, 3 * P:2 * P + T], ACT.Exp, bias=nm[r, 2:3],
                                             accum_out=su[r, 3:4]).then_inc(s["p_ready"], 1)

                def qt_copy(n, k, half):
                    act.wait_ge(s["qt_done"], n + 1)
                    need(act, s["s_done"], n)
                    nc.scalar.activation(qt[:, :, :], pP[:, :, 0:2 * T], ACT.Copy).then_inc(s["qt_ready"], 1)

                def v_copy(n, k, half):
                    act.wait_ge(s["v_done"], n + 1)
                    nc.scalar.activation(v0[k][:, :, :].rearrange("p b d -> p (b d)"), pV[:, 0, :], ACT.Copy).then_inc(s["v_ready"], 1)
                    nc.scalar.activation(vt[k][0:PT, :], pV[0:PT, 1, 0:D], ACT.Copy).then_inc(s["v_ready"], 1)

                def x1t_copy(n, k, half):
                    act.wait_ge(s["t1_done"], n + 1)
                    need(act, s["s_done"], n - 1)
                    nc.scalar.activation(x1t[k][:, :, :, 0:P], pT[:, :, 0:2 * P].rearrange("p c (b t) -> p c b t", b=2),
                                         ACT.Copy).then_inc(s["x1t_ready"], 1)
                    nc.scalar.activation(x1t[k][:, :, :, P:T],
                                         pT[:, :, 2 * P:3 * P].rearrange("p c (b t) -> p c b t", b=2)[:, :, :, 0:TAIL],
                                         ACT.Copy).then_inc(s["x1t_ready"], 1)

                def q_high(n, k, half):
                    act.wait_ge(s["q_done"], n + 1)
                    need(act, st_q[k], half * 64)
                    need(act, s["sim_done"], n)
                    q4 = pP[:, :, 0:2 * T].rearrange("p c (b t) -> p c b t", b=2)
                    nc.scalar.activation(qsq[:, :, :], pP[:, :, 0:2 * T], ACT.Square).then_inc(s["q_hi"], 1)
                    nc.scalar.activation(qh[k][:, :, :, 0:T], q4, ACT.Copy, scale=0.25).then_inc(s["q_hi"], 1)

                def k_high(n, k, half):
                    act.wait_ge(s["k_done"], n + 1)
                    need(act, st_k[k], half * 64)
                    nc.scalar.activation(kh[k][:, :, :], pP[:, :, 0:2 * T], ACT.Copy).then_inc(s["k_hi"], 1)

                def sim_copy(n, k, half):
                    act.wait_ge(s["sim_done"], n + 1)
                    need(act, st_s[k], half * 32)
                    nc.scalar.activation(ss[k][:, :], pR[0:64, 0:2 * T], ACT.Copy).then_inc(s["sim_evac"], 1)

                run_steps(act, [(3, NPAIR, exps), (2, NPAIR, v_copy), (2, NPAIR, qt_copy), (1, NPAIR, x1t_copy), (4, NPAIR, q_high),
                                (4, NPAIR, k_high), (4, NPAIR, sim_copy)], 0, *LOOP, NS, 2)

            @block.vector
            def _(dve):
                dve.wait_ge(ld_w0, 48)
                dve.tensor_copy(ident16[:, :], ident).then_inc(s["id16_ready"], 1)
                for n in range(NE):
                    dve.wait_ge(s["e_done"], n + 1)
                    if n >= 3:
                        dve.wait_ge(st_he[n % 3], 16 * (n // 3))
                    dve.tensor_tensor(he[n % 3][:, :], pP[:, n % 2, 0:D], bt[:, :], ALU.add).then_inc(s["e_evac"], 1)
                dve.wait_ge(ld_w2, 96)
                dve.tensor_tensor(gsq[:, :], gcol[:, :], gcol[:, :], ALU.mult).then_inc(s["gsq_ready"], 1)
                dve.wait_ge(s["gss_done"], 1)
                dve.tensor_copy(gss[:, :], pR[:, 0:KC]).then_inc(s["gss_ready"], 1)
                dve.wait_ge(s["grn_ready"], 1)
                dve.tensor_tensor(gn[:, :], gcol[:, :], grn[:, :], ALU.mult).then_inc(s["gn_ready"], 1)
                dve.wait_ge(s["gn_ready"], 1)
                for c in range(KC):
                    dve.tensor_scalar(gblk[:, c, :], con[:, C_OB + 32 * c:C_OB + 32 * c + H], gn[:, c:c + 1], None,
                                      ALU.mult).then_inc(s["gblk_ready"], 1)
                dve.wait_ge(s["wg_done"], 1)
                dve.wait_ge(s["cleared"], 8)
                dve.tensor_copy(wg[:, :, 0:H], pS[:, 0:KC * H].rearrange("p (c h) -> p c h", c=KC)).then_inc(s["wg_ready"], 1)

                def rows(n, j):
                    return h0[:, bass.ds(n * 2 + j, 1), :].rearrange("p a d -> p (a d)") if j < 2 else \
                        ht[0:PT, bass.ds(n, 1), :].rearrange("p a d -> p (a d)")

                def width(j):
                    return PT if j == 2 else P

                def stats(n, st, mv, i):
                    dve.sem_inc(s["dve_turn"], 1)
                    for j in range(3):
                        dve.bn_stats(st[0:width(j), j, :], rows(n, j)).then_inc(s[f"st{i}_done"], 1)
                    dve.wait_ge(s[f"st{i}_done"], 3 * n + 3)
                    dve.sem_inc(s["dve_turn"], 1)
                    for j in range(3):
                        dve.bn_aggr(mv[0:width(j), j, :], st[0:width(j), j, :]).then_inc(s[f"mv{i}_done"], 1)

                def normalise(n, x, mv, rs, ready):
                    for j in range(3):
                        w = width(j)
                        dve.tensor_scalar(x[0:w, j, :], rows(n, j), mv[0:w, j, 0:1], rs[0:w, j:j + 1],
                                          ALU.subtract, ALU.mult).then_inc(s[ready], 1)

                def stats1(n, k, half):
                    dve.wait_ge(ld_h[k], half * 96 + 96)
                    stats(n, st1, mv1, 1)

                def norm1(n, k, half):
                    dve.wait_ge(s["rs1_done"], n + 1)
                    need(dve, s["t1_done"], n)
                    normalise(n, x1, mv1, rs1, "x1_ready")

                def masks(n, k, half):
                    dve.wait_ge(s["s_done"], n + 1)
                    need(dve, s["p_ready"], 5 * n)
                    dve.sem_inc(s["dve_turn"], 1)
                    for j, (c0, w, c) in enumerate(((0, P, C_M0), (P, P, C_M0), (2 * P, T, C_MT))):
                        r = width(j)
                        dve.tensor_tensor_reduce(sm[0:r, c0:c0 + w], pS[0:r, c0:c0 + w], con[0:r, c:c + w], 1.0, -3e38,
                                                 ALU.add, ALU.max, mx[0:r, j:j + 1]).then_inc(s["sm_done"], 1)
                    dve.wait_ge(s["sm_done"], 3 * n + 3)
                    dve.tensor_scalar(nm[:, :], mx[:, :], -1.0, None, ALU.mult).then_inc(s["nm_ready"], 1)

                def sums(n, k, half):
                    dve.wait_ge(s["p_ready"], 5 * n + 5)
                    dve.tensor_tensor(su[0:PT, 2:3], su[0:PT, 2:3], su[0:PT, 3:4], ALU.add).then_inc(s["sum_added"], 1)
                    dve.wait_ge(s["sum_added"], n + 1)
                    dve.reciprocal(rsum[:, :], su[:, 0:3]).then_inc(s["rsum_ready"], 1)

                def pts_copy(n, k, half):
                    dve.wait_ge(s["pt_done"], n + 1)
                    need(dve, s["pv_done"], n)
                    dve.tensor_copy(pts[:, :], pR[:, 0:2 * P + PT]).then_inc(s["pts_ready"], 1)
                    dve.tensor_copy(ptt[0:PT, :], pR[0:PT, 2 * P + PT:2 * P + 2 * PT]).then_inc(s["pts_ready"], 1)

                def h1_stats2(n, k, half):
                    dve.wait_ge(s["pv_done"], n + 1)
                    dve.wait_ge(s["rsum_ready"], n + 1)
                    for j in range(3):
                        r = width(j)
                        src = pV[:, 0, j * D:(j + 1) * D] if j < 2 else pV[0:PT, 1, 0:D]
                        dve.scalar_tensor_tensor(out=rows(n, j), in0=src, scalar=rsum[0:r, j:j + 1], in1=rows(n, j),
                                                 op0=ALU.mult, op1=ALU.add).then_inc(s["h1_done"], 1)
                    dve.wait_ge(s["h1_done"], 3 * n + 3)
                    stats(n, st2, mv2, 2)

                def norm2(n, k, half):
                    dve.wait_ge(s["rs2_done"], n + 1)
                    need(dve, s["t2_done"], n)
                    normalise(n, x2, mv2, rs2, "x2_ready")

                def x2t_copy(n, k, half):
                    dve.wait_ge(s["t2_done"], n + 1)
                    pair = x2t[:, :, bass.ds(n * 2 * T, 2 * T)].rearrange("p c (b t) -> p c b t", b=2)
                    dve.tensor_copy(pair[:, :, :, 0:P], pT[:, :, 0:2 * P].rearrange("p c (b t) -> p c b t", b=2)).then_inc(s["x2t_ready"], 1)
                    dve.tensor_copy(pair[:, :, :, P:T],
                                    pT[:, :, 2 * P:3 * P].rearrange("p c (b t) -> p c b t", b=2)[:, :, :, 0:TAIL]).then_inc(s["x2t_ready"], 1)

                def q_low(n, k, half):
                    dve.wait_ge(s["q_hi"], 2 * n + 2)
                    q4 = pP[:, :, 0:2 * T].rearrange("p c (b t) -> p c b t", b=2)
                    dve.scalar_tensor_tensor(out=ql[k][:, :, :, 0:T], in0=q4, scalar=0.25, in1=qh[k][:, :, :, 0:T],
                                             op0=ALU.mult, op1=ALU.subtract).then_inc(s["q_lo"], 1)

                def k_low(n, k, half):
                    dve.wait_ge(s["k_hi"], n + 1)
                    dve.tensor_tensor(kl[k][:, :, :], pP[:, :, 0:2 * T], kh[k][:, :, :], ALU.subtract).then_inc(s["k_lo"], 1)

                run_steps(dve, [(3, NPAIR, masks), (1, NPAIR, norm1), (4, NPAIR, x2t_copy), (3, NPAIR, sums), (3, NPAIR, pts_copy),
                                (4, NPAIR, q_low), (0, NPAIR, stats1), (3, NPAIR, h1_stats2), (4, NPAIR, k_low), (3, NPAIR, norm2)],
                          0, 6, 16, NS, 2)


def second_phase(nc, keep, scratch, consts16, out):
    con, ident16, ident, h0, ht, x2t, wv2, wp, bp = keep
    with ExitStack() as ctx:
        def sb(name, shape, dt=F32):
            return ctx.enter_context(nc.sbuf_tensor(name, shape, dt))

        def sem(name):
            return ctx.enter_context(nc.semaphore(name))

        def ps(name, shape):
            return ctx.enter_context(nc.psum_tensor(name, shape, F32))

        QW = H * TQ + 32
        qs = [sb(f"qs{j}", [P, QW], F16) for j in range(4)]
        ks = [sb(f"ks{j}", [P, H, KPAD], F16) for j in range(4)]
        mx = [sb(f"mx{j}", [P, 24]) for j in range(2)]
        mh = [sb(f"mh{j}", [P, 24], F16) for j in range(2)]
        mr = [sb(f"mr{j}", [16, P], F16) for j in range(2)]
        mrt = [sb(f"mrt{j}", [8, P], F16) for j in range(2)]
        em = sb("em", [P, H, TQ])
        et = sb("et", [P, H // 2, TQ])
        xc = [sb(f"xc{j}", [P, KC, 2 * T]) for j in range(2)]
        vm = [sb(f"vm{j}", [P, H, 32]) for j in range(4)]
        vt = [sb(f"vt2_{j}", [P, H, 32]) for j in range(4)]
        os_ = sb("os", [P, 4, TQ])
        rd = sb("rd", [P, 2, H])
        on = sb("on", [P, 2, D])
        OFW = KC * TQ + 24
        of = [sb(f"of{j}", [P, OFW]) for j in range(2)]
        hb = sb("hb", [P, 3, D])
        ot = [sb(f"ot{j}", [P, 3, D]) for j in range(2)]
        HQ = H * QUARTER
        flat = em[:, :, :].rearrange("p h t -> p (h t)")
        sq, num, nrm, rec = (flat[:, i * HQ:(i + 1) * HQ] for i in range(4))
        cos = et[:, :, :].rearrange("p h t -> p (h t)")[:, 0:HQ]
        sim, nsim, pos, ca, cn = (sb(m, [P, QUARTER]) for m in ("sim", "nsim", "pos", "ca", "cn"))
        junk = sb("junk", [P, 2, QUARTER])
        ext, rng, dd = (sb(m, [P, 2]) for m in ("ext", "rng", "dd"))
        g2, gd, ones2 = sb("g2", [2, 1]), sb("gd", [2, 2]), sb("ones2", [2, P])
        cls = sb("cls", [P, 4, QUARTER], F16)

        pA = [ps(f"pA{j}", [P, 512]) for j in range(2)]
        pB = [ps(f"pB{j}", [P, 512]) for j in range(2)]
        pO = ps("pO", [P, 2, 512])
        pX = ps("pX", [P, 2, 512])
        pM16 = pX[:, 1, :].bitcast(F16)
        p_ext, p_rng = pO[:, 0, :], pO[:, 1, :]

        names = ("set_up dve_set_up a_done a_max mh_ready mt_done mt_evac b_done e_ready pv_done os_ready c1_done rd_ready on_ready "
                 "c2_done of_copied of_ready v_done v_ready f_done hb_ready out_ready pe_turn").split()
        s = {n: sem(n) for n in names}
        ld_set = sem("ld_set")
        ld_sim, nrm_ready, class_step, ext_t, ext_b, st_class = (sem(m) for m in (
            "ld_sim", "nrm_ready", "class_step", "ext_transposed", "range_spread", "st_class"))
        ld_stack = [sem(f"ld_stack{j}") for j in range(4)]
        ld_shift = [sem(f"ld_shift{j}") for j in range(4)]
        ld_xc = [sem(f"ld_xc{j}") for j in range(2)]
        st_out = [sem(f"st_out{j}") for j in range(2)]

        def q_head(j, rows, h, c0, w):
            return qs[j][0:rows, h * TQ + c0:h * TQ + c0 + w]

        GROUPS = [g for a in range(4) for g in ((False, 2 * a), (False, 2 * a + 1), (True, a))]
        NG = len(GROUPS)
        SETUP = 2 * 5 + 4 * 2 + 2 + 4 * 2
        CLASS_STEPS = 19
        DVE_SETUP = 2 * 5
        LOOP = (8, 32)
        NSTEP = 36

        def tiles(group):
            tail, g = group
            if not tail:
                return [(2 * g + i, 0, i) for i in range(2)]
            return [(4 * g + 2 * i + j, GAP * j, i) for i in range(2) for j in range(2)]

        def pair_of(n, half, k):
            return half * 2 + k // 2

        def blank_stack(j):
            k32 = ks[j][:, :, :].rearrange("p h t -> p (h t)").bitcast(F32)
            return [(qs[j][64:P, :].bitcast(F32), 0.0), (qs[j][0:64, H * TQ:QW], 0.0), (ks[j][0:64, :, T:KPAD], 0.0),
                    (k32[64:96, :], 0.0), (k32[96:P, :], TWO_ONES)]

        with nc.Block() as block:

            @block.gpsimd
            def _(pool):
                blank = [x for j in (1, 3) for x in blank_stack(j)]
                for j in range(4):
                    blank += [(vm[j][:, :, 16:32], 1.0), (vt[j][:, :, :], 0.0)]
                blank += [(of[j][:, KC * TQ:OFW], 0.0) for j in range(2)]
                for j in range(4):
                    v4 = vt[j][:, :, :].rearrange("p (g e) c -> p g e c", e=2)
                    blank += [(v4[GAP * e:GAP * e + TAIL, :, e, 16:17], 1.0) for e in range(2)]
                for i, (t, value) in enumerate(blank):
                    pool.memset(t, value).then_inc(s["set_up"], 1)
                    pool.wait_ge(s["set_up"], i + 1)

                def biased(n, k, half):
                    if k % 2 == 0:
                        return
                    p = pair_of(n, half, k)
                    need(pool, s["out_ready"], 3 * p)
                    pool.tensor_tensor(hb[:, 0:2, :], h0[:, bass.ds(p * 2, 2), :], bp[:, :].rearrange("p (a d) -> p a d", a=1).broadcast_to([P, 2, D]),
                                       ALU.add).then_inc(s["hb_ready"], 1)
                    pool.wait_ge(s["hb_ready"], 2 * p + 1)
                    pool.tensor_tensor(hb[0:PT, 2, :], ht[0:PT, bass.ds(p, 1), :].rearrange("p a d -> p (a d)"), bp[0:PT, :],
                                       ALU.add).then_inc(s["hb_ready"], 1)

                run_steps(pool, [(3, B, biased)], 2, *LOOP, NSTEP, 4)

            @block.sync
            def _(sp):
                for i, dst in enumerate((sq, num)):
                    sp.dma_start(dst.rearrange("p (h t) -> p h t", h=H),
                                 scratch["sim"][i, :, :].rearrange("h (p t) -> p h t", t=QUARTER)).then_inc(ld_sim, 16)

                def load_features(n, k):
                    q3 = qs[k][:, 0:H * TQ].rearrange("p (h t) -> p h t", h=H)
                    for r in range(2):
                        sp.dma_start(q3[32 * r:32 * r + 32, :, :],
                                     scratch["q"][:, :, :, bass.ds(n, 1), :].rearrange("h k d b t -> (k d) h (b t)")).then_inc(ld_stack[k], 16)
                    sp.dma_start(ks[k][0:32, :, 0:T],
                                 scratch["k"][:, :, :, bass.ds(n, 1), :].rearrange("h k d b t -> (k d) h (b t)")).then_inc(ld_stack[k], 16)
                    for r, i in ((32, 1), (48, 0)):
                        sp.dma_start(ks[k][r:r + 16, :, 0:T],
                                     scratch["k"][:, i, :, bass.ds(n, 1), :].rearrange("h d b t -> d h (b t)")).then_inc(ld_stack[k], 16)

                def load_classes(n, k):
                    q3 = qs[k][:, 0:H * TQ].rearrange("p (h t) -> p h t", h=H)
                    for i, dst in enumerate((q3[64:66, :, 0:T], ks[k][64:66, :, 0:T])):
                        row = scratch["cls"][2 * i:2 * i + 2, bass.ds(n * T, T)].rearrange("r (a t) -> r a t", a=1)
                        sp.dma_start(dst, row.broadcast_to([2, H, T])).then_inc(ld_stack[k], 16)

                def load_stack(n, k, half):
                    need(sp, s["b_done"], NG * (n - 3))
                    load_features(n, k)
                    load_classes(n, k)

                def load_xc(n, k, half):
                    if k % 2 == 1:
                        return
                    p = pair_of(n, half, k)
                    need(sp, s["v_done"], 3 * (p - 1))
                    sp.dma_start(xc[k // 2][:, :, :], x2t[:, :, bass.ds(p * 2 * T, 2 * T)]).then_inc(ld_xc[k // 2], 16)

                def load_shift(n, k, half):
                    sp.wait_ge(s["mt_evac"], 2 * n + 2)
                    q3 = qs[k][:, 0:H * TQ].rearrange("p (h t) -> p h t", h=H)
                    q4 = qs[k][:, 0:H * TQ].rearrange("p (g e t) -> p g e t", e=2, t=TQ)
                    sp.dma_start(q3[SHIFT_ROW:P, :, 0:P], mr[k % 2][:, :]).then_inc(ld_shift[k], 16)
                    for e in range(2):
                        sp.dma_start(q4[SHIFT_ROW:P, :, e, P:TQ], mrt[k % 2][:, GAP * e:GAP * e + QTAIL]).then_inc(ld_shift[k], 16)

                def store_out(n, k, half):
                    if k % 2 == 0:
                        return
                    p = pair_of(n, half, k)
                    pp = k // 2
                    sp.wait_ge(s["out_ready"], 3 * p + 3)
                    sp.dma_start(out[bass.ds(p * 2, 2), 0:P, :].rearrange("b t d -> t b d"), ot[pp][:, 0:2, :]).then_inc(st_out[pp], 16)
                    for b in range(2):
                        sp.dma_start(out[bass.ds(p * 2 + b, 1), P:T, :].rearrange("b t d -> t (b d)"),
                                     ot[pp][GAP * b:GAP * b + TAIL, 2, :]).then_inc(st_out[pp], 16)

                for n in range(3):
                    load_features(n, n)
                load_xc(0, 0, 0)
                sp.wait_ge(s["set_up"], SETUP)
                sp.wait_ge(s["dve_set_up"], DVE_SETUP)
                for j in range(4):
                    q3 = qs[j][:, 0:H * TQ].rearrange("p (h t) -> p h t", h=H)
                    sp.dma_start(q3[65:66, :, T:TQ], consts16[0:1, 0:H * REG].rearrange("o (h t) -> o h t", h=H)).then_inc(ld_set, 16)
                sp.wait_ge(class_step, CLASS_STEPS)
                sp.dma_start(scratch["cls"].rearrange("r (p t) -> p r t", t=QUARTER), cls[:, :, :]).then_inc(st_class, 16)
                sp.wait_ge(st_class, 16)
                for n in range(3):
                    load_classes(n, n)
                start = lambda first, emit: lambda n, k, half: None if isinstance(n, int) and n < first else emit(n, k, half)
                run_steps(sp, [(-1, B, start(3, load_stack)), (0, B, start(2, load_xc)), (1, B, load_shift), (3, B, store_out)],
                          0, 4, 28, NSTEP, 4)
                for j in range(2):
                    sp.wait_ge(st_out[j], 48 * NPAIR // 2)

            @block.tensor
            def _(pe):
                pe.wait_ge(class_step, 8)
                pe.transpose(p_ext[0:2, 0:P], ext[:, :], ident).then_inc(ext_t, 1)
                pe.wait_ge(class_step, 10)
                pe.matmul(p_rng[:, 0:2], ones2[:, :], gd[:, :], start=True, stop=True).then_inc(ext_b, 1)
                pe.wait_ge(ld_set, 64)
                pe.wait_ge(s["set_up"], SETUP)
                pe.wait_ge(s["dve_set_up"], DVE_SETUP)

                def logits(pD, group, n, k, rows, shifted):
                    for h, at, slot in tiles(group):
                        if shifted:
                            lhs = ks[k][:, h, P:KPAD] if group[0] else ks[k][:, h, 0:P]
                            rhs = q_head(k, P, h, 0, TQ)
                        else:
                            lhs = q_head(k, rows, h, P, GAP) if group[0] else q_head(k, rows, h, 0, P)
                            rhs = ks[k][0:rows, h, 0:T]
                        w = TQ if shifted else T
                        m = GAP if group[0] else P
                        mm = pe.matmul(pD[at:at + m, slot * w:(slot + 1) * w], lhs, rhs, start=True, stop=True)
                    return mm

                def a_group(i):
                    def emit(n, k, half):
                        if i == 0:
                            pe.wait_ge(ld_stack[k], half * 112 + 112)
                        need(pe, s["a_max"], NG * n + i - 1)
                        logits(pA[i % 2], GROUPS[i], n, k, SHIFT_ROW, False).then_inc(s["a_done"], 1)
                    return emit

                def b_group(i):
                    def emit(n, k, half):
                        if i == 0:
                            pe.wait_ge(ld_shift[k], half * 48 + 48)
                        need(pe, s["e_ready"], NG * n + i - 1)
                        logits(pB[i % 2], GROUPS[i], n, k, P, True).then_inc(s["b_done"], 1)
                    return emit

                def pv_group(a):
                    def emit(n, k, half):
                        if a == 0:
                            pe.wait_ge(s["v_ready"], 6 * pair_of(n, half, k) + 6)
                        if a % 2 == 0:
                            need(pe, s["os_ready"], 2 * n - 1 + a // 2)
                        pe.wait_ge(s["e_ready"], NG * n + 3 * a + 3)
                        for q in range(4):
                            h = 4 * a + q
                            dst = pO[32 * q:32 * q + 32, a // 2, (a % 2) * TQ:(a % 2 + 1) * TQ]
                            pe.matmul(dst, vm[k][:, h, :], em[:, h, :], start=True, stop=False, skip_group_check=True)
                        for q in range(4):
                            h = 4 * a + q
                            dst = pO[32 * q:32 * q + 32, a // 2, (a % 2) * TQ:(a % 2 + 1) * TQ]
                            mm = pe.matmul(dst, vt[k][:, h, :], et[:, h // 2, :], start=False, stop=True, skip_group_check=True)
                        mm.then_inc(s["pv_done"], 1)
                    return emit

                def max_rows(n, k, half):
                    pe.wait_ge(s["mh_ready"], n + 1)
                    if k % 2 == 0:
                        need(pe, s["out_ready"], 3 * (pair_of(n, half, k) - 2) + 1)
                    else:
                        pe.wait_ge(s["v_ready"], 6 * pair_of(n, half, k) + 4)
                    pe.transpose(pM16[0:16, 0:P], mh[k % 2][:, 0:16], ident16[:, :])
                    pe.transpose(pM16[0:8, P:2 * P], mh[k % 2][:, 16:24], ident16[:, :]).then_inc(s["mt_done"], 1)

                def c1_first(n, k, half):
                    pe.wait_ge(s["os_ready"], 2 * n + 2)
                    if k % 2 == 0:
                        need(pe, s["out_ready"], 3 * pair_of(n, half, k))
                    else:
                        pe.wait_ge(s["v_ready"], upto(6 * (pair_of(n, half, k) + 2), 6 * NPAIR))
                    need(pe, s["of_copied"], n)
                    for a in range(4):
                        mm = pe.transpose(pX[:, 0, a * P:(a + 1) * P], os_[:, a, 0:P], ident)
                    mm.then_inc(s["c1_done"], 1)

                def c1_tail(n, k, half):
                    pe.wait_ge(s["mt_evac"], upto(2 * n + 6, 2 * B))
                    pe.sem_inc(s["pe_turn"], 1)
                    for a in range(4):
                        mm = pe.transpose(pX[0:QTAIL, 1, a * P:(a + 1) * P], os_[:, a, P:TQ], ident)
                    mm.then_inc(s["c1_done"], 1)

                def c2(n, k, half):
                    pe.wait_ge(s["on_ready"], 2 * n + 2)
                    for c in range(KC):
                        pe.transpose(pX[:, 0, c * TQ:c * TQ + P], on[:, 0, c * P:(c + 1) * P], ident)
                        mm = pe.transpose(pX[:, 0, c * TQ + P:(c + 1) * TQ], on[0:QTAIL, 1, c * P:(c + 1) * P], ident[0:QTAIL, 0:QTAIL])
                    mm.then_inc(s["c2_done"], 1)

                def rows_of(part, lhs, w_, done):
                    for b in range(2) if part == 0 else (part - 1,):
                        w, t, at = (GAP if b == 0 else TAIL, P, GAP * b) if part == 0 else (P, 0, 0)
                        dst = pX[at:at + w, 1, 0:D] if part == 0 else pX[:, 0, b * D:(b + 1) * D]
                        for c in range(KC):
                            mm = pe.matmul(dst, lhs(b, c, t, w), w_[:, c, :], start=(c == 0), stop=(c == KC - 1))
                    mm.then_inc(s[done], 1)

                def vproj(part):
                    def emit(n, k, half):
                        if k % 2 == 1:
                            return
                        pp = k // 2
                        if part == 0:
                            pe.wait_ge(ld_xc[pp], half * 16 + 16)
                            pe.wait_ge(s["mt_evac"], 2 * n + 2)
                        if part == 1:
                            need(pe, s["of_copied"], n - 1)
                        rows_of(part, lambda b, c, t, w: xc[pp][:, c, b * T + t:b * T + t + w], wv2, "v_done")
                    return emit

                def project(part):
                    def emit(n, k, half):
                        if k % 2 == 0:
                            return
                        if part == 0:
                            pe.wait_ge(s["of_ready"], n + 1)
                        rows_of(part, lambda b, c, t, w: of[b][:, c * TQ + t:c * TQ + t + w], wp, "f_done")
                    return emit

                between = {0: [(3, B, pv_group(3))], 1: [(1, B, max_rows)], 2: [(3, B, c1_first)], 3: [(3, B, c1_tail)],
                           4: [(2, B, pv_group(0))], 6: [(2, B, pv_group(1))], 7: [(3, B, c2)],
                           9: [(1, B, vproj(0)), (3, B, project(0)), (2, B, pv_group(2))], 10: [(1, B, vproj(1)), (3, B, project(1))],
                           11: [(1, B, vproj(2)), (3, B, project(2))]}
                run_steps(pe, [stage for i in range(NG) for stage in [(2, B, b_group(i)), (0, B, a_group(i))] + between.get(i, [])],
                          0, *LOOP, NSTEP, 4)

            @block.scalar
            def _(act):
                act.wait_ge(ld_sim, 32)
                nc.scalar.activation(nrm, sq, ACT.Sqrt).then_inc(nrm_ready, 1)
                act.wait_ge(s["set_up"], SETUP)
                act.wait_ge(class_step, CLASS_STEPS)

                def mt_copy(n, k, half):
                    act.wait_ge(s["mt_done"], n + 1)
                    if not isinstance(n, int) or n >= 2:
                        act.wait_ge(ld_shift[(k - 2) % 4], 48 * (half + 1 if k >= 2 else half))
                    nc.scalar.activation(mr[k % 2][:, :], pM16[0:16, 0:P], ACT.Copy).then_inc(s["mt_evac"], 1)
                    nc.scalar.activation(mrt[k % 2][:, :], pM16[0:8, P:2 * P], ACT.Copy).then_inc(s["mt_evac"], 1)

                def os_copy(i):
                    def emit(n, k, half):
                        act.wait_ge(s["pv_done"], 4 * n + 2 * i + 2)
                        need(act, s["c1_done"], 2 * n)
                        nc.scalar.activation(os_[:, 2 * i:2 * i + 2, :].rearrange("p a t -> p (a t)"), pO[:, i, 0:2 * TQ],
                                             ACT.Copy).then_inc(s["os_ready"], 1)
                    return emit

                def of_copy(n, k, half):
                    act.wait_ge(s["c2_done"], n + 1)
                    nc.scalar.activation(of[k % 2][:, 0:KC * TQ], pX[:, 0, 0:KC * TQ], ACT.Copy).then_inc(s["of_copied"], 1)

                def v_tails(n, k, half):
                    if k % 2 == 1:
                        return
                    act.wait_ge(s["v_done"], 3 * pair_of(n, half, k) + 1)
                    need(act, s["pv_done"], 4 * (n - 2))
                    for b in range(2):
                        src = pX[GAP * b:GAP * b + TAIL, 1, 0:D].rearrange("p (g e d) -> p g e d", e=2, d=DH)
                        dst = vt[k + b][:, :, 0:16].rearrange("p (g e) d -> p g e d", e=2)
                        for e in range(2):
                            nc.scalar.activation(dst[GAP * e:GAP * e + TAIL, :, e, :], src[:, :, e, :], ACT.Copy).then_inc(s["v_ready"], 1)

                def v_first(n, k, half):
                    if k % 2 == 1:
                        return
                    act.wait_ge(s["v_done"], 3 * pair_of(n, half, k) + 3)
                    for b in range(2):
                        nc.scalar.activation(vm[k + b][:, :, 0:16], pX[:, 0, b * D:(b + 1) * D].rearrange("p (h d) -> p h d", h=H),
                                             ACT.Copy).then_inc(s["v_ready"], 1)

                def e_group(i):
                    tail, g = GROUPS[i]

                    def emit(n, k, half):
                        act.wait_ge(s["b_done"], NG * n + i + 1)
                        need(act, s["pv_done"], 4 * (n - 1) + i // 3 + 1)
                        dst = (et if tail else em)[:, 2 * g:2 * g + 2, :].rearrange("p a t -> p (a t)")
                        nc.scalar.activation(dst, pB[i % 2][:, 0:2 * TQ], ACT.Exp).then_inc(s["e_ready"], 1)
                    return emit

                between = {0: [(3, B, os_copy(1))], 1: [(1, B, mt_copy)], 7: [(3, B, of_copy), (2, B, os_copy(0))], 9: [(1, B, v_tails)],
                           11: [(1, B, v_first)]}
                run_steps(act, [stage for i in range(NG) for stage in [(2, B, e_group(i))] + between.get(i, [])], 0, *LOOP, NSTEP, 4)

            @block.vector
            def _(dve):
                for j in (0, 2):
                    for t, value in blank_stack(j):
                        dve.memset(t, value).then_inc(s["dve_set_up"], 1)

                chain = [0]

                def step(ins):
                    ins.then_inc(class_step, 1)
                    chain[0] += 1
                    dve.wait_ge(class_step, chain[0])

                step(dve.memset(ones2[:, :], 1.0))
                dve.wait_ge(nrm_ready, 1)
                step(dve.reciprocal(rec, nrm))
                step(dve.scalar_tensor_tensor(out=cos, in0=num, scalar=1.0 / H, in1=rec, op0=ALU.mult, op1=ALU.mult))
                step(dve.tensor_reduce(sim[:, :], cos.rearrange("p (h t) -> p t h", h=H), AX_X, ALU.add))
                step(dve.tensor_scalar(nsim[:, :], sim[:, :], -1.0, None, ALU.mult))
                big = con[:, C_REGBIG:C_REGBIG + QUARTER]
                step(dve.tensor_tensor_reduce(junk[:, 0, :], nsim[:, :], big, 1.0, -3e38, ALU.subtract, ALU.max, ext[:, 0:1]))
                step(dve.tensor_tensor_reduce(junk[:, 1, :], sim[:, :], big, 1.0, -3e38, ALU.subtract, ALU.max, ext[:, 1:2]))
                step(dve.memset(cls[:, :, :], 0.0))
                dve.wait_ge(ext_t, 1)
                step(dve.tensor_reduce(g2[:, :], p_ext[0:2, 0:P], AX_X, ALU.max))
                step(dve.tensor_scalar(gd[:, :], ident[0:2, 0:2], g2[:, 0:1], None, ALU.mult))
                dve.wait_ge(ext_b, 1)
                step(dve.tensor_copy(rng[:, :], p_rng[:, 0:2]))
                step(dve.tensor_tensor(dd[:, 0:1], rng[:, 0:1], rng[:, 1:2], ALU.add))
                step(dve.tensor_scalar(dd[:, 1:2], dd[:, 0:1], 0.9, None, ALU.mult))
                step(dve.tensor_scalar(pos[:, :], sim[:, :], rng[:, 0:1], dd[:, 1:2], ALU.add, ALU.is_gt))
                nreg = con[:, C_NREG:C_NREG + QUARTER]
                reg = con[:, C_REG:C_REG + QUARTER]
                step(dve.tensor_tensor(ca[:, :], pos[:, :], nreg, ALU.mult))
                step(dve.scalar_tensor_tensor(out=cn[:, :], in0=ca[:, :], scalar=-1.0, in1=nreg, op0=ALU.mult, op1=ALU.add))
                step(dve.tensor_scalar(cls[:, 3, :], ca[:, :], -CLASS, None, ALU.mult))
                step(dve.tensor_tensor(ca[:, :], ca[:, :], reg, ALU.add))
                dve.tensor_scalar(cls[:, 0, :], ca[:, :], CLASS, None, ALU.mult)
                dve.tensor_scalar(cls[:, 1, :], cn[:, :], CLASS, None, ALU.mult)
                dve.tensor_scalar(cls[:, 2, :], cn[:, :], -CLASS, None, ALU.mult).then_inc(class_step, 1)

                def a_max(i):
                    tail, g = GROUPS[i]

                    def emit(n, k, half):
                        dve.wait_ge(s["a_done"], NG * n + i + 1)
                        c0 = 16 + 2 * g if tail else 2 * g
                        dve.tensor_reduce(mx[k % 2][:, c0:c0 + 2], pA[i % 2][:, 0:2 * T].rearrange("p (a t) -> p a t", t=T),
                                          AX_X, ALU.max).then_inc(s["a_max"], 1)
                    return emit

                def negate(n, k, half):
                    dve.wait_ge(s["a_max"], NG * n + NG)
                    need(dve, s["mt_done"], n - 1)
                    dve.tensor_scalar(mh[k % 2][:, :], mx[k % 2][:, :], -1.0, -CLASS, ALU.mult, ALU.max).then_inc(s["mh_ready"], 1)

                def denominators(i):
                    def emit(n, k, half):
                        r = QTAIL if i else P
                        dve.wait_ge(s["c1_done"], 2 * n + 1 + i)
                        t4 = pX[0:r, i, :].rearrange("p (h e) -> p h e", e=32)
                        dve.reciprocal(rd[0:r, i, :].rearrange("p (h a) -> p h a", a=1), t4[:, :, 16:17]).then_inc(s["rd_ready"], 1)
                    return emit

                def norm(i):
                    def emit(n, k, half):
                        r = QTAIL if i else P
                        dve.wait_ge(s["rd_ready"], 2 * n + 1 + i)
                        need(dve, s["c2_done"], n)
                        t4 = pX[0:r, i, :].rearrange("p (h e) -> p h e", e=32)
                        dve.scalar_tensor_tensor(out=on[0:r, i, :].rearrange("p (h d) -> p h d", h=H), in0=t4[:, :, 0:16],
                                                 scalar=con[0:r, C_HALF + i:C_HALF + i + 1],
                                                 in1=rd[0:r, i, :].rearrange("p (h a) -> p h a", a=1).broadcast_to([r, H, DH]),
                                                 op0=ALU.mult, op1=ALU.mult).then_inc(s["on_ready"], 1)
                    return emit

                def registers(n, k, half):
                    dve.wait_ge(s["of_copied"], n + 1)
                    o3 = of[k % 2][:, 0:KC * TQ].rearrange("p (c t) -> p c t", c=KC)
                    dve.tensor_tensor(o3[:, :, 0:REG], o3[:, :, 0:REG], o3[:, :, T:TQ], ALU.add).then_inc(s["of_ready"], 1)

                def residual(tails):
                    def emit(n, k, half):
                        if k % 2 == 0:
                            return
                        p, pp = pair_of(n, half, k), k // 2
                        dve.wait_ge(s["f_done"], 3 * p + (1 if tails else 3))
                        dve.wait_ge(s["hb_ready"], 2 * p + 2)
                        need(dve, st_out[pp], 48 * half)
                        if tails:
                            dve.tensor_tensor(ot[pp][0:PT, 2, :], pX[0:PT, 1, 0:D], hb[0:PT, 2, :], ALU.add).then_inc(s["out_ready"], 1)
                        else:
                            for j in range(2):
                                dve.tensor_tensor(ot[pp][:, j, :], pX[:, 0, j * D:(j + 1) * D], hb[:, j, :], ALU.add).then_inc(s["out_ready"], 1)
                    return emit

                between = {3: [(3, B, denominators(0))], 4: [(3, B, norm(0)), (3, B, denominators(1))], 5: [(3, B, norm(1))],
                           7: [(3, B, registers)], 10: [(3, B, residual(True))], 11: [(0, B, negate), (3, B, residual(False))]}
                run_steps(dve, [stage for i in range(NG) for stage in [(0, B, a_max(i))] + between.get(i, [])], 0, *LOOP, NSTEP, 4)


def _constants(np):
    c = np.zeros((P, C_END), np.float32)
    r = np.arange(P)
    c[:, C_ID:C_ID + P] = np.eye(P)
    c[:, C_M0:C_M0 + P] = np.where(r[None, :] <= r[:, None], 0.0, MASKED)
    query = np.where(r < TAIL, P + r, np.where(r >= GAP, P + r - GAP, T))
    c[:, C_MT:C_MT + T] = np.where(np.arange(T)[None, :] <= query[:, None], 0.0, MASKED)
    c[:, C_BB:C_BB + P] = r[:, None] // DH == r[None, :] // DH
    for k in range(KC):
        c[:, C_OB + 32 * k:C_OB + 32 * k + H] = (k * P + r[:, None]) // DH == np.arange(H)[None, :]
    reg = (r[:, None] % 4 == 0) & (np.arange(QUARTER)[None, :] < REG)
    c[:, C_REGBIG:C_REGBIG + QUARTER] = np.where(reg, -MASKED, 0.0)
    c[:, C_NREG:C_NREG + QUARTER] = ~reg
    c[:, C_REG:C_REG + QUARTER] = reg
    c[:, C_HALF] = np.where(r < REG, 0.5, 1.0)
    c[:, C_HALF + 1] = np.where((r >= TAIL) & (r < QTAIL), 0.5, 1.0)
    c16 = np.zeros((2, H * T), np.float16)
    c16[0, 0:H * REG] = CLASS
    c16[1, :] = 1.0
    return c, c16


def kernel(**inputs):
    import numpy as np
    import concourse.bacc as bacc
    from concourse.bass_utils import run_bass_kernel_spmd

    a = {n: np.asarray(v) for n, v in inputs.items()}

    def chunks(w):
        return np.ascontiguousarray(w.reshape(-1, P, w.shape[1]).transpose(1, 0, 2))

    side = 16
    n = a["x"].shape[1] // side
    patches = a["x"].reshape(B, n, side, n, side, 3).transpose(2, 4, 5, 0, 1, 3).reshape(KE, P, NE, P)
    c, c16 = _constants(np)
    arrays = {
        "xt": np.ascontiguousarray(patches.transpose(1, 2, 0, 3)),
        "txt": np.ascontiguousarray(a["txt"]),
        "w_tok": chunks(a["L0_tok_W"].T),
        "b_tok": a["L0_tok_b"].reshape(1, D),
        "a_wqt": chunks(a["L0_attn_W_Q"].T),
        "a_wkt": chunks(a["L0_attn_W_K"].T),
        "a_wv": chunks(a["L0_attn_W_V"]),
        "f_wqkv": chunks(a["L0_ffn_W_qkv"]),
        "f_wqt": chunks(a["L0_ffn_W_qkv"][:, 0:D].T),
        "f_g": np.ascontiguousarray(a["L0_ffn_g_info"][0, 0].reshape(KC, P).T),
        "f_wp": chunks(a["L0_ffn_W_proj"]),
        "f_bp": a["L0_ffn_b_proj"].reshape(1, D),
        "consts": c,
        "consts16": c16,
    }
    nc = bacc.Bacc("TRN2", target_bir_lowering=False, num_devices=1)
    args = [nc.dram_tensor(m, v.shape, mybir.dt.from_np(v.dtype), kind="ExternalInput").ap() for m, v in arrays.items()]
    out = nc.dram_tensor("out", (B, T, D), F32, kind="ExternalOutput").ap()
    fusion_program(nc, *args, out)
    r = run_bass_kernel_spmd(nc, [arrays], core_ids=[0])
    return r.results[0]["out"]
```

```python
from contextlib import ExitStack

import concourse.bass as bass
from concourse import mybir

F32 = mybir.dt.float32
F16 = mybir.dt.float16
ALU = mybir.AluOpType
ACT = mybir.ActivationFunctionType
AX_X = mybir.AxisListType.X

B, D = 32, 256
NTOK, NTXT = 36, 128
T = NTOK + NTXT
PATCH = 768
H, DH, REG = 16, 16, 5
P = 128
TAIL = T - P
GAP = 64
PT = GAP + TAIL
NPAIR = B // 2
TQ = T + REG
QTAIL = TQ - P
KC = D // P
NE = B * NTOK // P
KE = PATCH // P
EPS = 1e-5
MASKED = -1e30
QUARTER = T // 4
UP = 16.0
VFIRST = 4
HALVES = ((0, 0), (0, 1), (1, 0))
CLASS = 60000.0
KPAD = 192
TWO_ONES = (1 + 15 * 2.0 ** -13) * 2.0 ** -7
SHIFT_ROW = 127

C_ID, C_M0, C_MT, C_BB, C_OB = 0, 128, 256, 420, 548
C_REGBIG, C_NREG, C_REG, C_HALF = 612, 653, 694, 735
C_END = 737


def need(eng, sem, count):
    if not isinstance(count, int) or count > 0:
        eng.wait_ge(sem, count)


def upto(count, most):
    return min(count, most) if isinstance(count, int) else count


def run_steps(eng, stages, first, loop_from, loop_to, last, unroll):
    def one(step, t, u):
        for lag, total, emit in stages:
            if t is not None and (lag + total <= loop_from or lag >= loop_to):
                continue
            if t is None:
                n = step - lag
                if 0 <= n < total:
                    emit(n, n % unroll, n // unroll)
            else:
                emit(t * unroll + (u - lag), (u - lag) % unroll, t + (u - lag) // unroll)

    for step in range(first, loop_from):
        one(step, None, 0)
    with eng.Fori(loop_from // unroll, loop_to // unroll) as t:
        for u in range(unroll):
            one(None, t, u)
    for step in range(loop_to, last):
        one(step, None, 0)


def fusion_program(nc, xt, txt, w_tok, b_tok, a_wqt, a_wkt, a_wv, f_wqkv, f_wqt, f_g, f_wp, f_bp, consts, consts16, out):
    scratch = {
        "h_tok": nc.dram_tensor("h_tok", (B * NTOK, D), F32).ap(),
        "q": nc.dram_tensor("q_split", (H, DH, 2, B, TQ), F16).ap(),
        "k": nc.dram_tensor("k_split", (H, DH, 2, B, T), F16).ap(),
        "x2": nc.dram_tensor("x2_split", (P, 2 * KC, B * T), F16).ap(),
        "sim": nc.dram_tensor("sim_parts", (2, H, B * T), F32).ap(),
        "cls": nc.dram_tensor("class_rows", (4, B * T), F16).ap(),
    }
    with ExitStack() as whole:
        def sb(name, shape, dt=F32, ctx=whole):
            return ctx.enter_context(nc.sbuf_tensor(name, shape, dt))

        con = sb("con", [P, C_END])
        ident16 = sb("ident16", [P, P], F16)
        h0 = sb("h0", [P, B, D])
        ht = sb("ht", [P, NPAIR, D])
        wv2 = sb("wv2", [P, 2, KC, D], F16)
        wp = sb("wp", [P, KC, D])
        bp = sb("bp", [P, D])
        va = sb("va", [P, B, D])
        vta = sb("vta", [P, NPAIR, D])
        ident = con[:, C_ID:C_ID + P]
        keep = (con, ident16, ident, h0, ht, wv2, wp, bp, va, vta)
        first_phase(nc, keep, scratch, xt, txt, w_tok, b_tok, a_wqt, a_wkt, a_wv, f_wqkv, f_wqt, f_g, f_wp, f_bp, consts)
        second_phase(nc, keep, scratch, consts16, out)


def first_phase(nc, keep, scratch, xt, txt, w_tok, b_tok, a_wqt, a_wkt, a_wv, f_wqkv, f_wqt, f_g, f_wp, f_bp, consts):
    con, ident16, ident, h0, ht, wv2, wp, bp, va, vta = keep
    with ExitStack() as ctx:
        def sb(name, shape, dt=F32):
            return ctx.enter_context(nc.sbuf_tensor(name, shape, dt))

        def sem(name):
            return ctx.enter_context(nc.semaphore(name))

        wt = sb("wt", [P, KE, D])
        bt = sb("bt", [P, D])
        wqt, wkt, wv = (sb(n, [P, KC, D]) for n in ("wqt", "wkt", "wv"))
        wqkv2 = sb("wqkv2", [P, KC, 3 * D])
        wqks = sb("wqks", [P, 2, KC, D], F16)
        wvs = sb("wvs", [P, 2, KC, D], F16)
        wqk2 = sb("wqk2", [P, 2, KC, 2 * D], F16)
        wqt2 = sb("wqt2", [P, KC, D])
        gcol = sb("gcol", [P, KC])
        gsq = sb("gsq", [P, KC])
        gss = sb("gss", [P, KC])
        grn = sb("grn", [P, KC])
        gn = sb("gn", [P, KC])
        gblk = sb("gblk", [P, KC, H])
        wg = sb("wg", [P, 2, KC, 32], F16)
        mhalf = sb("mhalf", [P, 3])
        xi = [sb(f"xi{j}", [P, KE, P]) for j in range(3)]
        he = [sb(f"he{j}", [P, D]) for j in range(3)]
        st1, st2 = sb("st1", [P, 3, 6]), sb("st2", [P, 3, 6])
        mv1, mv2 = sb("mv1", [P, 3, 2]), sb("mv2", [P, 3, 2])
        ve1, ve2 = sb("ve1", [P, 3]), sb("ve2", [P, 3])
        rs1, rs2 = sb("rs1", [P, 3]), sb("rs2", [P, 3])
        x1, x2 = sb("x1", [P, 3, D]), sb("x2", [P, 3, D])
        x1t = [sb(f"x1t{j}", [P, 2, KC, 2 * T], F16) for j in range(2)]
        x2t = [sb(f"x2t{j}", [P, 2, KC, 2 * T], F16) for j in range(2)]
        qt = sb("qt", [P, 2, KC, 2 * T], F16)
        v0 = [sb(f"v0_{j}", [P, 2, D]) for j in range(2)]
        vt = [sb(f"vt_{j}", [P, D]) for j in range(2)]
        sm = sb("sm", [P, 2 * P + T])
        mx, nm, su, rsum = sb("mx", [P, 3]), sb("nm", [P, 3]), sb("su", [P, 4]), sb("rsum", [P, 3])
        p0 = sb("p0", [P, 2, P])
        p2 = sb("p2", [P, P + PT])
        pts = sb("pts", [P, 2 * P + PT])
        ptt = sb("ptt", [P, PT])
        qhl = [sb(f"qhl{j}", [P, 2, KC, 2, TQ], F16) for j in range(2)]
        khl = [sb(f"khl{j}", [P, 2, KC, 2 * T], F16) for j in range(2)]
        qsq = sb("qsq", [P, KC, 2 * T])
        xc = [sb(f"xc{j}", [P, 2 * KC, 2 * T], F16) for j in range(VFIRST)]
        ss = [sb(f"ss{j}", [P, T]) for j in range(2)]

        def ps(name, shape):
            return ctx.enter_context(nc.psum_tensor(name, shape, F32))

        pT = ps("pT", [P, 2, 512])
        pP = ps("pP", [P, 2, 512])
        pV = ps("pV", [P, 2, 512])
        pS = ps("pS", [P, 512])
        pR = ps("pR", [P, 512])

        ld_wt, ld_w0, ld_w1, ld_w2, ld_w3 = (sem(m) for m in ("ld_wt", "ld_w0", "ld_w1", "ld_w2", "ld_w3"))
        ld_xi = [sem(f"ld_xi{j}") for j in range(3)]
        ld_h = [sem(f"ld_h{j}") for j in range(2)]
        names = ("cleared e_done e_evac wqk_done wqk_hi wqk_lo wv_hi wv_lo w2_hi w2_lo wg_hi gsq_ready gss_done gss_ready grn_ready gn_ready gblk_ready "
                 "wg_done wg_ready id16_ready st1_done mv1_done ve1_done rs1_done x1_ready t1_done x1t_hi x1t_lo qt_done qt_hi qt_lo "
                 "v_done v_ready s_done sm_done nm_ready p_ready sum_added rsum_ready pt_done pts_ready pv_done h1_done "
                 "st2_done mv2_done ve2_done rs2_done x2_ready t2_done x2t_hi x2t_lo q_done q_hi q_lo q_dup k_done k_hi k_lo "
                 "sim_done sim_evac dve_turn pool_turn sp_turn").split()
        s = {n: sem(n) for n in names}
        st_he = [sem(f"st_he{j}") for j in range(3)]
        st_q = [sem(f"st_q{j}") for j in range(2)]
        st_k = [sem(f"st_k{j}") for j in range(2)]
        ld_xc, first_v, first_va = sem("ld_xc"), sem("first_v"), sem("first_va")
        st_x = [sem(f"st_x{j}") for j in range(2)]
        st_s = [sem(f"st_s{j}") for j in range(2)]

        EARLY = 3
        LASTV = NPAIR + 3
        NS = 20
        LOOP = (6, 16)

        VBANKS = ((pV[:, 0, :], pV[:, 1, :]), (pT[:, 0, :], pT[:, 1, :]))

        def transposed_parts():
            return ((pT[:, :, 0:2 * P].rearrange("p c (b t) -> p c b t", b=2), 0, P),
                    (pT[:, :, 2 * P:3 * P].rearrange("p c (b t) -> p c b t", b=2)[:, :, :, 0:TAIL], P, T))

        with nc.Block() as block:

            @block.sync
            def _(sp):
                def load_patches(n):
                    sp.dma_start(xi[n % 3][:, :, :], xt[:, n, :, :]).then_inc(ld_xi[n % 3], 16)

                sp.dma_start(wt[:, 0:KE // 2, :], w_tok[:, 0:KE // 2, :]).then_inc(ld_wt, 16)
                load_patches(0)
                sp.dma_start(wt[:, KE // 2:KE, :], w_tok[:, KE // 2:KE, :]).then_inc(ld_w0, 16)
                load_patches(1)
                sp.dma_start(bt[:, :], b_tok.broadcast_to([P, D])).then_inc(ld_w0, 16)
                sp.dma_start(con[:, :], consts).then_inc(ld_w0, 16)
                load_patches(2)
                for dst, src in ((wqt, a_wqt), (wkt, a_wkt), (wv, a_wv)):
                    sp.dma_start(dst[:, :, :], src).then_inc(ld_w1, 16)
                sp.dma_start(gcol[:, :], f_g).then_inc(ld_w2, 16)
                sp.dma_start(wqt2[:, :, :], f_wqt).then_inc(ld_w2, 16)

                def embedded(n, k, half):
                    sp.wait_ge(s["e_evac"], n + 1)
                    sp.dma_start(scratch["h_tok"][n * P:(n + 1) * P, :], he[n % 3][:, :]).then_inc(st_he[n % 3], 16)
                    if n + 3 < NE:
                        load_patches(n + 3)

                def late_weights(n, k, half):
                    sp.dma_start(wqkv2[:, :, :], f_wqkv).then_inc(ld_w3, 16)
                    sp.dma_start(wp[:, :, :], f_wp).then_inc(ld_w3, 16)
                    sp.dma_start(bp[:, :], f_bp.broadcast_to([P, D])).then_inc(ld_w3, 16)

                for n in range(EARLY):
                    embedded(n, 0, 0)

                def load_h(n, k, half):
                    need(sp, s["st1_done"], (n - 1) * 3)
                    if isinstance(n, int) and n == 0:
                        sp.wait_ge(s["cleared"], 1)
                    tiles = -(-(n + 1) * 2 * NTOK // P) if isinstance(n, int) and n < 7 else NE
                    for j in range(3):
                        need(sp, st_he[j], 16 * ((tiles + 2 - j) // 3))
                    tok = scratch["h_tok"][bass.ds(n * 2 * NTOK, 2 * NTOK), :].rearrange("(b t) d -> t b d", b=2)
                    sp.dma_start(h0[0:NTOK, bass.ds(n * 2, 2), :], tok).then_inc(ld_h[k], 16)
                    sp.dma_start(h0[NTOK:P, bass.ds(n * 2, 2), :],
                                 txt[bass.ds(n * 2, 2), 0:P - NTOK, :].rearrange("b t d -> t b d")).then_inc(ld_h[k], 16)
                    for b in range(2):
                        sp.dma_start(ht[GAP * b:GAP * b + TAIL, bass.ds(n, 1), :],
                                     txt[bass.ds(n * 2 + b, 1), P - NTOK:NTXT, :].rearrange("b t d -> t b d")).then_inc(ld_h[k], 16)

                def load_first(n, k, half):
                    for j in range(2):
                        sp.wait_ge(st_x[j], 16 * VFIRST // 2)
                    for p in range(VFIRST):
                        sp.dma_start(xc[p][:, :, :], scratch["x2"][:, :, p * 2 * T:(p + 1) * 2 * T]).then_inc(ld_xc, 16)

                def store_q(n, k, half):
                    sp.wait_ge(s["q_dup"], 2 * n + 2)
                    for c in range(KC):
                        dst = scratch["q"][c * 8:c * 8 + 8, :, :, :, :].rearrange("h d i b t -> (h d) i (b t)")
                        sp.dma_start(dst[:, :, bass.ds(n * 2 * TQ, 2 * TQ)],
                                     qhl[k][:, :, c, :, :].rearrange("p i b t -> p i (b t)")).then_inc(st_q[k], 16)

                def store_k(n, k, half):
                    sp.wait_ge(s["k_lo"], n + 1)
                    for c in range(KC):
                        dst = scratch["k"][c * 8:c * 8 + 8, :, :, :, :].rearrange("h d i b t -> (h d) i (b t)")
                        sp.dma_start(dst[:, :, bass.ds(n * 2 * T, 2 * T)], khl[k][:, :, c, :]).then_inc(st_k[k], 16)

                def store_sim(n, k, half):
                    sp.wait_ge(s["sim_evac"], n + 1)
                    sp.sem_inc(s["sp_turn"], 1)
                    for i in range(2):
                        for b in range(2):
                            at = GAP * b + 32 * (1 - i)
                            sp.dma_start(scratch["sim"][i, :, bass.ds((n * 2 + b) * T, T)], ss[k][at:at + H, :]).then_inc(st_s[k], 16)

                def store_x2(n, k, half):
                    sp.wait_ge(s["x2t_lo"], 2 * n + 2)
                    sp.dma_start(scratch["x2"][:, :, bass.ds(n * 2 * T, 2 * T)],
                                 x2t[k][:, :, :, :].rearrange("p i c t -> p (i c) t")).then_inc(st_x[k], 16)

                run_steps(sp, [(-1, NPAIR, load_h), (-EARLY, NE, lambda n, k, half: embedded(n, k, half) if n >= EARLY else None),
                               (0, 1, late_weights), (4, NPAIR, store_x2), (4, NPAIR, store_q), (4, NPAIR, store_sim), (4, NPAIR, store_k), (NPAIR, 1, load_first)],
                          -1, 6, 14, NS, 2)
                for j in range(2):
                    sp.wait_ge(st_q[j], 32 * NPAIR // 2)
                    sp.wait_ge(st_k[j], 32 * NPAIR // 2)
                    sp.wait_ge(st_s[j], 64 * NPAIR // 2)
                    sp.wait_ge(st_x[j], 16 * NPAIR // 2)

            @block.gpsimd
            def _(pool):
                for i, (t, value) in enumerate(((ht[32:64, :, :], 0.0), (p2[:, P:P + PT], 0.0), (mx[96:P, :], 0.0),
                                                (mv1[96:P, :, :], 0.0), (mv2[96:P, :, :], 0.0), (su[:, :], 1.0),
                                                (mhalf[:, :], -0.5), (wg[:, :, :, :], 0.0))):
                    pool.memset(t, value).then_inc(s["cleared"], 1)
                    pool.wait_ge(s["cleared"], i + 1)

                def weights(n, k, half):
                    pool.wait_ge(s["gss_ready"], 1)
                    pool.tensor_tensor(grn[:, :], gss[:, :], mhalf[:, 0:KC], ALU.pow).then_inc(s["grn_ready"], 1)
                    pool.wait_ge(s["grn_ready"], 1)

                def rstd(mv, ve, rs, i):
                    def emit(n, k, half):
                        pool.wait_ge(s[f"mv{i}_done"], (n + 1) * 3)
                        pool.sem_inc(s["pool_turn"], 1)
                        pool.tensor_scalar(ve[:, :], mv[:, :, 1], EPS, 1.0, ALU.add, ALU.mult).then_inc(s[f"ve{i}_done"], 1)
                        pool.wait_ge(s[f"ve{i}_done"], n + 1)
                        pool.tensor_tensor(rs[:, :], ve[:, :], mhalf[:, :], ALU.pow).then_inc(s[f"rs{i}_done"], 1)
                        pool.wait_ge(s[f"rs{i}_done"], n + 1)
                    return emit

                def register_copies(n, k, half):
                    pool.wait_ge(s["q_lo"], n + 1)
                    pool.sem_inc(s["pool_turn"], 1)
                    for i in range(2):
                        t3 = qhl[k][:, i, :, :, :].rearrange("p c b t -> p (c b) t")
                        pool.tensor_copy(t3[:, :, T:TQ], t3[:, :, 0:REG]).then_inc(s["q_dup"], 1)
                        pool.wait_ge(s["q_dup"], 2 * n + i + 1)
                        pool.sem_inc(s["pool_turn"], 1)

                run_steps(pool, [(1, 1, weights), (0, NPAIR, rstd(mv1, ve1, rs1, 1)), (3, NPAIR, rstd(mv2, ve2, rs2, 2)), (4, NPAIR, register_copies)],
                          0, 6, 16, NS, 2)

            @block.tensor
            def _(pe):
                def embed(n, k, half):
                    step = n - EARLY
                    pe.wait_ge(ld_xi[n % 3], 16 * (n // 3 + 1))
                    need(pe, s["e_evac"], n - 1)
                    if step >= 0:
                        need(pe, s["qt_lo"], step - 2)
                        need(pe, s["k_lo"], step - 4)
                    for c in range(KE):
                        if n == 0 and c in (0, KE // 2):
                            pe.wait_ge(ld_w0 if c else ld_wt, 48 if c else 16)
                        mm = pe.matmul(pP[:, n % 2, 0:D], xi[n % 3][:, c, :], wt[:, c, :], start=(c == 0), stop=(c == KE - 1))
                    mm.then_inc(s["e_done"], 1)

                def weights(n, k, half):
                    pe.wait_ge(ld_w1, 48)
                    for i in range(KC):
                        for c in range(KC):
                            mm = pe.matmul(pV[:, 0, i * D:(i + 1) * D], wqt[:, c, i * P:(i + 1) * P], wkt[:, c, :],
                                           start=(c == 0), stop=(c == KC - 1))
                    mm.then_inc(s["wqk_done"], 1)
                    pe.wait_ge(s["gsq_ready"], 1)
                    pe.matmul(pR[:, 0:KC], con[:, C_BB:C_BB + P], gsq[:, :], start=True, stop=True).then_inc(s["gss_done"], 1)

                def weights_g(n, k, half):
                    pe.wait_ge(s["gblk_ready"], KC)
                    for i in range(KC):
                        for c in range(KC):
                            mm = pe.matmul(pR[:, i * H:(i + 1) * H], wqt2[:, c, i * P:(i + 1) * P], gblk[:, c, :],
                                           start=(c == 0), stop=(c == KC - 1))
                    mm.then_inc(s["wg_done"], 1)

                for n in range(EARLY):
                    embed(n, 0, 0)

                def split_product(dst, lhs, rhs):
                    terms = [(i, j, c) for c in range(KC) for i, j in HALVES]
                    for m, (i, j, c) in enumerate(terms):
                        mm = pe.matmul(dst, lhs(i, c), rhs(j, c), start=(m == 0), stop=(m == len(terms) - 1), skip_group_check=True)
                    return mm

                def transpose_in(x, done):
                    for c in range(KC):
                        for j in range(3):
                            w = PT if j == 2 else P
                            mm = pe.transpose(pT[:, c, j * P:j * P + w], x[0:w, j, c * P:(c + 1) * P], ident[0:w, 0:w])
                    mm.then_inc(s[done], 1)

                def t1(n, k, half):
                    pe.wait_ge(s["x1_ready"], 3 * n + 3)
                    need(pe, s["x2t_lo"], (n - 2) * 2)
                    transpose_in(x1, "t1_done")

                def t2(n, k, half):
                    pe.wait_ge(s["x2_ready"], 3 * n + 3)
                    need(pe, s["x1t_lo"], upto((n + 3) * 2, 2 * NPAIR))
                    transpose_in(x2, "t2_done")

                def qproj(n, k, half):
                    pe.wait_ge(s["x1t_lo"], (n + 1) * 2)
                    need(pe, s["k_lo"], n - 2)
                    if isinstance(n, int) and n == 0:
                        pe.wait_ge(s["wqk_lo"], 1)
                    if isinstance(n, int) and n + 2 + EARLY < NE:
                        pe.wait_ge(s["e_evac"], n + 3 + EARLY)
                    for m in range(KC):
                        mm = split_product(pP[:, m, 0:2 * T], lambda i, c: wqks[:, i, c, m * P:(m + 1) * P], lambda i, c: x1t[k][:, i, c, :])
                    mm.then_inc(s["qt_done"], 1)

                def vproj(n, k, half):
                    if isinstance(n, int) and n == 0:
                        pe.wait_ge(s["wv_lo"], 1)
                    need(pe, s["h1_done"], n * 3)
                    for b in range(2):
                        split_product(pV[:, 0, b * D:(b + 1) * D], lambda i, c: x1t[k][:, i, c, b * T:b * T + P], lambda i, c: wvs[:, i, c, :])
                    for b in range(2):
                        w = GAP if b == 0 else TAIL
                        mm = split_product(pV[GAP * b:GAP * b + w, 1, 0:D], lambda i, c: x1t[k][:, i, c, b * T + P:b * T + P + w],
                                           lambda i, c: wvs[:, i, c, :])
                    mm.then_inc(s["v_done"], 1)

                def scores(n, k, half):
                    pe.wait_ge(s["qt_lo"], n + 1)
                    need(pe, s["sm_done"], 3 * n)
                    for b in range(2):
                        split_product(pS[:, b * P:(b + 1) * P], lambda i, c: qt[:, i, c, b * T:b * T + P],
                                      lambda i, c: x1t[k][:, i, c, b * T:b * T + P])
                    for b in range(2):
                        w = GAP if b == 0 else TAIL
                        mm = split_product(pS[GAP * b:GAP * b + w, 2 * P:2 * P + T], lambda i, c: qt[:, i, c, b * T + P:b * T + P + w],
                                           lambda i, c: x1t[k][:, i, c, b * T:b * T + T])
                    mm.then_inc(s["s_done"], 1)

                def ptrans(n, k, half):
                    pe.wait_ge(s["p_ready"], 5 * n + 5)
                    need(pe, s["sim_evac"], n - 1)
                    if isinstance(n, int) and n == 0:
                        pe.wait_ge(s["wg_ready"], 1)
                    for b in range(2):
                        pe.transpose(pR[:, b * P:(b + 1) * P], p0[:, b, :], ident)
                    pe.transpose(pR[:, 2 * P:2 * P + PT], p2[0:PT, 0:P], ident[0:PT, 0:PT])
                    pe.transpose(pR[0:PT, 2 * P + PT:2 * P + 2 * PT], p2[0:PT, P:P + PT], ident[0:PT, 0:PT]).then_inc(s["pt_done"], 1)

                def context(n, k, half):
                    pe.wait_ge(s["pts_ready"], (n + 1) * 2)
                    pe.wait_ge(s["v_ready"], (n + 1) * 2)
                    for b in range(2):
                        pe.matmul(pV[:, 0, b * D:(b + 1) * D], pts[:, b * P:(b + 1) * P], v0[k][:, b, :], start=True, stop=True)
                    for b in range(2):
                        w = GAP if b == 0 else TAIL
                        pe.matmul(pV[GAP * b:GAP * b + w, 1, 0:D], pts[:, 2 * P + GAP * b:2 * P + GAP * b + w], v0[k][:, b, :],
                                  start=True, stop=False, skip_group_check=True)
                    pe.matmul(pV[0:PT, 1, 0:D], ptt[0:PT, :], vt[k][0:PT, :], start=False, stop=True,
                              skip_group_check=True).then_inc(s["pv_done"], 1)

                def qk_columns(k, col, done):
                    for m in range(KC):
                        mm = split_product(pP[:, m, 0:2 * T], lambda i, c: wqk2[:, i, c, col + m * P:col + (m + 1) * P],
                                           lambda i, c: x2t[k][:, i, c, :])
                    mm.then_inc(s[done], 1)

                def qcols(n, k, half):
                    pe.wait_ge(s["x2t_lo"], (n + 1) * 2)
                    if isinstance(n, int) and n == 0:
                        pe.wait_ge(s["w2_lo"], 2)
                    need(pe, s["qt_lo"], upto(n + 3, NPAIR))
                    qk_columns(k, 0, "q_done")

                def kcols(n, k, half):
                    pe.wait_ge(s["q_lo"], n + 1)
                    qk_columns(k, D, "k_done")

                def first_values(p):
                    def emit(n, k, half):
                        first, tails = VBANKS[p % 2]
                        pe.wait_ge(ld_xc, 16 * VFIRST)
                        pe.wait_ge(s["h1_done"], 3 * NPAIR)
                        pe.wait_ge(s["x2t_lo"], 2 * NPAIR)
                        need(pe, first_va, 2 * (p - 1))
                        for b in range(2):
                            split_product(first[:, b * D:(b + 1) * D], lambda i, c: xc[p][:, i * KC + c, b * T:b * T + P], lambda i, c: wv2[:, i, c, :])
                        for b in range(2):
                            w = GAP if b == 0 else TAIL
                            mm = split_product(tails[GAP * b:GAP * b + w, 0:D], lambda i, c: xc[p][:, i * KC + c, b * T + P:b * T + P + w],
                                               lambda i, c: wv2[:, i, c, :])
                        mm.then_inc(first_v, 1)
                    return emit

                def simparts(n, k, half):
                    pe.wait_ge(s["q_hi"], 2 * n + 2)
                    need(pe, s["pts_ready"], upto((n + 2) * 2, 2 * NPAIR))
                    for c in range(KC):
                        for m, (i, j) in enumerate(HALVES):
                            for b in range(2):
                                t = slice(b * T, (b + 1) * T)
                                mm = pe.matmul(pR[GAP * b:GAP * b + 32, 0:T], wg[:, i, c, :], x2t[k][:, j, c, t],
                                               start=(c == 0 and m == 0), stop=(c == KC - 1 and m == 2), skip_group_check=True)
                                if m == 0:
                                    pe.matmul(pR[GAP * b + 32:GAP * b + 64, 0:T], con[:, C_OB + 32 * c:C_OB + 32 * c + 32],
                                              qsq[:, c, t], start=(c == 0), stop=(c == KC - 1), skip_group_check=True)
                    mm.then_inc(s["sim_done"], 1)

                run_steps(pe, [(-EARLY, NE, lambda n, k, half: embed(n, k, half) if n >= EARLY else None), (1, 1, weights), (2, 1, weights_g),
                               (3, NPAIR, ptrans), (2, NPAIR, qproj), (1, NPAIR, t1), (3, NPAIR, context), (4, NPAIR, qcols),
                               (2, NPAIR, scores), (2, NPAIR, vproj), (LASTV, 1, first_values(0)), (4, NPAIR, kcols), (3, NPAIR, t2),
                               (4, NPAIR, simparts)] + [(LASTV, 1, first_values(p)) for p in range(1, VFIRST)], 0, *LOOP, NS, 2)

            @block.scalar
            def _(act):
                def wqk_copy(n, k, half):
                    act.wait_ge(s["wqk_done"], 1)
                    nc.scalar.activation(wqks[:, 0, :, :].rearrange("p c d -> p (c d)"), pV[:, 0, :], ACT.Copy, scale=UP / 16.0).then_inc(s["wqk_hi"], 1)
                    act.wait_ge(ld_w1, 48)
                    nc.scalar.activation(wvs[:, 0, :, :], wv[:, :, :], ACT.Copy, scale=UP).then_inc(s["wv_hi"], 1)

                def split_wg(n, k, half):
                    act.wait_ge(s["wg_done"], 1)
                    act.wait_ge(s["cleared"], 8)
                    nc.scalar.activation(wg[:, 0, :, 0:H], pR[:, 0:KC * H].rearrange("p (c h) -> p c h", c=KC), ACT.Copy, scale=UP).then_inc(s["wg_hi"], 1)

                def split_w2(n, k, half):
                    act.wait_ge(ld_w3, 48)
                    nc.scalar.activation(wqk2[:, 0, :, :], wqkv2[:, :, 0:2 * D], ACT.Copy, scale=UP).then_inc(s["w2_hi"], 1)
                    nc.scalar.activation(wv2[:, 0, :, :], wqkv2[:, :, 2 * D:3 * D], ACT.Copy, scale=UP).then_inc(s["w2_hi"], 1)

                def exps_first(n, k, half):
                    act.wait_ge(s["nm_ready"], n + 1)
                    need(act, s["pt_done"], n)
                    for b in range(2):
                        nc.scalar.activation(p0[:, b, :], sm[:, b * P:(b + 1) * P], ACT.Exp, bias=nm[:, b:b + 1],
                                             accum_out=su[:, b:b + 1]).then_inc(s["p_ready"], 1)

                def exps_tails(n, k, half):
                    nc.scalar.activation(p2[0:PT, 0:P], sm[0:PT, 2 * P:3 * P], ACT.Exp, bias=nm[0:PT, 2:3],
                                         accum_out=su[0:PT, 2:3]).then_inc(s["p_ready"], 1)
                    for b in range(2):
                        r = slice(GAP * b, GAP * b + (GAP if b == 0 else TAIL))
                        nc.scalar.activation(p2[r, P + GAP * b:P + GAP * b + TAIL], sm[r, 3 * P:2 * P + T], ACT.Exp, bias=nm[r, 2:3],
                                             accum_out=su[r, 3:4]).then_inc(s["p_ready"], 1)

                def pts_copy(n, k, half):
                    act.wait_ge(s["pt_done"], n + 1)
                    need(act, s["pv_done"], n)
                    nc.scalar.activation(pts[:, :], pR[:, 0:2 * P + PT], ACT.Copy).then_inc(s["pts_ready"], 1)
                    nc.scalar.activation(ptt[0:PT, :], pR[0:PT, 2 * P + PT:2 * P + 2 * PT], ACT.Copy).then_inc(s["pts_ready"], 1)

                def qt_copy(n, k, half):
                    act.wait_ge(s["qt_done"], n + 1)
                    need(act, s["s_done"], n)
                    nc.scalar.activation(qt[:, 0, :, :], pP[:, :, 0:2 * T], ACT.Copy, scale=1 / UP).then_inc(s["qt_hi"], 1)

                def v_copy(n, k, half):
                    act.wait_ge(s["v_done"], n + 1)
                    nc.scalar.activation(v0[k][:, :, :].rearrange("p b d -> p (b d)"), pV[:, 0, :], ACT.Copy, scale=1 / UP).then_inc(s["v_ready"], 1)
                    nc.scalar.activation(vt[k][0:PT, :], pV[0:PT, 1, 0:D], ACT.Copy, scale=1 / UP).then_inc(s["v_ready"], 1)

                def transposed_high(dst, done):
                    d4 = dst[:, 0, :, :].rearrange("p c (b t) -> p c b t", b=2)
                    for src, lo, hi in transposed_parts():
                        nc.scalar.activation(d4[:, :, :, lo:hi], src, ACT.Copy).then_inc(s[done], 1)

                def x1t_high(n, k, half):
                    act.wait_ge(s["t1_done"], n + 1)
                    need(act, s["v_done"], n - 1)
                    transposed_high(x1t[k], "x1t_hi")

                def x2t_high(n, k, half):
                    act.wait_ge(s["t2_done"], n + 1)
                    need(act, s["sim_done"], n - 1)
                    need(act, st_x[k], half * 16)
                    transposed_high(x2t[k], "x2t_hi")

                def q_high(n, k, half):
                    act.wait_ge(s["q_done"], n + 1)
                    need(act, st_q[k], half * 32)
                    need(act, s["sim_done"], n)
                    q4 = pP[:, :, 0:2 * T].rearrange("p c (b t) -> p c b t", b=2)
                    nc.scalar.activation(qsq[:, :, :], pP[:, :, 0:2 * T], ACT.Square, scale=1 / UP).then_inc(s["q_hi"], 1)
                    nc.scalar.activation(qhl[k][:, 0, :, :, 0:T], q4, ACT.Copy, scale=0.25 / UP).then_inc(s["q_hi"], 1)

                def k_high(n, k, half):
                    act.wait_ge(s["k_done"], n + 1)
                    need(act, st_k[k], half * 32)
                    nc.scalar.activation(khl[k][:, 0, :, :], pP[:, :, 0:2 * T], ACT.Copy, scale=1 / UP).then_inc(s["k_hi"], 1)

                def first_values(p):
                    def emit(n, k, half):
                        act.wait_ge(first_v, p + 1)
                        first, tails = VBANKS[p % 2]
                        nc.scalar.activation(va[:, 2 * p:2 * p + 2, :].rearrange("p b d -> p (b d)"), first, ACT.Copy,
                                             scale=1 / UP).then_inc(first_va, 1)
                        nc.scalar.activation(vta[0:PT, p, :], tails[0:PT, 0:D], ACT.Copy, scale=1 / UP).then_inc(first_va, 1)
                    return emit

                def sim_copy(n, k, half):
                    act.wait_ge(s["sim_done"], n + 1)
                    need(act, st_s[k], half * 64)
                    nc.scalar.activation(ss[k][:, :], pR[:, 0:T], ACT.Copy).then_inc(s["sim_evac"], 1)

                run_steps(act, [(1, 1, wqk_copy), (2, 1, split_wg), (3, 1, split_w2), (4, NPAIR, x2t_high), (3, NPAIR, pts_copy),
                                (3, NPAIR, v_copy), (2, NPAIR, qt_copy), (1, NPAIR, x1t_high), (4, NPAIR, q_high), (2, NPAIR, exps_first),
                                (2, NPAIR, exps_tails), (4, NPAIR, k_high), (4, NPAIR, sim_copy)] +
                          [(LASTV, 1, first_values(p)) for p in range(VFIRST)], 0, *LOOP, NS, 2)

            @block.vector
            def _(dve):
                dve.wait_ge(ld_w0, 48)

                def low(dst, src, scale, high):
                    return dve.scalar_tensor_tensor(out=dst, in0=src, scalar=scale, in1=high, op0=ALU.mult, op1=ALU.subtract)

                def embed_bias(n, k, half):
                    dve.wait_ge(s["e_done"], n + 1)
                    need(dve, st_he[n % 3], 16 * (n // 3))
                    dve.tensor_tensor(he[n % 3][:, :], pP[:, n % 2, 0:D], bt[:, :], ALU.add).then_inc(s["e_evac"], 1)

                def weights(n, k, half):
                    dve.tensor_copy(ident16[:, :], ident).then_inc(s["id16_ready"], 1)
                    dve.wait_ge(ld_w2, 32)
                    dve.tensor_tensor(gsq[:, :], gcol[:, :], gcol[:, :], ALU.mult).then_inc(s["gsq_ready"], 1)
                    dve.wait_ge(s["gss_done"], 1)
                    dve.tensor_copy(gss[:, :], pR[:, 0:KC]).then_inc(s["gss_ready"], 1)
                    dve.wait_ge(s["wqk_hi"], 1)
                    low(wqks[:, 1, :, :].rearrange("p c d -> p (c d)"), pV[:, 0, :], UP / 16.0,
                        wqks[:, 0, :, :].rearrange("p c d -> p (c d)")).then_inc(s["wqk_lo"], 1)
                    dve.wait_ge(s["wv_hi"], 1)
                    low(wvs[:, 1, :, :], wv[:, :, :], UP, wvs[:, 0, :, :]).then_inc(s["wv_lo"], 1)

                def split_w2(n, k, half):
                    dve.wait_ge(s["w2_hi"], 2)
                    low(wqk2[:, 1, :, :], wqkv2[:, :, 0:2 * D], UP, wqk2[:, 0, :, :]).then_inc(s["w2_lo"], 1)
                    low(wv2[:, 1, :, :], wqkv2[:, :, 2 * D:3 * D], UP, wv2[:, 0, :, :]).then_inc(s["w2_lo"], 1)

                def weights_g(n, k, half):
                    dve.wait_ge(s["grn_ready"], 1)
                    dve.tensor_tensor(gn[:, :], gcol[:, :], grn[:, :], ALU.mult).then_inc(s["gn_ready"], 1)
                    dve.wait_ge(s["gn_ready"], 1)
                    for c in range(KC):
                        dve.tensor_scalar(gblk[:, c, :], con[:, C_OB + 32 * c:C_OB + 32 * c + H], gn[:, c:c + 1], None,
                                          ALU.mult).then_inc(s["gblk_ready"], 1)
                    dve.wait_ge(s["wg_hi"], 1)
                    low(wg[:, 1, :, 0:H], pR[:, 0:KC * H].rearrange("p (c h) -> p c h", c=KC), UP, wg[:, 0, :, 0:H]).then_inc(s["wg_ready"], 1)

                for n in range(EARLY):
                    embed_bias(n, 0, 0)
                dve.wait_ge(s["cleared"], 8)

                def rows(n, j):
                    return h0[:, bass.ds(n * 2 + j, 1), :].rearrange("p a d -> p (a d)") if j < 2 else \
                        ht[0:PT, bass.ds(n, 1), :].rearrange("p a d -> p (a d)")

                def width(j):
                    return PT if j == 2 else P

                def stats(n, st, mv, i):
                    dve.sem_inc(s["dve_turn"], 1)
                    for j in range(3):
                        dve.bn_stats(st[0:width(j), j, :], rows(n, j)).then_inc(s[f"st{i}_done"], 1)
                    dve.wait_ge(s[f"st{i}_done"], 3 * n + 3)
                    dve.sem_inc(s["dve_turn"], 1)
                    for j in range(3):
                        dve.bn_aggr(mv[0:width(j), j, :], st[0:width(j), j, :]).then_inc(s[f"mv{i}_done"], 1)

                def normalise(n, x, mv, rs, ready):
                    for j in range(3):
                        w = width(j)
                        dve.tensor_scalar(x[0:w, j, :], rows(n, j), mv[0:w, j, 0:1], rs[0:w, j:j + 1],
                                          ALU.subtract, ALU.mult).then_inc(s[ready], 1)

                def stats1(n, k, half):
                    dve.wait_ge(ld_h[k], half * 64 + 64)
                    stats(n, st1, mv1, 1)

                def norm1(n, k, half):
                    dve.wait_ge(s["rs1_done"], n + 1)
                    need(dve, s["t1_done"], n)
                    normalise(n, x1, mv1, rs1, "x1_ready")

                def masks(n, k, half):
                    dve.wait_ge(s["s_done"], n + 1)
                    need(dve, s["p_ready"], 5 * n)
                    dve.sem_inc(s["dve_turn"], 1)
                    for j, (c0, w, c) in enumerate(((0, P, C_M0), (P, P, C_M0), (2 * P, T, C_MT))):
                        r = width(j)
                        dve.tensor_tensor_reduce(sm[0:r, c0:c0 + w], pS[0:r, c0:c0 + w], con[0:r, c:c + w], 1.0, -3e38,
                                                 ALU.add, ALU.max, mx[0:r, j:j + 1]).then_inc(s["sm_done"], 1)
                    dve.wait_ge(s["sm_done"], 3 * n + 3)
                    dve.tensor_scalar(nm[:, :], mx[:, :], -1.0, None, ALU.mult).then_inc(s["nm_ready"], 1)

                def sums(n, k, half):
                    dve.wait_ge(s["p_ready"], 5 * n + 5)
                    dve.tensor_tensor(su[0:PT, 2:3], su[0:PT, 2:3], su[0:PT, 3:4], ALU.add).then_inc(s["sum_added"], 1)
                    dve.wait_ge(s["sum_added"], n + 1)
                    dve.reciprocal(rsum[:, :], su[:, 0:3]).then_inc(s["rsum_ready"], 1)

                def h1_stats2(n, k, half):
                    dve.wait_ge(s["pv_done"], n + 1)
                    dve.wait_ge(s["rsum_ready"], n + 1)
                    for j in range(3):
                        r = width(j)
                        src = pV[:, 0, j * D:(j + 1) * D] if j < 2 else pV[0:PT, 1, 0:D]
                        dve.scalar_tensor_tensor(out=rows(n, j), in0=src, scalar=rsum[0:r, j:j + 1], in1=rows(n, j),
                                                 op0=ALU.mult, op1=ALU.add).then_inc(s["h1_done"], 1)
                    dve.wait_ge(s["h1_done"], 3 * n + 3)
                    stats(n, st2, mv2, 2)

                def norm2(n, k, half):
                    dve.wait_ge(s["rs2_done"], n + 1)
                    need(dve, s["t2_done"], n)
                    normalise(n, x2, mv2, rs2, "x2_ready")

                def transposed_low(dst, done):
                    h4, l4 = (dst[:, i, :, :].rearrange("p c (b t) -> p c b t", b=2) for i in range(2))
                    for src, lo, hi in transposed_parts():
                        dve.tensor_tensor(l4[:, :, :, lo:hi], src, h4[:, :, :, lo:hi], ALU.subtract).then_inc(s[done], 1)

                def x1t_low(n, k, half):
                    dve.wait_ge(s["x1t_hi"], 2 * n + 2)
                    transposed_low(x1t[k], "x1t_lo")

                def x2t_low(n, k, half):
                    dve.wait_ge(s["x2t_hi"], 2 * n + 2)
                    transposed_low(x2t[k], "x2t_lo")

                def qt_low(n, k, half):
                    dve.wait_ge(s["qt_hi"], n + 1)
                    low(qt[:, 1, :, :], pP[:, :, 0:2 * T], 1 / UP, qt[:, 0, :, :]).then_inc(s["qt_lo"], 1)

                def q_low(n, k, half):
                    dve.wait_ge(s["q_hi"], 2 * n + 2)
                    q4 = pP[:, :, 0:2 * T].rearrange("p c (b t) -> p c b t", b=2)
                    low(qhl[k][:, 1, :, :, 0:T], q4, 0.25 / UP, qhl[k][:, 0, :, :, 0:T]).then_inc(s["q_lo"], 1)

                def k_low(n, k, half):
                    dve.wait_ge(s["k_hi"], n + 1)
                    low(khl[k][:, 1, :, :], pP[:, :, 0:2 * T], 1 / UP, khl[k][:, 0, :, :]).then_inc(s["k_lo"], 1)

                run_steps(dve, [(-EARLY, NE, lambda n, k, half: embed_bias(n, k, half) if n >= EARLY else None), (1, 1, weights), (2, 1, weights_g), (3, 1, split_w2),
                                (4, NPAIR, x2t_low), (3, NPAIR, sums), (0, NPAIR, stats1), (2, NPAIR, qt_low),
                                (1, NPAIR, x1t_low), (3, NPAIR, h1_stats2), (4, NPAIR, q_low), (2, NPAIR, masks),
                                (3, NPAIR, norm2), (0, NPAIR, norm1), (4, NPAIR, k_low)],
                          0, 6, 16, NS, 2)


def second_phase(nc, keep, scratch, consts16, out):
    con, ident16, ident, h0, ht, wv2, wp, bp, va, vta = keep
    with ExitStack() as ctx:
        def sb(name, shape, dt=F32):
            return ctx.enter_context(nc.sbuf_tensor(name, shape, dt))

        def sem(name):
            return ctx.enter_context(nc.semaphore(name))

        def ps(name, shape):
            return ctx.enter_context(nc.psum_tensor(name, shape, F32))

        QW = H * TQ + 32
        qs = [sb(f"qs{j}", [P, QW], F16) for j in range(4)]
        ks = [sb(f"ks{j}", [P, H, KPAD], F16) for j in range(4)]
        mx = [sb(f"mx{j}", [P, 24]) for j in range(2)]
        mh = [sb(f"mh{j}", [P, 24], F16) for j in range(2)]
        mr = [sb(f"mr{j}", [16, P], F16) for j in range(2)]
        mrt = [sb(f"mrt{j}", [8, P], F16) for j in range(2)]
        em = sb("em", [P, H, TQ])
        et = sb("et", [P, H // 2, TQ])
        vm = [sb(f"vm{j}", [P, H, 32]) for j in range(4)]
        vt = [sb(f"vt2_{j}", [P, H, 32]) for j in range(4)]
        os_ = sb("os", [P, 4, TQ])
        rd = sb("rd", [P, 2, H])
        on = sb("on", [P, 2, D])
        OFW = KC * TQ + 24
        of = [sb(f"of{j}", [P, OFW]) for j in range(2)]
        hb = sb("hb", [P, 3, D])
        ot = [sb(f"ot{j}", [P, 3, D]) for j in range(2)]
        xc = [t[:, :, :].rearrange("p j d -> p (j d)").bitcast(F16)[:, 0:4 * KC * T].rearrange("p (c t) -> p c t", t=2 * T)
              for t in (ot[0], ot[1], hb, os_)]
        HQ = H * QUARTER
        flat = em[:, :, :].rearrange("p h t -> p (h t)")
        sq, num, nrm, rec = (flat[:, i * HQ:(i + 1) * HQ] for i in range(4))
        cos = et[:, :, :].rearrange("p h t -> p (h t)")[:, 0:HQ]
        sim, nsim, pos, ca, cn = (sb(m, [P, QUARTER]) for m in ("sim", "nsim", "pos", "ca", "cn"))
        junk = sb("junk", [P, 2, QUARTER])
        ext, rng, dd = (sb(m, [P, 2]) for m in ("ext", "rng", "dd"))
        g2, gd, ones2 = sb("g2", [2, 1]), sb("gd", [2, 2]), sb("ones2", [2, P])
        cls = sb("cls", [P, 4, QUARTER], F16)

        pA = [ps(f"pA{j}", [P, 512]) for j in range(2)]
        pB = [ps(f"pB{j}", [P, 512]) for j in range(2)]
        pO = ps("pO", [P, 2, 512])
        pX = ps("pX", [P, 2, 512])
        pM16 = pX[:, 1, :].bitcast(F16)
        p_ext, p_rng = pX[:, 0, :], pX[:, 1, :]
        VBANKS = ((pB[0][:, :], pB[1][:, :]), (pO[:, 0, :], pO[:, 1, :]))
        VEARLY, VSTEP = 10, 3
        VCLASS = 7

        names = ("set_up dve_set_up a_done a_max mh_ready mt_done mt_evac b_done e_ready pv_done os_ready c1_done rd_ready on_ready "
                 "c2_done of_copied of_ready v_done va_ready v_ready f_done hb_ready out_ready pe_turn").split()
        s = {n: sem(n) for n in names}
        ld_set = sem("ld_set")
        ld_sim, nrm_ready, class_step, ext_t, ext_b, st_class = (sem(m) for m in (
            "ld_sim", "nrm_ready", "class_step", "ext_transposed", "range_spread", "st_class"))
        ld_stack = [sem(f"ld_stack{j}") for j in range(4)]
        ld_shift = [sem(f"ld_shift{j}") for j in range(4)]
        ld_xc = [sem(f"ld_xc{j}") for j in range(4)]
        st_out = [sem(f"st_out{j}") for j in range(2)]

        def q_head(j, rows, h, c0, w):
            return qs[j][0:rows, h * TQ + c0:h * TQ + c0 + w]

        GROUPS = [g for a in range(4) for g in ((False, 2 * a), (False, 2 * a + 1), (True, a))]
        NG = len(GROUPS)
        SETUP = 2 * 5 + 4 * 2 + 2 + 4 * 2
        DVE_SETUP = 2 * 5
        CLASS_STEPS = 19
        LOOP = (8, 32)
        NSTEP = 36

        def tiles(group):
            tail, g = group
            if not tail:
                return [(2 * g + i, 0, i) for i in range(2)]
            return [(4 * g + 2 * i + j, GAP * j, i) for i in range(2) for j in range(2)]

        def pair_of(n, half, k):
            return half * 2 + k // 2

        def blank_stack(j):
            k32 = ks[j][:, :, :].rearrange("p h t -> p (h t)").bitcast(F32)
            return [(qs[j][64:P, :].bitcast(F32), 0.0), (qs[j][0:64, H * TQ:QW], 0.0), (ks[j][0:64, :, T:KPAD], 0.0),
                    (k32[64:96, :], 0.0), (k32[96:P, :], TWO_ONES)]

        def load_xc(eng, p, j):
            eng.dma_start(xc[j], scratch["x2"][:, :, bass.ds(p * 2 * T, 2 * T)]).then_inc(ld_xc[j], 16)

        with nc.Block() as block:

            @block.gpsimd
            def _(pool):
                blank = [x for j in (1, 3) for x in blank_stack(j)]
                for j in range(4):
                    blank += [(vm[j][:, :, 16:32], 1.0), (vt[j][:, :, :], 0.0)]
                blank += [(of[j][:, KC * TQ:OFW], 0.0) for j in range(2)]
                for j in range(4):
                    v4 = vt[j][:, :, :].rearrange("p (g e) c -> p g e c", e=2)
                    blank += [(v4[GAP * e:GAP * e + TAIL, :, e, 16:17], 1.0) for e in range(2)]
                for i, (t, value) in enumerate(blank):
                    pool.memset(t, value).then_inc(s["set_up"], 1)
                    pool.wait_ge(s["set_up"], i + 1)

                def biased(n, k, half):
                    if k % 2 == 0:
                        return
                    p = pair_of(n, half, k)
                    need(pool, s["out_ready"], 3 * p)
                    pool.wait_ge(s["v_done"], 3 * (NPAIR - VFIRST))
                    pool.tensor_tensor(hb[:, 0:2, :], h0[:, bass.ds(p * 2, 2), :], bp[:, :].rearrange("p (a d) -> p a d", a=1).broadcast_to([P, 2, D]),
                                       ALU.add).then_inc(s["hb_ready"], 1)
                    pool.wait_ge(s["hb_ready"], 2 * p + 1)
                    pool.tensor_tensor(hb[0:PT, 2, :], ht[0:PT, bass.ds(p, 1), :].rearrange("p a d -> p (a d)"), bp[0:PT, :],
                                       ALU.add).then_inc(s["hb_ready"], 1)

                run_steps(pool, [(3, B, biased)], 2, *LOOP, NSTEP, 4)

            @block.sync
            def _(sp):
                load_xc(sp, VFIRST, 0)
                for i, dst in enumerate((sq, num)):
                    sp.dma_start(dst.rearrange("p (h t) -> p h t", h=H),
                                 scratch["sim"][i, :, :].rearrange("h (p t) -> p h t", t=QUARTER)).then_inc(ld_sim, 16)

                def load_features(n, k):
                    q3 = qs[k][:, 0:H * TQ].rearrange("p (h t) -> p h t", h=H)
                    for r in range(2):
                        sp.dma_start(q3[32 * r:32 * r + 32, :, :],
                                     scratch["q"][:, :, :, bass.ds(n, 1), :].rearrange("h d i b t -> (d i) h (b t)")).then_inc(ld_stack[k], 16)
                    sp.dma_start(ks[k][0:32, :, 0:T],
                                 scratch["k"][:, :, :, bass.ds(n, 1), :].rearrange("h d i b t -> (d i) h (b t)")).then_inc(ld_stack[k], 16)
                    for i in range(2):
                        sp.dma_start(ks[k][33 - i:64:2, :, 0:T],
                                     scratch["k"][:, :, i, bass.ds(n, 1), :].rearrange("h d b t -> d h (b t)")).then_inc(ld_stack[k], 16)

                def load_classes(n, k):
                    q3 = qs[k][:, 0:H * TQ].rearrange("p (h t) -> p h t", h=H)
                    for i, dst in enumerate((q3[64:66, :, 0:T], ks[k][64:66, :, 0:T])):
                        row = scratch["cls"][2 * i:2 * i + 2, bass.ds(n * T, T)].rearrange("r (a t) -> r a t", a=1)
                        sp.dma_start(dst, row.broadcast_to([2, H, T])).then_inc(ld_stack[k], 16)

                def load_stack(n, k, half):
                    need(sp, s["b_done"], NG * (n - 3))
                    load_features(n, k)
                    load_classes(n, k)

                def load_shift(n, k, half):
                    sp.wait_ge(s["mt_evac"], 2 * n + 2)
                    q3 = qs[k][:, 0:H * TQ].rearrange("p (h t) -> p h t", h=H)
                    q4 = qs[k][:, 0:H * TQ].rearrange("p (g e t) -> p g e t", e=2, t=TQ)
                    sp.dma_start(q3[SHIFT_ROW:P, :, 0:P], mr[k % 2][:, :]).then_inc(ld_shift[k], 16)
                    for e in range(2):
                        sp.dma_start(q4[SHIFT_ROW:P, :, e, P:TQ], mrt[k % 2][:, GAP * e:GAP * e + QTAIL]).then_inc(ld_shift[k], 16)

                def store_out(n, k, half):
                    if k % 2 == 0:
                        return
                    p = pair_of(n, half, k)
                    pp = k // 2
                    sp.wait_ge(s["out_ready"], 3 * p + 3)
                    sp.dma_start(out[bass.ds(p * 2, 2), 0:P, :].rearrange("b t d -> t b d"), ot[pp][:, 0:2, :]).then_inc(st_out[pp], 16)
                    for b in range(2):
                        sp.dma_start(out[bass.ds(p * 2 + b, 1), P:T, :].rearrange("b t d -> t (b d)"),
                                     ot[pp][GAP * b:GAP * b + TAIL, 2, :]).then_inc(st_out[pp], 16)

                for p in range(VFIRST + 1, VFIRST + 4):
                    load_xc(sp, p, p % 4)
                for n in range(2):
                    load_features(n, n)
                sp.wait_ge(s["dve_set_up"], DVE_SETUP // 2)
                sp.wait_ge(s["set_up"], 5)

                def second_registers(j):
                    q3 = qs[j][:, 0:H * TQ].rearrange("p (h t) -> p h t", h=H)
                    sp.dma_start(q3[65:66, :, T:TQ], consts16.rearrange("o (h t) -> o h t", h=H)).then_inc(ld_set, 16)
                for j in (0, 1):
                    second_registers(j)
                sp.wait_ge(class_step, CLASS_STEPS)
                sp.dma_start(scratch["cls"].rearrange("r (p t) -> p r t", t=QUARTER), cls[:, :, :]).then_inc(st_class, 16)
                sp.wait_ge(st_class, 16)
                load_classes(0, 0)
                load_classes(1, 1)
                load_features(2, 2)
                sp.wait_ge(s["dve_set_up"], DVE_SETUP)
                sp.wait_ge(s["set_up"], 10)
                load_classes(2, 2)
                second_registers(2)
                second_registers(3)
                run_steps(sp, [(-1, B, lambda n, k, half: None if isinstance(n, int) and n < 3 else load_stack(n, k, half)), (4, B, store_out), (1, B, load_shift)],
                          0, 4, 28, NSTEP, 4)
                for j in range(2):
                    sp.wait_ge(st_out[j], 48 * NPAIR // 2)

            @block.tensor
            def _(pe):
                def rows_of(part, banks, lhs, rhs, terms, done):
                    for b in range(2) if part == 0 else (part - 1,):
                        w, t, at = (GAP if b == 0 else TAIL, P, GAP * b) if part == 0 else (P, 0, 0)
                        dst = banks[1][at:at + w, 0:D] if part == 0 else banks[0][:, b * D:(b + 1) * D]
                        for m, (i, j, c) in enumerate(terms):
                            mm = pe.matmul(dst, lhs(b, i, c, t, w), rhs(j, c), start=(m == 0), stop=(m == len(terms) - 1))
                    mm.then_inc(s[done], 1)

                def vproj(p, j, quarter, part=None):
                    for m in range(3) if part is None else (part,):
                        if m == 0:
                            pe.wait_ge(ld_xc[j], quarter * 16)
                            need(pe, s["va_ready"], 2 * (p - VFIRST - 1))
                        rows_of(m, VBANKS[j % 2], lambda b, i, c, t, w: xc[j][:, i * KC + c, b * T + t:b * T + t + w],
                                lambda j, c: wv2[:, j, c, :], [(i, j, c) for c in range(KC) for i, j in HALVES], "v_done")

                for p in range(VFIRST, VCLASS):
                    vproj(p, p % 4, p // 4)
                pe.wait_ge(class_step, 8)
                pe.transpose(p_ext[0:2, 0:P], ext[:, :], ident).then_inc(ext_t, 1)
                pe.wait_ge(class_step, 10)
                pe.matmul(p_rng[:, 0:2], ones2[:, :], gd[:, :], start=True, stop=True).then_inc(ext_b, 1)
                for p in range(VCLASS, VEARLY):
                    vproj(p, p % 4, p // 4)
                pe.wait_ge(ld_set, 32)
                pe.wait_ge(s["set_up"], 5)
                pe.wait_ge(s["dve_set_up"], DVE_SETUP // 2)

                def logits(pD, group, n, k, rows, shifted):
                    for h, at, slot in tiles(group):
                        if shifted:
                            lhs = ks[k][:, h, P:KPAD] if group[0] else ks[k][:, h, 0:P]
                            rhs = q_head(k, P, h, 0, TQ)
                        else:
                            lhs = q_head(k, rows, h, P, GAP) if group[0] else q_head(k, rows, h, 0, P)
                            rhs = ks[k][0:rows, h, 0:T]
                        w = TQ if shifted else T
                        m = GAP if group[0] else P
                        mm = pe.matmul(pD[at:at + m, slot * w:(slot + 1) * w], lhs, rhs, start=True, stop=True)
                    return mm

                def a_group(i):
                    def emit(n, k, half):
                        if i == 0:
                            pe.wait_ge(ld_stack[k], half * 112 + 112)
                            if isinstance(n, int) and n == 2:
                                pe.wait_ge(ld_set, 64)
                                pe.wait_ge(s["set_up"], SETUP)
                                pe.wait_ge(s["dve_set_up"], DVE_SETUP)
                        need(pe, s["a_max"], NG * n + i - 1)
                        logits(pA[i % 2], GROUPS[i], n, k, SHIFT_ROW, False).then_inc(s["a_done"], 1)
                    return emit

                def b_group(i):
                    def emit(n, k, half):
                        if i == 0:
                            pe.wait_ge(ld_shift[k], half * 48 + 48)
                            if isinstance(n, int) and n == 0:
                                pe.wait_ge(s["va_ready"], 2 * (NPAIR - VFIRST))
                        need(pe, s["e_ready"], NG * n + i - 1)
                        logits(pB[i % 2], GROUPS[i], n, k, P, True).then_inc(s["b_done"], 1)
                    return emit

                def pv_group(a):
                    def emit(n, k, half):
                        if a == 0:
                            pe.wait_ge(s["v_ready"], 3 * n + 3)
                        if a % 2 == 0:
                            need(pe, s["os_ready"], 2 * n - 1 + a // 2)
                        pe.wait_ge(s["e_ready"], NG * n + 3 * a + 3)
                        for q in range(4):
                            h = 4 * a + q
                            dst = pO[32 * q:32 * q + 32, a // 2, (a % 2) * TQ:(a % 2 + 1) * TQ]
                            pe.matmul(dst, vm[k][:, h, :], em[:, h, :], start=True, stop=False, skip_group_check=True)
                        for q in range(4):
                            h = 4 * a + q
                            dst = pO[32 * q:32 * q + 32, a // 2, (a % 2) * TQ:(a % 2 + 1) * TQ]
                            mm = pe.matmul(dst, vt[k][:, h, :], et[:, h // 2, :], start=False, stop=True, skip_group_check=True)
                        mm.then_inc(s["pv_done"], 1)
                    return emit

                def max_rows(n, k, half):
                    pe.wait_ge(s["mh_ready"], n + 1)
                    if k % 2 == 0:
                        need(pe, s["out_ready"], 3 * (pair_of(n, half, k) - 2) + 1)
                    pe.transpose(pM16[0:16, 0:P], mh[k % 2][:, 0:16], ident16[:, :])
                    pe.transpose(pM16[0:8, P:2 * P], mh[k % 2][:, 16:24], ident16[:, :]).then_inc(s["mt_done"], 1)

                def c1_first(n, k, half):
                    pe.wait_ge(s["os_ready"], 2 * n + 2)
                    if k % 2 == 0:
                        need(pe, s["out_ready"], 3 * pair_of(n, half, k))
                    need(pe, s["of_copied"], n)
                    for a in range(4):
                        mm = pe.transpose(pX[:, 0, a * P:(a + 1) * P], os_[:, a, 0:P], ident)
                    mm.then_inc(s["c1_done"], 1)

                def c1_tail(n, k, half):
                    pe.wait_ge(s["mt_evac"], upto(2 * n + 6, 2 * B))
                    pe.sem_inc(s["pe_turn"], 1)
                    for a in range(4):
                        mm = pe.transpose(pX[0:QTAIL, 1, a * P:(a + 1) * P], os_[:, a, P:TQ], ident)
                    mm.then_inc(s["c1_done"], 1)

                def c2(n, k, half):
                    pe.wait_ge(s["on_ready"], 2 * n + 2)
                    for c in range(KC):
                        pe.transpose(pX[:, 0, c * TQ:c * TQ + P], on[:, 0, c * P:(c + 1) * P], ident)
                        mm = pe.transpose(pX[:, 0, c * TQ + P:(c + 1) * TQ], on[0:QTAIL, 1, c * P:(c + 1) * P], ident[0:QTAIL, 0:QTAIL])
                    mm.then_inc(s["c2_done"], 1)

                def late_v(i):
                    def emit(n, k, half):
                        p = VEARLY + VSTEP * n + i // 3
                        vproj(p, p % 4, p // 4, i % 3)
                    return emit

                def project(part):
                    def emit(n, k, half):
                        if k % 2 == 0:
                            return
                        if part == 0:
                            pe.wait_ge(s["of_ready"], n + 1)
                        rows_of(part, (pX[:, 0, :], pX[:, 1, :]), lambda b, i, c, t, w: of[b][:, c * TQ + t:c * TQ + t + w],
                                lambda j, c: wp[:, c, :], [(0, 0, c) for c in range(KC)], "f_done")
                    return emit

                between = {0: [(3, B, pv_group(3))], 1: [(1, B, max_rows)], 2: [(3, B, c1_first)], 3: [(3, B, c1_tail)],
                           4: [(2, B, pv_group(0))], 6: [(2, B, pv_group(1))], 7: [(3, B, c2)],
                           9: [(3, B, project(0)), (2, B, pv_group(2))], 10: [(3, B, project(1))], 11: [(3, B, project(2))]}
                for i in range(3 * VSTEP):
                    between.setdefault(i + 1, []).append((0, 2, late_v(i)))
                run_steps(pe, [stage for i in range(NG) for stage in [(2, B, b_group(i)), (0, B, a_group(i))] + between.get(i, [])],
                          0, *LOOP, NSTEP, 4)

            @block.scalar
            def _(act):
                act.wait_ge(ld_sim, 32)
                nc.scalar.activation(nrm, sq, ACT.Sqrt).then_inc(nrm_ready, 1)

                def v_evac(p, j, quarter):
                    act.wait_ge(s["v_done"], 3 * (p - VFIRST) + 3)
                    nc.scalar.activation(va[:, bass.ds(p * 2, 2), :].rearrange("p b d -> p (b d)"), VBANKS[j % 2][0], ACT.Copy,
                                         scale=1 / UP).then_inc(s["va_ready"], 1)
                    nc.scalar.activation(vta[0:PT, bass.ds(p, 1), :].rearrange("p a d -> p (a d)"), VBANKS[j % 2][1][0:PT, 0:D], ACT.Copy,
                                         scale=1 / UP).then_inc(s["va_ready"], 1)
                    if p + 4 < NPAIR:
                        load_xc(act, p + 4, j)

                def late_v(i):
                    def emit(n, k, half):
                        p = VEARLY + VSTEP * n + i
                        v_evac(p, p % 4, p // 4)
                    return emit

                for p in range(VFIRST, VEARLY):
                    v_evac(p, p % 4, p // 4)
                act.wait_ge(class_step, CLASS_STEPS)

                def mt_copy(n, k, half):
                    act.wait_ge(s["mt_done"], n + 1)
                    if not isinstance(n, int) or n >= 2:
                        act.wait_ge(ld_shift[(k - 2) % 4], 48 * (half + 1 if k >= 2 else half))
                    nc.scalar.activation(mr[k % 2][:, :], pM16[0:16, 0:P], ACT.Copy).then_inc(s["mt_evac"], 1)
                    nc.scalar.activation(mrt[k % 2][:, :], pM16[0:8, P:2 * P], ACT.Copy).then_inc(s["mt_evac"], 1)

                def os_copy(i):
                    def emit(n, k, half):
                        act.wait_ge(s["pv_done"], 4 * n + 2 * i + 2)
                        need(act, s["c1_done"], 2 * n)
                        nc.scalar.activation(os_[:, 2 * i:2 * i + 2, :].rearrange("p a t -> p (a t)"), pO[:, i, 0:2 * TQ],
                                             ACT.Copy).then_inc(s["os_ready"], 1)
                    return emit

                def of_copy(n, k, half):
                    act.wait_ge(s["c2_done"], n + 1)
                    nc.scalar.activation(of[k % 2][:, 0:KC * TQ], pX[:, 0, 0:KC * TQ], ACT.Copy).then_inc(s["of_copied"], 1)

                def v_first(n, k, half):
                    need(act, s["pv_done"], 4 * (n - 3))
                    if isinstance(n, int) and n == 0:
                        act.wait_ge(s["set_up"], SETUP)
                    if isinstance(n, int) and n < 4:
                        need(act, s["va_ready"], 2 * (n // 2 + 1 - VFIRST))
                    else:
                        act.wait_ge(s["va_ready"], 2 * (NPAIR - VFIRST))
                    nc.scalar.activation(vm[k][:, :, 0:16], va[:, bass.ds(n, 1), :].rearrange("p a (h d) -> p (a h) d", h=H),
                                         ACT.Copy).then_inc(s["v_ready"], 1)

                def v_tails(n, k, half):
                    b = k % 2
                    src = vta[GAP * b:GAP * b + TAIL, bass.ds(pair_of(n, half, k), 1), :].rearrange("p a (g e d) -> p (a g) e d", e=2, d=DH)
                    dst = vt[k][:, :, 0:16].rearrange("p (g e) d -> p g e d", e=2)
                    for e in range(2):
                        nc.scalar.activation(dst[GAP * e:GAP * e + TAIL, :, e, :], src[:, :, e, :], ACT.Copy).then_inc(s["v_ready"], 1)

                def e_group(i):
                    tail, g = GROUPS[i]

                    def emit(n, k, half):
                        act.wait_ge(s["b_done"], NG * n + i + 1)
                        need(act, s["pv_done"], 4 * (n - 1) + i // 3 + 1)
                        dst = (et if tail else em)[:, 2 * g:2 * g + 2, :].rearrange("p a t -> p (a t)")
                        nc.scalar.activation(dst, pB[i % 2][:, 0:2 * TQ], ACT.Exp).then_inc(s["e_ready"], 1)
                    return emit

                between = {0: [(3, B, os_copy(1))], 1: [(1, B, mt_copy)], 3: [(1, B, v_first)], 5: [(1, B, v_tails)], 7: [(3, B, of_copy)],
                           9: [(2, B, os_copy(0))]}
                for i in range(VSTEP):
                    between.setdefault(3 * i + 3, []).append((0, 2, late_v(i)))
                run_steps(act, [stage for i in range(NG) for stage in [(2, B, e_group(i))] + between.get(i, [])], 0, *LOOP, NSTEP, 4)

            @block.vector
            def _(dve):
                def set_up(j):
                    for t, value in blank_stack(j):
                        dve.memset(t, value).then_inc(s["dve_set_up"], 1)

                set_up(0)

                chain = [0]

                def step(ins):
                    ins.then_inc(class_step, 1)
                    chain[0] += 1
                    dve.wait_ge(class_step, chain[0])

                step(dve.memset(ones2[:, :], 1.0))
                dve.wait_ge(nrm_ready, 1)
                step(dve.reciprocal(rec, nrm))
                step(dve.scalar_tensor_tensor(out=cos, in0=num, scalar=1.0 / H / UP, in1=rec, op0=ALU.mult, op1=ALU.mult))
                step(dve.tensor_reduce(sim[:, :], cos.rearrange("p (h t) -> p t h", h=H), AX_X, ALU.add))
                step(dve.tensor_scalar(nsim[:, :], sim[:, :], -1.0, None, ALU.mult))
                big = con[:, C_REGBIG:C_REGBIG + QUARTER]
                step(dve.tensor_tensor_reduce(junk[:, 0, :], nsim[:, :], big, 1.0, -3e38, ALU.subtract, ALU.max, ext[:, 0:1]))
                step(dve.tensor_tensor_reduce(junk[:, 1, :], sim[:, :], big, 1.0, -3e38, ALU.subtract, ALU.max, ext[:, 1:2]))
                step(dve.memset(cls[:, :, :], 0.0))
                dve.wait_ge(ext_t, 1)
                step(dve.tensor_reduce(g2[:, :], p_ext[0:2, 0:P], AX_X, ALU.max))
                step(dve.tensor_scalar(gd[:, :], ident[0:2, 0:2], g2[:, 0:1], None, ALU.mult))
                dve.wait_ge(ext_b, 1)
                step(dve.tensor_copy(rng[:, :], p_rng[:, 0:2]))
                step(dve.tensor_tensor(dd[:, 0:1], rng[:, 0:1], rng[:, 1:2], ALU.add))
                step(dve.tensor_scalar(dd[:, 1:2], dd[:, 0:1], 0.9, None, ALU.mult))
                step(dve.tensor_scalar(pos[:, :], sim[:, :], rng[:, 0:1], dd[:, 1:2], ALU.add, ALU.is_gt))
                nreg = con[:, C_NREG:C_NREG + QUARTER]
                reg = con[:, C_REG:C_REG + QUARTER]
                step(dve.tensor_tensor(ca[:, :], pos[:, :], nreg, ALU.mult))
                step(dve.scalar_tensor_tensor(out=cn[:, :], in0=ca[:, :], scalar=-1.0, in1=nreg, op0=ALU.mult, op1=ALU.add))
                step(dve.tensor_scalar(cls[:, 3, :], ca[:, :], -CLASS, None, ALU.mult))
                step(dve.tensor_tensor(ca[:, :], ca[:, :], reg, ALU.add))
                dve.tensor_scalar(cls[:, 0, :], ca[:, :], CLASS, None, ALU.mult)
                dve.tensor_scalar(cls[:, 1, :], cn[:, :], CLASS, None, ALU.mult)
                dve.tensor_scalar(cls[:, 2, :], cn[:, :], -CLASS, None, ALU.mult).then_inc(class_step, 1)
                set_up(2)

                def a_max(i):
                    tail, g = GROUPS[i]

                    def emit(n, k, half):
                        dve.wait_ge(s["a_done"], NG * n + i + 1)
                        c0 = 16 + 2 * g if tail else 2 * g
                        dve.tensor_reduce(mx[k % 2][:, c0:c0 + 2], pA[i % 2][:, 0:2 * T].rearrange("p (a t) -> p a t", t=T),
                                          AX_X, ALU.max).then_inc(s["a_max"], 1)
                    return emit

                def negate(n, k, half):
                    dve.wait_ge(s["a_max"], NG * n + NG)
                    need(dve, s["mt_done"], n - 1)
                    dve.tensor_scalar(mh[k % 2][:, :], mx[k % 2][:, :], -1.0, -CLASS, ALU.mult, ALU.max).then_inc(s["mh_ready"], 1)

                def denominators(i):
                    def emit(n, k, half):
                        r = QTAIL if i else P
                        dve.wait_ge(s["c1_done"], 2 * n + 1 + i)
                        t4 = pX[0:r, i, :].rearrange("p (h e) -> p h e", e=32)
                        dve.reciprocal(rd[0:r, i, :].rearrange("p (h a) -> p h a", a=1), t4[:, :, 16:17]).then_inc(s["rd_ready"], 1)
                    return emit

                def norm(i):
                    def emit(n, k, half):
                        r = QTAIL if i else P
                        dve.wait_ge(s["rd_ready"], 2 * n + 1 + i)
                        need(dve, s["c2_done"], n)
                        t4 = pX[0:r, i, :].rearrange("p (h e) -> p h e", e=32)
                        dve.scalar_tensor_tensor(out=on[0:r, i, :].rearrange("p (h d) -> p h d", h=H), in0=t4[:, :, 0:16],
                                                 scalar=con[0:r, C_HALF + i:C_HALF + i + 1],
                                                 in1=rd[0:r, i, :].rearrange("p (h a) -> p h a", a=1).broadcast_to([r, H, DH]),
                                                 op0=ALU.mult, op1=ALU.mult).then_inc(s["on_ready"], 1)
                    return emit

                def registers(n, k, half):
                    dve.wait_ge(s["of_copied"], n + 1)
                    o3 = of[k % 2][:, 0:KC * TQ].rearrange("p (c t) -> p c t", c=KC)
                    dve.tensor_tensor(o3[:, :, 0:REG], o3[:, :, 0:REG], o3[:, :, T:TQ], ALU.add).then_inc(s["of_ready"], 1)

                def residual(tails):
                    def emit(n, k, half):
                        if k % 2 == 0:
                            return
                        p, pp = pair_of(n, half, k), k // 2
                        dve.wait_ge(s["f_done"], 3 * p + (1 if tails else 3))
                        dve.wait_ge(s["hb_ready"], 2 * p + 2)
                        need(dve, st_out[pp], 48 * half)
                        if tails:
                            dve.tensor_tensor(ot[pp][0:PT, 2, :], pX[0:PT, 1, 0:D], hb[0:PT, 2, :], ALU.add).then_inc(s["out_ready"], 1)
                        else:
                            for j in range(2):
                                dve.tensor_tensor(ot[pp][:, j, :], pX[:, 0, j * D:(j + 1) * D], hb[:, j, :], ALU.add).then_inc(s["out_ready"], 1)
                    return emit

                between = {3: [(3, B, denominators(0))], 4: [(3, B, norm(0)), (3, B, denominators(1))], 5: [(3, B, norm(1))],
                           7: [(3, B, registers)], 10: [(3, B, residual(True))], 11: [(0, B, negate), (3, B, residual(False))]}
                run_steps(dve, [stage for i in range(NG) for stage in [(0, B, a_max(i))] + between.get(i, [])], 0, *LOOP, NSTEP, 4)


def _constants(np):
    c = np.zeros((P, C_END), np.float32)
    r = np.arange(P)
    c[:, C_ID:C_ID + P] = np.eye(P)
    c[:, C_M0:C_M0 + P] = np.where(r[None, :] <= r[:, None], 0.0, MASKED)
    query = np.where(r < TAIL, P + r, np.where(r >= GAP, P + r - GAP, T))
    c[:, C_MT:C_MT + T] = np.where(np.arange(T)[None, :] <= query[:, None], 0.0, MASKED)
    c[:, C_BB:C_BB + P] = r[:, None] // DH == r[None, :] // DH
    for k in range(KC):
        c[:, C_OB + 32 * k:C_OB + 32 * k + H] = (k * P + r[:, None]) // DH == np.arange(H)[None, :]
    reg = (r[:, None] % 4 == 0) & (np.arange(QUARTER)[None, :] < REG)
    c[:, C_REGBIG:C_REGBIG + QUARTER] = np.where(reg, -MASKED, 0.0)
    c[:, C_NREG:C_NREG + QUARTER] = ~reg
    c[:, C_REG:C_REG + QUARTER] = reg
    c[:, C_HALF] = np.where(r < REG, 0.5, 1.0)
    c[:, C_HALF + 1] = np.where((r >= TAIL) & (r < QTAIL), 0.5, 1.0)
    c16 = np.full((1, H * REG), CLASS, np.float16)
    return c, c16


def kernel(**inputs):
    import numpy as np
    import concourse.bacc as bacc
    from concourse.bass_utils import run_bass_kernel_spmd

    a = {n: np.asarray(v) for n, v in inputs.items()}

    def chunks(w):
        return np.ascontiguousarray(w.reshape(-1, P, w.shape[1]).transpose(1, 0, 2))

    side = 16
    n = a["x"].shape[1] // side
    patches = a["x"].reshape(B, n, side, n, side, 3).transpose(2, 4, 5, 0, 1, 3).reshape(KE, P, NE, P)
    c, c16 = _constants(np)
    arrays = {
        "xt": np.ascontiguousarray(patches.transpose(1, 2, 0, 3)),
        "txt": np.ascontiguousarray(a["txt"]),
        "w_tok": chunks(a["L0_tok_W"].T),
        "b_tok": a["L0_tok_b"].reshape(1, D),
        "a_wqt": chunks(a["L0_attn_W_Q"].T),
        "a_wkt": chunks(a["L0_attn_W_K"].T),
        "a_wv": chunks(a["L0_attn_W_V"]),
        "f_wqkv": chunks(a["L0_ffn_W_qkv"]),
        "f_wqt": chunks(a["L0_ffn_W_qkv"][:, 0:D].T),
        "f_g": np.ascontiguousarray(a["L0_ffn_g_info"][0, 0].reshape(KC, P).T),
        "f_wp": chunks(a["L0_ffn_W_proj"]),
        "f_bp": a["L0_ffn_b_proj"].reshape(1, D),
        "consts": c,
        "consts16": c16,
    }
    nc = bacc.Bacc("TRN2", target_bir_lowering=False, num_devices=1)
    args = [nc.dram_tensor(m, v.shape, mybir.dt.from_np(v.dtype), kind="ExternalInput").ap() for m, v in arrays.items()]
    out = nc.dram_tensor("out", (B, T, D), F32, kind="ExternalOutput").ap()
    fusion_program(nc, *args, out)
    r = run_bass_kernel_spmd(nc, [arrays], core_ids=[0])
    return r.results[0]["out"]
```
